# Optimizing a Trainium2 kernel written in Bass

```python
import numpy as np
import jax
import jax.numpy as jnp

def _softmax(x, axis=-1):
    return jax.nn.softmax(x, axis=axis)

def _gelu(x):
    return jax.nn.gelu(x, approximate=True)

def _silu(x):
    return jax.nn.silu(x)

def _sigmoid(x):
    return jax.nn.sigmoid(x)

def _layernorm(x, axis=-1, eps=1e-05):
    m = jnp.mean(x, axis=axis, keepdims=True)
    v = jnp.var(x, axis=axis, keepdims=True)
    return (x - m) / jnp.sqrt(v + eps)

def _scatter_add(tgt, idx, src, axis=0):
    return tgt.at[idx].add(src)

def _segment_sum(src, seg, n):
    return jax.ops.segment_sum(src, seg, n)
kernel_name = 'mk_adaln_d1_jaxref_r4_ba7015'

def setup_inputs(seed: int=0):
    np.random.seed(seed)
    _w = jnp.asarray

    def _L0_attn_setup():
        import jax, jax.numpy as jnp
        import numpy as np
        import math
        HIDDEN = 512
        NUM_HEADS = 16
        HEAD_SIZE = HIDDEN // NUM_HEADS
        BATCH = 2
        SEQ = 512
        key = jax.random.key(seed)
        k_x, k_wq, k_bq, k_wo, k_bo = jax.random.split(key, 5)
        scale_in = 1.0 / math.sqrt(HIDDEN)
        return {'x': jax.random.normal(k_x, (BATCH, SEQ, HIDDEN), dtype=jnp.float32), 'Wqkv': jax.random.normal(k_wq, (HIDDEN, 3 * HIDDEN), dtype=jnp.float32) * scale_in, 'bqkv': jax.random.normal(k_bq, (3 * HIDDEN,), dtype=jnp.float32) * 0.01, 'Wo': jax.random.normal(k_wo, (HIDDEN, HIDDEN), dtype=jnp.float32) * scale_in, 'bo': jax.random.normal(k_bo, (HIDDEN,), dtype=jnp.float32) * 0.01}
    _L0_attn_in = _L0_attn_setup()

    def _L0_ffn_setup():
        import jax, jax.numpy as jnp
        import numpy as np
        HIDDEN = 512
        MOE_INTER = 256
        SHARED_INTER = 1024
        N_EXPERTS = 16
        TOP_K = 2
        N_GROUP = 4
        TOPK_GROUP = 2
        NORM_TOPK_PROB = True
        ROUTED_SCALING = 1.0

        def relu2(x):
            r = jax.nn.relu(x)
            return r * r

        def _get_topk_indices(scores, e_bias):
            T, E = scores.shape
            s = scores + e_bias[None, :]
            gsz = E // N_GROUP
            group_scores = jax.lax.top_k(s.reshape(T, N_GROUP, gsz), 2)[0].sum(-1)
            group_idx = jax.lax.top_k(group_scores, TOPK_GROUP)[1]
            group_mask = jnp.zeros((T, N_GROUP), dtype=bool).at[jnp.arange(T)[:, None], group_idx].set(True)
            score_mask = jnp.repeat(group_mask, gsz, axis=1)
            masked = jnp.where(score_mask, s, 0.0)
            topk_indices = jax.lax.top_k(masked, TOP_K)[1]
            return jax.lax.stop_gradient(topk_indices)

        def _router(x_flat, router_weight, e_bias):
            logits = jnp.einsum('th,eh->te', x_flat.astype(jnp.float32), router_weight.astype(jnp.float32))
            scores = jax.nn.sigmoid(logits)
            topk_indices = _get_topk_indices(scores, e_bias)
            topk_weights = jnp.take_along_axis(scores, topk_indices, axis=1)
            if NORM_TOPK_PROB:
                topk_weights = topk_weights / (topk_weights.sum(-1, keepdims=True) + 1e-20)
            return (topk_indices, topk_weights * ROUTED_SCALING)
        key = jax.random.key(seed)
        ks = jax.random.split(key, 6)
        s = 0.02
        hidden_states = jax.random.normal(ks[0], (1, 512, HIDDEN), dtype=jnp.float32)
        router_weight = jax.random.normal(ks[1], (N_EXPERTS, HIDDEN), dtype=jnp.float32) * s
        e_bias = jnp.zeros((N_EXPERTS,), dtype=jnp.float32)
        w_up = jax.random.normal(ks[2], (N_EXPERTS, HIDDEN, MOE_INTER), dtype=jnp.float32) * s
        w_down = jax.random.normal(ks[3], (N_EXPERTS, MOE_INTER, HIDDEN), dtype=jnp.float32) * s
        shared_up = jax.random.normal(ks[4], (HIDDEN, SHARED_INTER), dtype=jnp.float32) * s
        shared_down = jax.random.normal(ks[5], (SHARED_INTER, HIDDEN), dtype=jnp.float32) * s
        return {'hidden_states': hidden_states, 'router_weight': router_weight, 'e_bias': e_bias, 'w_up': w_up, 'w_down': w_down, 'shared_up': shared_up, 'shared_down': shared_down}
    _L0_ffn_in = _L0_ffn_setup()
    _L0_c = _w((lambda *s: np.random.randn(*s).astype(np.float32) * 0.05)(4, 512))
    _L0_wmod = _w((lambda *s: np.random.randn(*s).astype(np.float32) * 0.05)(512, 6 * 512) * 512 ** (-0.5))
    _d = {'L0_attn_x': _L0_attn_in['x'], 'L0_attn_Wqkv': _L0_attn_in['Wqkv'], 'L0_attn_bqkv': _L0_attn_in['bqkv'], 'L0_attn_Wo': _L0_attn_in['Wo'], 'L0_attn_bo': _L0_attn_in['bo'], 'L0_ffn_router_weight': _L0_ffn_in['router_weight'], 'L0_ffn_e_bias': _L0_ffn_in['e_bias'], 'L0_ffn_w_up': _L0_ffn_in['w_up'], 'L0_ffn_w_down': _L0_ffn_in['w_down'], 'L0_ffn_shared_up': _L0_ffn_in['shared_up'], 'L0_ffn_shared_down': _L0_ffn_in['shared_down'], 'L0_c': _L0_c, 'L0_wmod': _L0_wmod}
    _x0 = _d['L0_attn_x']
    _d['L0_attn_x'] = jax.random.normal(jax.random.fold_in(jax.random.key(seed), 1), (4, 1024, 512), dtype=_x0.dtype)
    del _x0
    return _d

def reference(L0_attn_x, L0_attn_Wqkv, L0_attn_bqkv, L0_attn_Wo, L0_attn_bo, L0_ffn_router_weight, L0_ffn_e_bias, L0_ffn_w_up, L0_ffn_w_down, L0_ffn_shared_up, L0_ffn_shared_down, L0_c, L0_wmod):

    def _L0_attn_ref(x, Wqkv, bqkv, Wo, bo):
        import jax, jax.numpy as jnp
        import numpy as np
        import math
        HIDDEN = 512
        NUM_HEADS = 16
        HEAD_SIZE = HIDDEN // NUM_HEADS
        BATCH = 2
        SEQ = 512
        b, s, _ = x.shape
        kqv = x @ Wqkv + bqkv
        kqv = kqv.reshape(b, s, 3, NUM_HEADS, HEAD_SIZE)
        q = kqv[:, :, 0]
        k = kqv[:, :, 1]
        v = kqv[:, :, 2]
        scores = jnp.einsum('bsnh,btnh->bnst', k, q) / math.sqrt(HEAD_SIZE)
        ones = jnp.ones_like(scores)
        scores = jnp.triu(scores) + -10000.0 * jnp.tril(ones, k=-1)
        attn = jax.nn.softmax(scores, axis=2)
        out = jnp.einsum('bnkq,bknh->bqnh', attn, v)
        out = out.reshape(b, s, NUM_HEADS * HEAD_SIZE)
        return out @ Wo + bo

    def _L0_ffn_ref(hidden_states, router_weight, e_bias, w_up, w_down, shared_up, shared_down):
        import jax, jax.numpy as jnp
        import numpy as np
        HIDDEN = 512
        MOE_INTER = 256
        SHARED_INTER = 1024
        N_EXPERTS = 16
        TOP_K = 2
        N_GROUP = 4
        TOPK_GROUP = 2
        NORM_TOPK_PROB = True
        ROUTED_SCALING = 1.0

        def relu2(x):
            r = jax.nn.relu(x)
            return r * r

        def _get_topk_indices(scores, e_bias):
            T, E = scores.shape
            s = scores + e_bias[None, :]
            gsz = E // N_GROUP
            group_scores = jax.lax.top_k(s.reshape(T, N_GROUP, gsz), 2)[0].sum(-1)
            group_idx = jax.lax.top_k(group_scores, TOPK_GROUP)[1]
            group_mask = jnp.zeros((T, N_GROUP), dtype=bool).at[jnp.arange(T)[:, None], group_idx].set(True)
            score_mask = jnp.repeat(group_mask, gsz, axis=1)
            masked = jnp.where(score_mask, s, 0.0)
            topk_indices = jax.lax.top_k(masked, TOP_K)[1]
            return jax.lax.stop_gradient(topk_indices)

        def _router(x_flat, router_weight, e_bias):
            logits = jnp.einsum('th,eh->te', x_flat.astype(jnp.float32), router_weight.astype(jnp.float32))
            scores = jax.nn.sigmoid(logits)
            topk_indices = _get_topk_indices(scores, e_bias)
            topk_weights = jnp.take_along_axis(scores, topk_indices, axis=1)
            if NORM_TOPK_PROB:
                topk_weights = topk_weights / (topk_weights.sum(-1, keepdims=True) + 1e-20)
            return (topk_indices, topk_weights * ROUTED_SCALING)
        orig_shape = hidden_states.shape
        x = hidden_states.reshape(-1, HIDDEN)
        T = x.shape[0]
        topk_indices, topk_weights = _router(x, router_weight, e_bias)
        combine = jnp.zeros((T, N_EXPERTS), dtype=topk_weights.dtype).at[jnp.arange(T)[:, None], topk_indices].add(topk_weights)
        h1 = jnp.einsum('th,ehi->tei', x, w_up)
        a = relu2(h1) * combine[:, :, None]
        routed = jnp.einsum('tei,eih->th', a, w_down)
        shared = relu2(hidden_states @ shared_up) @ shared_down
        return routed.reshape(orig_shape) + shared
    x = L0_attn_x
    mod = (_silu(L0_c) @ L0_wmod).reshape(L0_c.shape[0], 6, 1, -1)
    sa, ca, ga, sb, cb, gb = (mod[:, 0], mod[:, 1], mod[:, 2], mod[:, 3], mod[:, 4], mod[:, 5])
    ga = (2 * (ga >= 0) - 1) * jnp.maximum(jnp.abs(ga), 0.25)
    gb = (2 * (gb >= 0) - 1) * jnp.maximum(jnp.abs(gb), 0.25)
    h = _layernorm(x, axis=-1) * (1 + ca) + sa
    x = x + ga * _L0_attn_ref(h, L0_attn_Wqkv, L0_attn_bqkv, L0_attn_Wo, L0_attn_bo)
    h = _layernorm(x, axis=-1) * (1 + cb) + sb
    x = x + gb * _L0_ffn_ref(h, L0_ffn_router_weight, L0_ffn_e_bias, L0_ffn_w_up, L0_ffn_w_down, L0_ffn_shared_up, L0_ffn_shared_down)
    return x

_drawn_inputs = setup_inputs


def setup_inputs(seed=0):
    import zlib

    import numpy as np

    out = dict(_drawn_inputs(seed))
    spreads = {'L0_ffn_e_bias': (0.0, 0.493)}
    factors = {'L0_attn_bqkv': 8.0,
     'L0_attn_bo': 8.0,
     'L0_ffn_router_weight': 5.392,
     'L0_ffn_w_up': 4.353,
     'L0_ffn_w_down': 3.974}
    for name, (base, spread) in spreads.items():
        noise = np.random.default_rng([zlib.crc32(name.encode()), seed]).standard_normal(out[name].shape)
        drawn = base * np.exp(spread * noise) if base else spread * noise
        out[name] = jnp.asarray(drawn.astype(out[name].dtype))
    for name, factor in factors.items():
        out[name] = (out[name] * factor).astype(out[name].dtype)
    return out
```

```python
import concourse.bass as bass
from concourse import mybir
from contextlib import ExitStack

P = 128
D = 512
KC = D // P
H, DH = 16, 32
NB, S = 4, 1024
T = NB * S
NT = S // P
SCALE = float(DH) ** -0.5
MASKED = -10000.0 / SCALE
NEG = -1e30
EPS = 1e-5
SA, CA1, GA, SB, CB1, GB, GABO = range(7)


def setup_phase(nc, K):
    f32, f32r, bf16 = mybir.dt.float32, mybir.dt.float32r, mybir.dt.bfloat16
    ALU, ACT = mybir.AluOpType, mybir.ActivationFunctionType
    ctx = ExitStack()
    with ctx:
        sb = lambda n, s, d=f32: ctx.enter_context(nc.sbuf_tensor(n, s, d))
        sem = lambda n: ctx.enter_context(nc.semaphore(n))
        wraw = sb("wraw", [P, KC, 3 * D])
        wmod = sb("wmod_sb", [P, KC, 6 * D])
        cT = sb("cT", [P, KC, NB])
        sig = sb("sig", [P, KC, NB])
        silu = sb("silu", [P, KC, NB])
        bv4 = sb("bv4", [P, KC, NB])
        bo4 = sb("bo4", [NB, D])
        modr = sb("modr", [NB, 7, D])
        sgn = sb("sgn", [NB, 2, D])
        mag = sb("mag", [NB, 2, D])
        pm = [ctx.enter_context(nc.psum_tensor(f"pmod{i}", [P, 512], f32)) for i in range(7)]
        small_in, w_in, wmod_in = sem("small_in"), sem("w_in"), sem("wmod_in")
        sig_done, silu_done, mod_mm, bo_mm = sem("sig_done"), sem("silu_done"), sem("mod_mm"), sem("bo_mm")
        hi_done, step, mod_stored, zeroed, consts = sem("w_hi_done"), sem("setup_step"), sem("mod_stored"), sem("c_zeroed"), sem("consts")
        bv_done, mag_done = sem("bv_done"), sem("mag_done")
        block = ctx.enter_context(nc.Block())

        @block.sync
        def _(sp):
            with nc.allow_non_contiguous_dma(reason="small vectors by partition"):
                for k in range(KC):
                    sp.dma_start(cT[:, k, :], K.c[:, k * P:(k + 1) * P].rearrange("b p -> p b")).then_inc(small_in, 16)
                sp.dma_start(K.bias[:, :], K.bqkv.rearrange("(g p) -> p g", p=P)).then_inc(small_in, 16)
            sp.dma_start(bo4[:, :], K.bo.rearrange("(a n) -> a n", a=1).broadcast_to([NB, D])).then_inc(small_in, 16)
            sp.dma_start(wmod[:, :, :], K.wmod.rearrange("(k p) n -> p k n", p=P)).then_inc(wmod_in, 16)
            sp.dma_start(K.wo[:, :, :], K.Wo.rearrange("(k p) n -> p k n", p=P)).then_inc(w_in, 16)
            sp.dma_start(wraw[:, :, :], K.Wqkv.rearrange("(k p) n -> p k n", p=P)).then_inc(w_in, 16)
            sp.wait_ge(step, 9)
            sp.dma_start(K.modd, modr[:, :, :]).then_inc(mod_stored, 16)
            sp.wait_ge(mod_stored, 16)

        @block.gpsimd
        def _(pool):
            nc.gpsimd.memset(K.expo[:, :], -0.5).then_inc(zeroed, 1)
            nc.gpsimd.memset(K.ident[:, :], 0.0).then_inc(zeroed, 1)
            nc.gpsimd.memset(K.identb[:, :], 0.0).then_inc(zeroed, 1)
            nc.gpsimd.memset(K.mask_qk[:, :], 0.0).then_inc(zeroed, 1)
            nc.gpsimd.memset(K.mask_kq[:, :], 0.0).then_inc(zeroed, 1)
            nc.gpsimd.memset(K.V[:, NT * D:NT * D + DH], 1.0).then_inc(zeroed, 1)
            nc.gpsimd.memset(K.S[:, :, :], 0.0).then_inc(zeroed, 1)
            nc.gpsimd.memset(K.ones_row[:, :], 1.0).then_inc(zeroed, 1)
            pool.wait_ge(zeroed, 8)
            for m in (K.ident, K.identb):
                nc.gpsimd.affine_select(out=m[:, :], in_=m[:, :], compare_op=ALU.not_equal, fill=1.0, base=0,
                                        pattern=[[-1, P]], channel_multiplier=1).then_inc(consts, 1)
            nc.gpsimd.affine_select(out=K.mask_qk[:, :], in_=K.mask_qk[:, :], compare_op=ALU.is_ge, fill=NEG, base=0,
                                    pattern=[[-1, P]], channel_multiplier=1).then_inc(consts, 1)
            nc.gpsimd.affine_select(out=K.mask_kq[:, :], in_=K.mask_kq[:, :], compare_op=ALU.is_ge, fill=NEG, base=0,
                                    pattern=[[1, P]], channel_multiplier=-1).then_inc(consts, 1)
            for k in range(KC):
                pool.wait_ge(hi_done, k + 1)
                nc.gpsimd.tensor_tensor(K.wlo[:, k, :], wraw[:, k, :], K.whi[:, k, :].bitcast(f32), ALU.subtract).then_inc(consts, 1)
            pool.wait_ge(consts, 4 + KC)

        @block.scalar
        def _(act):
            act.wait_ge(small_in, 96)
            nc.scalar.activation(sig[:, :, :], cT[:, :, :], ACT.Sigmoid).then_inc(sig_done, 1)
            act.wait_ge(mod_mm, 6)
            for i, src in ((0, 2), (1, 5)):
                nc.scalar.activation(mag[:, i, :], pm[src][0:NB, :], ACT.Abs, scale=2.0).then_inc(mag_done, 1)
            act.wait_ge(w_in, 32)
            for k in range(KC):
                nc.scalar.activation(K.whi[:, k, :], wraw[:, k, :], ACT.Copy).then_inc(hi_done, 1)

        @block.vector
        def _(dve):
            dve.wait_ge(zeroed, 8)
            for s in range(2):
                for e in range(2):
                    nc.vector.tensor_copy(K.kst[96:128, s, e, :], K.ones_row[96:128, :])
            dve.wait_ge(sig_done, 1)
            nc.vector.tensor_tensor(silu[:, :, :], cT[:, :, :], sig[:, :, :], ALU.mult).then_inc(silu_done, 1)
            for i in range(NB):
                last = nc.vector.tensor_copy(bv4[:, :, i], K.bias[:, 2 * KC:3 * KC])
            last.then_inc(bv_done, 1)
            dve.wait_ge(mod_mm, 6)
            for kind, src, add in ((SA, 0, 0.0), (CA1, 1, 1.0), (SB, 3, 0.0), (CB1, 4, 1.0)):
                nc.vector.tensor_scalar(modr[:, kind, :], pm[src][0:NB, :], add, None, ALU.add).then_inc(step, 1)
            for i, src in ((0, 2), (1, 5)):
                dve.wait_ge(mag_done, i + 1)
                nc.vector.tensor_scalar(sgn[:, i, :], pm[src][0:NB, :], 0.0, 0.5, ALU.is_ge, ALU.subtract).then_inc(step, 1)
            dve.wait_ge(step, 6)
            for i, kind in ((0, GA), (1, GB)):
                nc.vector.scalar_tensor_tensor(modr[:, kind, :], mag[:, i, :], 0.5, sgn[:, i, :], ALU.max, ALU.mult)\
                    .then_inc(step, 1)
            dve.wait_ge(bo_mm, 1)
            nc.vector.tensor_tensor(bo4[:, :], pm[6][0:NB, :], bo4[:, :], ALU.add).then_inc(bo_mm, 1)
            dve.wait_ge(bo_mm, 2)
            dve.wait_ge(step, 8)
            nc.vector.tensor_tensor(modr[:, GABO, :], modr[:, GA, :], bo4[:, :], ALU.mult).then_inc(step, 1)

        @block.tensor
        def _(pe):
            pe.wait_ge(silu_done, 1)
            pe.wait_ge(wmod_in, 16)
            for n in range(6):
                for k in range(KC):
                    last = nc.tensor.matmul(pm[n][0:NB, :], silu[:, k, :], wmod[:, k, n * D:(n + 1) * D],
                                            start=(k == 0), stop=(k == KC - 1))
                last.then_inc(mod_mm, 1)
            pe.wait_ge(bv_done, 1)
            pe.wait_ge(w_in, 32)
            for k in range(KC):
                last = nc.tensor.matmul(pm[6][0:NB, :], bv4[:, k, :], K.wo[:, k, :], start=(k == 0), stop=(k == KC - 1))
            last.then_inc(bo_mm, 1)


def attention_phase(nc, K):
    f32, f32r, bf16 = mybir.dt.float32, mybir.dt.float32r, mybir.dt.bfloat16
    ALU, ACT, AX = mybir.AluOpType, mybir.ActivationFunctionType, mybir.AxisListType
    NPAIR = H // 2
    NHG = H // 4
    CH = 512
    STEPS = [(c, i) for c in range(2) for i in range(4 * c + 4)]
    NST = len(STEPS)
    MUSES = []
    for qt in range(NT):
        first = min((qt + 1) * P, CH)
        rest = (qt + 1) * P - first
        for n, k0, part in ((first, 0, 0), (rest, CH, 1)):
            if not n:
                continue
            if 2 * n <= CH:
                MUSES.append(((0, 1), qt, k0, n, part))
            else:
                MUSES += [((e,), qt, k0, n, part) for e in range(2)]
    NM = len(MUSES)
    ring = []
    for j in range(NT):
        ring.append("hT")
        if j >= 1:
            ring.append("v")
    ring.append("v")
    ring += ["p"] * 4 + ["m"] * NM + ["mt"] * 2
    for p in range(NPAIR):
        if p % 2 and p + 1 < NPAIR:
            ring += ["p"] * 4
        if p + 1 < NPAIR:
            ring += ["m"] * NM + ["mt"] * 2
    ring += ["w"] * NT
    TOTAL = {k: ring.count(k) for k in set(ring)}
    assert len(ring) % 3 == 0, len(ring)

    ctx = ExitStack()
    with ctx:
        sb = lambda n, s, d=f32: ctx.enter_context(nc.sbuf_tensor(n, s, d))
        sem = lambda n: ctx.enter_context(nc.semaphore(n))
        mod_t = sb("mod_t", [P, 2, KC])
        ga_bc = sb("ga_bc", [P, D])
        gabo_bc = sb("gabo_bc", [P, D])
        xa = sb("xa", [P, 2, D])
        stats = sb("stats", [P, 2, 6])
        mv = sb("mv", [P, 2, 2])
        rstd = sb("rstd", [P, 2, 2])
        h = sb("h", [P, 2, KC, P])
        hhi = sb("hhi", [P, KC, S], f32r)
        hlo = sb("hlo", [P, KC, S], f32r)
        st = sb("st", [P, 2, 2, S], f32r)
        qst = sb("qst", [P, 2, 2, S], f32r)
        kst, V, S_t = K.kst, K.V, K.S
        mx = sb("mx", [P, 2, NT, 2])
        negm = sb("negm", [P, NT, 2])
        mhi = sb("mhi", [P, NT, 2], f32r)
        pr = sb("pr", [P, 3, 2, CH])
        oV = sb("oV", [P, 2, CH])
        oD = sb("oD", [P, 2, CH])
        oT = sb("oT", [P, KC, S])
        xr = xa
        u = h.rearrange("p a k t -> p a (k t)") if hasattr(h, "rearrange") else h[:, :, :, :].rearrange("p a k t -> p a (k t)")
        pb = lambda n, s: ctx.enter_context(nc.psum_tensor(n, s, f32))
        rb = [pb(f"ring{i}", [P, 512]) for i in range(3)]
        sc = [pb(f"sc{i}", [P, 2, 512]) for i in range(2)]
        O = pb("O", [P, 512])

        mod_in, mod2_in = sem("mod_in"), sem("mod2_in")
        xa_in = [sem(f"xa_in{i}") for i in range(2)]
        xr_in = [sem(f"xr_in{i}") for i in range(2)]
        x1_out = [sem(f"x1_out{i}") for i in range(2)]
        stk_in = [sem(f"stk_in{i}") for i in range(2)]
        bn, mv_ready, rstd_ready, xn_ready = sem("bn"), sem("mv_ready"), sem("rstd_ready"), sem("xn_ready")
        var_eps = sem("var_eps")
        t_done, h_ready, hhi_ready, hlo_ready = sem("t_done"), sem("h_ready"), sem("hhi_ready"), sem("hlo_ready")
        v_done, v_ready = sem("v_done"), sem("v_ready")
        p_done, p_hi, p_lo = sem("p_done"), sem("p_hi"), sem("p_lo")
        m_done, m_red, mstep, s_ready = sem("m_done"), sem("m_red"), sem("mstep"), sem("s_ready")
        mt_done, mt_ready = sem("mt_done"), sem("mt_ready")
        sc_done, exp_done, pv_done = sem("sc_done"), sem("exp_done"), sem("pv_done")
        o_copied, o_rec, o_norm = sem("o_copied"), sem("o_rec"), sem("o_norm")
        w_done, u_ready, xg_ready, x1_ready = sem("w_done"), sem("u_ready"), sem("xg_ready"), sem("x1_ready")
        freed = {"hT": h_ready, "v": v_ready, "p": p_lo, "m": m_red, "mt": mt_ready, "w": u_ready}
        positions = {}
        for at, kind in enumerate(ring):
            positions.setdefault(kind, []).append(at)

        def ring_at(kind, n):
            return positions[kind][n]

        block = ctx.enter_context(nc.Block())

        @block.sync
        def _(sp):
            with sp.Fori(0, NB) as b:
                sp.wait_ge(h_ready, b * NT)
                with nc.allow_non_contiguous_dma(reason="512 numbers by partition"):
                    for i, kind in ((0, SA), (1, CA1)):
                        for k in range(KC):
                            sp.dma_start(mod_t[:, i, k:k + 1], K.modd[bass.ds(b, 1), kind, k * P:(k + 1) * P].rearrange("a p -> p a"))\
                                .then_inc(mod_in, 16)
                sp.wait_ge(u_ready, b * NT)
                sp.dma_start(ga_bc[:, :], K.modd[bass.ds(b, 1), GA, :].broadcast_to([P, D])).then_inc(mod2_in, 16)
                sp.wait_ge(x1_ready, b * NT)
                sp.dma_start(gabo_bc[:, :], K.modd[bass.ds(b, 1), GABO, :].broadcast_to([P, D])).then_inc(mod2_in, 16)
                for j in range(NT):
                    if j >= 2:
                        sp.wait_ge(t_done, b * NT + j - 1)
                    else:
                        sp.wait_ge(x1_ready, b * NT)
                    sp.dma_start(xa[:, j % 2, :], K.x[bass.ds(b * S + j * P, P), :]).then_inc(xa_in[j % 2], 16)
                for p in range(NPAIR):
                    if p >= 2:
                        sp.wait_ge(pv_done, b * (NPAIR * NST) + NST * (p - 1))
                        apart(sp)
                    sp.wait_ge(p_lo, b * 16 + 4 * (p // 2) + 4)
                    for e in range(2):
                        r = 2 * (p % 2) + e
                        rows = slice(32 * r, 32 * r + 32)
                        for n, (qp, kp) in enumerate(((0, 0), (1, 0), (0, 1))):
                            sp.dma_start(qst[32 * n:32 * n + 32, p % 2, e, :].bitcast(f32), st[rows, 0, qp, :].bitcast(f32)).then_inc(stk_in[p % 2], 16)
                            sp.dma_start(kst[32 * n:32 * n + 32, p % 2, e, :].bitcast(f32), st[rows, 1, kp, :].bitcast(f32)).then_inc(stk_in[p % 2], 16)
                for j in range(NT):
                    if j < 2:
                        sp.wait_ge(t_done, b * NT + NT)
                    else:
                        sp.wait_ge(x1_ready, b * NT + j - 1)
                    sp.dma_start(xr[:, j % 2, :], K.x[bass.ds(b * S + j * P, P), :]).then_inc(xr_in[j % 2], 16)
                    if j >= 1:
                        sp.wait_ge(x1_ready, b * NT + j)
                        sp.dma_start(K.x1d[bass.ds(b * S + (j - 1) * P, P), :], u[:, (j - 1) % 2, :]).then_inc(x1_out[(j - 1) % 2], 16)
                sp.wait_ge(x1_ready, b * NT + NT)
                sp.dma_start(K.x1d[bass.ds(b * S + (NT - 1) * P, P), :], u[:, (NT - 1) % 2, :]).then_inc(x1_out[(NT - 1) % 2], 16)
            for i in range(2):
                sp.wait_ge(x1_out[i], NB * NT // 2 * 16)

        @block.gpsimd
        def _(pool):
            def split_low(b, j):
                pool.wait_ge(h_ready, b * NT + j + 1)
                pool.wait_ge(hhi_ready, b * NT + j + 1)
                nc.gpsimd.tensor_tensor(hlo[:, :, j * P:(j + 1) * P], h[:, j % 2, :, :],
                                        hhi[:, :, j * P:(j + 1) * P].bitcast(f32), ALU.subtract).then_inc(hlo_ready, 1)

            with pool.Fori(0, NB) as b:
                for j in range(NT):
                    pool.wait_ge(mv_ready, b * NT + j + 1)
                    apart(pool)
                    nc.gpsimd.tensor_scalar(rstd[:, j % 2, 0:1], mv[:, j % 2, 1:2], EPS, None, ALU.add).then_inc(var_eps, 1)
                    pool.wait_ge(var_eps, b * NT + j + 1)
                    nc.gpsimd.tensor_tensor(rstd[:, j % 2, 1:2], rstd[:, j % 2, 0:1], K.expo[:, 0:1], ALU.pow).then_inc(rstd_ready, 1)
                    if j >= 2:
                        split_low(b, j - 2)
                split_low(b, NT - 2)
                split_low(b, NT - 1)
                for n in range(2 * NHG):
                    hg, c = n // 2, n % 2
                    pool.wait_ge(o_rec, b * 8 + n + 1)
                    nc.gpsimd.tensor_tensor(oT[:, hg, c * CH:(c + 1) * CH], oV[:, c, :], oD[:, c, :], ALU.mult).then_inc(o_norm, 1)
                pool.wait_ge(mod2_in, b * 32 + 32)
                for j in range(NT):
                    pool.wait_ge(xr_in[j % 2], b * (NT // 2 * 16) + (j // 2 + 1) * 16)
                    nc.gpsimd.tensor_tensor(xr[:, j % 2, :], xr[:, j % 2, :], gabo_bc[:, :], ALU.add).then_inc(xg_ready, 1)
                    pool.wait_ge(xg_ready, b * NT + j + 1)
                    pool.wait_ge(u_ready, b * NT + j + 1)
                    nc.gpsimd.tensor_tensor(u[:, j % 2, :], u[:, j % 2, :], xr[:, j % 2, :], ALU.add).then_inc(x1_ready, 1)

        @block.scalar
        def _(act):
            def p_evac(b, hg):
                for n in range(4):
                    which, c = n // 2, n % 2
                    if n == 0 and hg >= 1:
                        for s in range(2):
                            act.wait_ge(stk_in[s], b * 4 * 192 + hg * 192)
                    elif n == 0:
                        for s in range(2):
                            act.wait_ge(stk_in[s], b * 4 * 192)
                    u_ = ring_at("p", 4 * hg + n)
                    act.wait_ge(p_done, b * 16 + 4 * hg + n + 1)
                    nc.scalar.activation(st[:, which, 0, c * CH:(c + 1) * CH], rb[u_ % 3][:, :], ACT.Identity,
                                         bias=K.bias[:, which * KC + hg:which * KC + hg + 1]).then_inc(p_hi, 1)

            def mt_evac(b, p):
                if p >= 2:
                    act.wait_ge(pv_done, b * NPAIR * NST + NST * (p - 1))
                for c in range(2):
                    act.wait_ge(mt_done, b * 16 + 2 * p + c + 1)
                    bank = rb[ring_at("mt", 2 * p + c) % 3]
                    for e in range(2):
                        last = nc.scalar.activation(qst[96:128, p % 2, e, c * CH:(c + 1) * CH], bank[32 * e:32 * e + 32, :], ACT.Copy)
                    last.then_inc(mt_ready, 1)

            def exp(b, p, s):
                c, i = STEPS[s]
                off = max(0, i * P - c * CH)
                g = p * NST + s
                act.wait_ge(sc_done, b * NPAIR * NST + g + 1)
                if g >= 3:
                    act.wait_ge(pv_done, b * NPAIR * NST + g - 2)
                nc.scalar.activation(pr[:, g % 3, :, off:], sc[g % 2][:, :, off:], ACT.Exp, scale=SCALE).then_inc(exp_done, 1)

            def o_copy(b, n):
                act.wait_ge(pv_done, b * NPAIR * NST + (n // 2) * NST + (4, NST)[n % 2])
                p, c = n // 2, n % 2
                if p % 2 == 0 and p >= 2:
                    act.wait_ge(o_norm, b * 8 + p - 2 + c + 1)
                elif p == 0:
                    act.wait_ge(o_norm, b * 8)
                z = 64 * (p % 2)
                nc.scalar.activation(oV[z:z + 64, c, :], O[z:z + 64, :], ACT.Copy)
                nc.scalar.activation(oD[z:z + 64, c, :], O[64 - z:128 - z, :], ACT.Copy).then_inc(o_copied, 1)

            with act.Fori(0, NB) as b:
                act.wait_ge(mod_in, b * 128 + 128)
                for j in range(NT + 1):
                    if j < NT:
                        act.wait_ge(t_done, b * NT + j + 1)
                        if j >= 2:
                            act.wait_ge(hlo_ready, b * NT + j - 1)
                        else:
                            act.wait_ge(x1_out[j % 2], b * (NT // 2 * 16))
                        bank = rb[ring_at("hT", j) % 3]
                        for k in range(KC):
                            last = nc.scalar.activation(h[:, j % 2, k, :], bank[:, k * P:(k + 1) * P], ACT.Identity,
                                                        scale=mod_t[:, 1, k:k + 1], bias=mod_t[:, 0, k:k + 1])
                        last.then_inc(h_ready, 1)
                    if j >= 1:
                        act.wait_ge(v_done, b * NT + j)
                        nc.scalar.activation(V[:, (j - 1) * D:j * D], rb[ring_at("v", j - 1) % 3][:, :], ACT.Copy).then_inc(v_ready, 1)
                p_evac(b, 0)
                mt_evac(b, 0)
                for p in range(NPAIR):
                    if p % 2 and p + 1 < NPAIR:
                        p_evac(b, (p + 1) // 2)
                    for s in range(NST):
                        exp(b, p, s)
                        if s == 4:
                            o_copy(b, 2 * p)
                    o_copy(b, 2 * p + 1)
                    if p + 1 < NPAIR:
                        mt_evac(b, p + 1)

        @block.vector
        def _(dve):

            def ln_stats(b, j):
                dve.wait_ge(xa_in[j % 2], b * (NT // 2 * 16) + (j // 2 + 1) * 16)
                nc.vector.bn_stats(stats[:, j % 2, :], xa[:, j % 2, :]).then_inc(bn, 1)
                if j >= 2:
                    dve.wait_ge(rstd_ready, b * NT + j - 1)
                dve.wait_ge(bn, b * NT + j + 1)
                apart(dve)
                nc.vector.bn_aggr(mv[:, j % 2, :], stats[:, j % 2, :]).then_inc(mv_ready, 1)

            def ln_norm(b, j):
                dve.wait_ge(rstd_ready, b * NT + j + 1)
                nc.vector.tensor_scalar(xa[:, j % 2, :], xa[:, j % 2, :], mv[:, j % 2, 0:1], rstd[:, j % 2, 1:2],
                                        ALU.subtract, ALU.mult).then_inc(xn_ready, 1)

            def split_high(b, j):
                dve.wait_ge(h_ready, b * NT + j + 1)
                nc.vector.tensor_copy(hhi[:, :, j * P:(j + 1) * P], h[:, j % 2, :, :]).then_inc(hhi_ready, 1)

            def p_low(b, hg):
                for n in range(4):
                    which, c = n // 2, n % 2
                    bank = rb[ring_at("p", 4 * hg + n) % 3]
                    dve.wait_ge(p_hi, b * 16 + 4 * hg + n + 1)
                    nc.vector.scalar_tensor_tensor(st[:, which, 1, c * CH:(c + 1) * CH], bank[:, :],
                                                   K.bias[:, which * KC + hg:which * KC + hg + 1],
                                                   st[:, which, 0, c * CH:(c + 1) * CH].bitcast(f32),
                                                   ALU.add, ALU.subtract).then_inc(p_lo, 1)

            def m_reduce(b, p, n):
                heads, qt, k0, w, part = MUSES[n]
                bank = rb[ring_at("m", NM * p + n) % 3]
                dve.wait_ge(m_done, b * NPAIR * NM + p * NM + n + 1)
                nc.vector.tensor_reduce(mx[:, heads[0]:heads[-1] + 1, qt, part],
                                        bank[:, 0:len(heads) * w].rearrange("p (e k) -> p e k", e=len(heads)),
                                        AX.X, ALU.max).then_inc(m_red, 1)

            def m_rows(b, p):
                base = b * NPAIR * 3 + p * 3
                dve.wait_ge(m_red, b * NPAIR * NM + (p + 1) * NM)
                nc.vector.tensor_tensor(mx[:, :, 4:NT, 0], mx[:, :, 4:NT, 0], mx[:, :, 4:NT, 1], ALU.max).then_inc(mstep, 1)
                dve.wait_ge(mstep, base + 1)
                nc.vector.tensor_scalar(negm[:, :, :], mx[:, :, :, 0].rearrange("p e t -> p t e"), MASKED, -1.0, ALU.max, ALU.mult)\
                    .then_inc(mstep, 1)
                dve.wait_ge(mstep, base + 2)
                nc.vector.tensor_copy(mhi[:, :, :], negm[:, :, :]).then_inc(mstep, 1)
                dve.wait_ge(mstep, base + 3)
                dve.wait_ge(mt_done, b * 16 + 2 * p)
                nc.vector.tensor_copy(S_t[:, :, 0::32], mhi[:, :, :].bitcast(f32))
                nc.vector.tensor_tensor(S_t[:, :, 1::32], negm[:, :, :], mhi[:, :, :].bitcast(f32), ALU.subtract).then_inc(s_ready, 1)

            def o_recip(b, n):
                hg, c = n // 2, n % 2
                dve.wait_ge(o_copied, b * 16 + 4 * hg + 3 + c)
                nc.vector.reciprocal(oD[:, c, :], oD[:, c, :]).then_inc(o_rec, 1)

            with dve.Fori(0, NB) as b:
                ln_stats(b, 0)
                for j in range(NT):
                    if j + 1 < NT:
                        ln_stats(b, j + 1)
                    ln_norm(b, j)
                    if j >= 1:
                        split_high(b, j - 1)
                split_high(b, NT - 1)
                p_low(b, 0)
                for n in range(NM):
                    m_reduce(b, 0, n)
                m_rows(b, 0)
                for p in range(NPAIR):
                    if p % 2 and p + 1 < NPAIR:
                        p_low(b, (p + 1) // 2)
                    n = 0
                    for s in range(NST + 1):
                        if p + 1 < NPAIR:
                            while n < min(NM, 2 * s + 2):
                                m_reduce(b, p + 1, n)
                                n += 1
                        if s == 5 and p % 2:
                            o_recip(b, p - 1)
                    if p + 1 < NPAIR:
                        m_rows(b, p + 1)
                    if p % 2:
                        o_recip(b, p)
                dve.wait_ge(mod2_in, b * 32 + 32)
                for j in range(NT):
                    bank = rb[ring_at("w", j) % 3]
                    dve.wait_ge(w_done, b * NT + j + 1)
                    dve.wait_ge(x1_out[j % 2], b * (NT // 2 * 16) + (j // 2) * 16)
                    nc.vector.tensor_tensor(u[:, j % 2, :], bank[:, :], ga_bc[:, :], ALU.mult).then_inc(u_ready, 1)

        @block.tensor
        def _(pe):

            def bank_for(b, kind, n):
                at = ring_at(kind, n)
                if at < 3:
                    pe.wait_ge(u_ready, b * NT)
                else:
                    before = ring[at - 3]
                    pe.wait_ge(freed[before], b * TOTAL[before] + positions[before].index(at - 3) + 1)
                return rb[at % 3]

            def three_terms(out, hi, lo, whi, wlo, stationary_is_w, chunks, first=True, last=True):
                pass

            def transposes(b, j):
                bank = bank_for(b, "hT", j)
                pe.wait_ge(xn_ready, b * NT + j + 1)
                for k in range(KC):
                    last = nc.tensor.transpose(bank[:, k * P:(k + 1) * P], xa[:, j % 2, k * P:(k + 1) * P], K.ident[:, :])
                last.then_inc(t_done, 1)

            def values(b, j):
                bank = bank_for(b, "v", j)
                pe.wait_ge(hlo_ready, b * NT + j + 1)
                terms = [(x_, w_, k) for k in range(KC) for x_, w_ in ((hhi, K.whi), (hhi, K.wlo), (hlo, K.whi))]
                for n, (x_, w_, k) in enumerate(terms):
                    last = nc.tensor.matmul(bank[:, :], x_[:, k, j * P:(j + 1) * P], w_[:, k, 2 * D:3 * D],
                                            start=(n == 0), stop=(n == len(terms) - 1))
                last.then_inc(v_done, 1)

            def project(b, hg):
                for n in range(4):
                    which, c = n // 2, n % 2
                    bank = bank_for(b, "p", 4 * hg + n)
                    cols = slice(which * D + hg * P, which * D + (hg + 1) * P)
                    terms = [(w_, x_, k) for k in range(KC) for w_, x_ in ((K.whi, hhi), (K.whi, hlo), (K.wlo, hhi))]
                    for t, (w_, x_, k) in enumerate(terms):
                        last = nc.tensor.matmul(bank[:, :], w_[:, k, cols], x_[:, k, c * CH:(c + 1) * CH],
                                                start=(t == 0), stop=(t == len(terms) - 1))
                    last.then_inc(p_done, 1)

            def m_scores(b, p, n):
                heads, qt, k0, w, part = MUSES[n]
                bank = bank_for(b, "m", NM * p + n)
                diag = k0 <= qt * P < k0 + w
                for x_, e in enumerate(heads):
                    o = bank[:, x_ * w:(x_ + 1) * w]
                    last = nc.tensor.matmul(o, qst[0:96, p % 2, e, qt * P:(qt + 1) * P], kst[0:96, p % 2, e, k0:k0 + w],
                                            start=True, stop=not diag)
                    if diag:
                        last = nc.tensor.matmul(o[:, qt * P - k0:qt * P - k0 + P], K.identb[:, :], K.mask_qk[:, :],
                                                start=False, stop=True)
                last.then_inc(m_done, 1)

            def m_transpose(b, p):
                for c in range(2):
                    bank = bank_for(b, "mt", 2 * p + c)
                    pe.wait_ge(s_ready, b * NPAIR + p + 1)
                    apart(pe)
                    for t in range(4):
                        last = nc.tensor.transpose(bank[0:64, t * P:(t + 1) * P], S_t[:, 4 * c + t, :], K.ident[:, :])
                    last.then_inc(mt_done, 1)

            def scores(b, p, s):
                c, i = STEPS[s]
                off = max(0, i * P - c * CH)
                g = p * NST + s
                if g >= 2:
                    pe.wait_ge(exp_done, b * NPAIR * NST + g - 1)
                else:
                    pe.wait_ge(exp_done, b * NPAIR * NST)
                pe.wait_ge(mt_ready, b * 16 + 2 * p + c + 1)
                diag = i * P >= c * CH
                for e in range(2):
                    last = nc.tensor.matmul(sc[g % 2][:, e, off:], kst[:, p % 2, e, i * P:(i + 1) * P],
                                            qst[:, p % 2, e, c * CH + off:(c + 1) * CH], start=True, stop=not diag)
                    if diag:
                        last = nc.tensor.matmul(sc[g % 2][:, e, off:off + P], K.identb[:, :], K.mask_kq[:, :], start=False, stop=True)
                last.then_inc(sc_done, 1)

            def weighted(b, p, s):
                c, i = STEPS[s]
                off = max(0, i * P - c * CH)
                g = p * NST + s
                n = 2 * p + c
                if i == 0:
                    pe.wait_ge(o_copied, b * 16 + n)
                pe.wait_ge(exp_done, b * NPAIR * NST + g + 1)
                for e in range(2):
                    at = i * D + (2 * p + e) * DH
                    for z, col in ((p % 2, at), (1 - p % 2, NT * D)):
                        row = 64 * z + 32 * e
                        last = nc.tensor.matmul(O[row:row + 32, off:], V[:, col:col + DH], pr[:, g % 3, e, off:],
                                                start=(i == 0), stop=(i == 4 * c + 3))
                last.then_inc(pv_done, 1)

            def output(b, j):
                bank = bank_for(b, "w", j)
                pe.wait_ge(o_norm, b * 8 + 8)
                for k in range(KC):
                    last = nc.tensor.matmul(bank[:, :], oT[:, k, j * P:(j + 1) * P], K.wo[:, k, :], start=(k == 0), stop=(k == KC - 1))
                last.then_inc(w_done, 1)

            with pe.Fori(0, NB) as b:
                for j in range(NT):
                    transposes(b, j)
                    if j >= 1:
                        values(b, j - 1)
                values(b, NT - 1)
                project(b, 0)
                pe.wait_ge(stk_in[0], b * 4 * 192 + 192)
                for n in range(NM):
                    m_scores(b, 0, n)
                m_transpose(b, 0)
                for p in range(NPAIR):
                    if p % 2 and p + 1 < NPAIR:
                        project(b, (p + 1) // 2)
                    n = 0
                    for s in range(NST + 1):
                        if s < NST:
                            scores(b, p, s)
                        if p + 1 < NPAIR:
                            if s == 0:
                                pe.wait_ge(stk_in[(p + 1) % 2], b * 4 * 192 + ((p + 1) // 2 + 1) * 192)
                            while n < min(NM, 2 * s + 2):
                                m_scores(b, p + 1, n)
                                n += 1
                        if s >= 1:
                            weighted(b, p, s - 1)
                    if p + 1 < NPAIR:
                        m_transpose(b, p + 1)
                for j in range(NT):
                    output(b, j)


def apart(eng):
    eng.nop(nofuse=True)


class Kept:
    pass


def program_a(nc, K, ctx):
    f32, f32r, bf16 = mybir.dt.float32, mybir.dt.float32r, mybir.dt.bfloat16
    sb = lambda n, s, d=f32: ctx.enter_context(nc.sbuf_tensor(n, s, d))
    K.ident = sb("ident", [P, P])
    K.expo = sb("expo", [P, 1])
    a = ExitStack()
    with a:
        sb = lambda n, s, d=f32: a.enter_context(nc.sbuf_tensor(n, s, d))
        K.whi = sb("whi", [P, KC, 3 * D], f32r)
        K.wlo = sb("wlo", [P, KC, 3 * D], f32r)
        K.wo = sb("wo_sb", [P, KC, D])
        K.bias = sb("bias", [P, 3 * KC])
        K.identb = sb("identb", [P, P], bf16)
        K.mask_qk = sb("mask_qk", [P, P], bf16)
        K.mask_kq = sb("mask_kq", [P, P], bf16)
        K.V = sb("V", [P, NT * D + DH])
        K.S = sb("S", [P, NT, 64])
        K.kst = sb("kst", [P, 2, 2, S], f32r)
        with nc.sbuf_tensor("ones_row", [P, S], f32) as K.ones_row:
            setup_phase(nc, K)
        attention_phase(nc, K)

E = 16
NG, GSZ = 4, 4
F = 1024
FC = F // P
EI = 256
EC = EI // P
CH = 512
TPC = CH // P
NCH = T // CH
NTILE = T // P
REGION = T + P
NET = (2 * T + E * (P - 1)) // P
DUMMY = E * REGION
ROWS = DUMMY + P


def shared_setup(nc, K):
    f32, f32r, bf16 = mybir.dt.float32, mybir.dt.float32r, mybir.dt.bfloat16
    ALU, ACT = mybir.AluOpType, mybir.ActivationFunctionType
    ctx = ExitStack()
    with ctx:
        sb = lambda n, s, d=f32: ctx.enter_context(nc.sbuf_tensor(n, s, d))
        sem = lambda n: ctx.enter_context(nc.semaphore(n))
        up_raw = sb("up_raw", [P, KC, F])
        dn_raw = sb("dn_raw", [P, FC, D])
        rw_raw = sb("rw_raw", [E, D])
        zero = sb("zero", [P, D])
        pt = ctx.enter_context(nc.psum_tensor("pt_rw", [P, KC, E], f32))
        raw_in, rw_in, hi_done, lo_done, rw_t, rw_hi, rw_lo = (sem(n) for n in
            ("c_raw_in", "rw_in", "c_hi_done", "c_lo_done", "rw_t", "rw_hi", "rw_lo"))
        zeroed, consts, zero_out = sem("c_zeroed2"), sem("c_consts"), sem("zero_out")
        block = ctx.enter_context(nc.Block())

        @block.sync
        def _(sp):
            sp.dma_start(rw_raw[:, :], K.rw).then_inc(rw_in, 16)
            sp.dma_start(K.ebias[:, :], K.eb.rearrange("(a n) -> a n", a=1).broadcast_to([P, E])).then_inc(rw_in, 16)
            for k in range(KC):
                sp.dma_start(up_raw[:, k, :], K.sup[k * P:(k + 1) * P, :]).then_inc(raw_in, 16)
            sp.dma_start(dn_raw[:, :, :], K.sdn.rearrange("(k p) n -> p k n", p=P)).then_inc(raw_in, 16)
            sp.wait_ge(zeroed, 1)
            sp.dma_start(K.xs[DUMMY:DUMMY + P, :], zero[:, :]).then_inc(zero_out, 16)
            sp.wait_ge(zero_out, 16)

        @block.gpsimd
        def _(pool):
            nc.gpsimd.memset(zero[:, :], 0.0).then_inc(zeroed, 1)
            nc.gpsimd.memset(K.tri[:, :], 1.0).then_inc(zeroed, 1)
            nc.gpsimd.memset(K.ones[:, :], 1.0)
            nc.gpsimd.memset(K.expo[:, :], -0.5)
            pool.wait_ge(zeroed, 2)
            nc.gpsimd.affine_select(out=K.tri[:, :], in_=K.tri[:, :], compare_op=ALU.is_gt, fill=0.0, base=0,
                                    pattern=[[1, P]], channel_multiplier=-1).then_inc(consts, 1)
            pool.wait_ge(consts, 1)
            pool.wait_ge(hi_done, 2)
            nc.gpsimd.tensor_tensor(K.dnlo[:, :, :], dn_raw[:, :, :], K.dnhi[:, :, :].bitcast(f32), ALU.subtract).then_inc(lo_done, 1)
            pool.wait_ge(lo_done, 1)

        @block.scalar
        def _(act):
            act.wait_ge(raw_in, 16 * (KC + 1))
            nc.scalar.activation(K.uphi[:, :, :], up_raw[:, :, :], ACT.Copy).then_inc(hi_done, 1)
            nc.scalar.activation(K.dnhi[:, :, :], dn_raw[:, :, :], ACT.Copy).then_inc(hi_done, 1)

        @block.vector
        def _(dve):
            for e in range(E):
                nc.vector.memset(K.order[:, e:e + 1], float(E - e))
                nc.vector.memset(K.region[:, e:e + 1], float(e * REGION))
            for i in range(NG):
                for j in range(NG):
                    nc.vector.memset(K.gtri[:, j, i:i + 1], 1.0 if i < j else 0.0)
            nc.vector.memset(K.count[:, :], 0.0)
            dve.wait_ge(rw_t, 1)
            nc.vector.tensor_copy(K.rwhi[:, :, :], pt[:, :, :]).then_inc(rw_hi, 1)
            dve.wait_ge(rw_hi, 1)
            nc.vector.tensor_tensor(K.rwlo[:, :, :], pt[:, :, :], K.rwhi[:, :, :].bitcast(f32), ALU.subtract)
            dve.wait_ge(hi_done, 1)
            nc.vector.tensor_tensor(K.uplo[:, :, :], up_raw[:, :, :], K.uphi[:, :, :].bitcast(f32), ALU.subtract).then_inc(rw_lo, 1)
            dve.wait_ge(rw_lo, 1)

        @block.tensor
        def _(pe):
            pe.wait_ge(rw_in, 32)
            for k in range(KC):
                last = nc.tensor.transpose(pt[:, k, :], rw_raw[:, k * P:(k + 1) * P], K.ident[0:E, 0:E])
            last.then_inc(rw_t, 1)


def shared_phase(nc, K):
    f32, f32r, bf16, u32 = mybir.dt.float32, mybir.dt.float32r, mybir.dt.bfloat16, mybir.dt.uint32
    ALU, ACT, AX = mybir.AluOpType, mybir.ActivationFunctionType, mybir.AxisListType
    ctx = ExitStack()
    with ctx:
        sb = lambda n, s, d=f32: ctx.enter_context(nc.sbuf_tensor(n, s, d))
        pb = lambda n, s: ctx.enter_context(nc.psum_tensor(n, s, f32))
        sem = lambda n: ctx.enter_context(nc.semaphore(n))
        xb = sb("xb", [P, 2, TPC, D])
        h2 = sb("h2", [P, 2, TPC, D])
        bc = sb("bc", [P, 2, 3, D])
        stats = sb("stats2", [P, 2, 6])
        mv = sb("mv2", [P, 2, 2])
        rstd = sb("rstd2", [P, 2, 2])
        thi = sb("thi", [P, 2, KC, CH], f32r)
        tlo = sb("tlo", [P, 2, KC, CH], f32r)
        relu = sb("relu", [P, 2, CH])
        sq = sb("sq", [P, 2, CH])
        ahi = sb("ahi", [P, FC, CH], f32r)
        alo = sb("alo", [P, FC, CH], f32r)
        y = sb("y_sh", [P, 2, D])
        lg = sb("lg", [P, TPC, E])
        s_ = sb("s_", [P, TPC, E])
        sbias = sb("sbias", [P, TPC, E])
        g2 = sb("g2", [P, 6, TPC, NG])
        cmp = sb("cmp", [P, 3, TPC, NG, NG])
        rank = sb("rank", [P, TPC, NG])
        m16 = sb("m16", [P, 3, TPC, E])
        top = sb("top", [P, 2, TPC, 1])
        oh = sb("oh", [P, 2, TPC, E])
        chosen = sb("chosen", [P, TPC, E], bf16)
        ws = sb("ws", [P, 4, TPC])
        place = sb("place", [P, TPC, E])
        slotf = sb("slotf", [P, 2, TPC])
        slotu = sb("slotu", [P, 2, 2, TPC], u32)
        tp = [pb(f"tp{i}", [P, KC, P]) for i in range(2)]
        rp = pb("rp", [P, 512])
        pl = pb("pl", [P, 512])
        upb = [pb(f"up{i}", [P, CH]) for i in range(2)]
        dnb = [pb(f"dn{i}", [P, D]) for i in range(2)]

        xb_in = [sem(f"xb_in{i}") for i in range(2)]
        bc_in = [sem(f"bc_in{i}") for i in range(2)]
        bn, mv_ready, var_eps, rstd_ready = sem("bn2"), sem("mv2_ready"), sem("var_eps2"), sem("rstd2_ready")
        xn_ready, h2_scaled, h2_ready = sem("xn2_ready"), sem("h2_scaled"), sem("h2_ready")
        t_done, thi_ready, tlo_ready = sem("t2_done"), sem("thi_ready"), sem("tlo_ready")
        r_done, lg_ready, s_ready, step = sem("r_done"), sem("lg_ready"), sem("sig_ready"), sem("route_step")
        chosen_ready, place_done, slots_ready = sem("chosen_ready"), sem("place_done"), sem("slots_ready")
        sent = [sem(f"sent{i}") for i in range(2)]
        up_done, relu_ready, sq_ready, ahi_ready, alo_ready = (sem(n) for n in
            ("up_done", "relu_ready", "sq_ready", "ahi_ready", "alo_ready"))
        dn_done, y_scaled, y_ready = sem("dn_done"), sem("y_scaled"), sem("y_ready")
        y_out = [sem(f"y_out{i}") for i in range(2)]
        block = ctx.enter_context(nc.Block())

        def rounds(eng, first, chunk):
            first()
            with eng.Fori(0, NCH // 2 - 1) as i:
                chunk(2 * i, 0, True, i, 1)
                chunk(2 * i + 1, 1, True, i + 1, 0)
            chunk(NCH - 2, 0, True, NB - 1, 1)
            chunk(NCH - 1, 1, False, 0, 0)

        @block.sync
        def _(sp):
            def load(t0, par, b):
                sp.dma_start(bc[:, par, :, :], K.modd[bass.ds(b, 1), SB:GB + 1, :].broadcast_to([P, 3, D])).then_inc(bc_in[par], 16)
                sp.dma_start(xb[:, par, :, :], K.x1d[bass.ds(t0 * CH, CH), :].rearrange("(j p) d -> p j d", p=P)).then_inc(xb_in[par], 16)

            def chunk(q, par, nxt, b, half):
                if nxt:
                    sp.wait_ge(y_ready, q * TPC)
                    load(q + 1, 1 - par, b)
                for j in range(TPC):
                    sp.wait_ge(y_ready, q * TPC + j + 1)
                    sp.dma_start(K.part[bass.ds(q * CH + j * P, P), :], y[:, j % 2, :]).then_inc(y_out[j % 2], 16)

            rounds(sp, lambda: load(0, 0, 0), chunk)
            for i in range(2):
                sp.wait_ge(y_out[i], NCH * TPC // 2 * 16)

        @block.gpsimd
        def _(pool):

            def norm(r, par, j, b):
                if j < TPC:
                    pool.wait_ge(mv_ready, r * TPC + j + 1)
                    apart(pool)
                    nc.gpsimd.tensor_scalar(rstd[:, j % 2, 0:1], mv[:, j % 2, 1:2], EPS, None, ALU.add).then_inc(var_eps, 1)
                    pool.wait_ge(var_eps, r * TPC + j + 1)
                    nc.gpsimd.tensor_tensor(rstd[:, j % 2, 1:2], rstd[:, j % 2, 0:1], K.expo[:, 0:1], ALU.pow).then_inc(rstd_ready, 1)
                if j >= 1:
                    i = j - 1
                    pool.wait_ge(xn_ready, r * TPC + i + 1)
                    if i == 0:
                        pool.wait_ge(bc_in[par], b * 16 + 16)
                    nc.gpsimd.tensor_tensor(h2[:, par, i, :], h2[:, par, i, :], bc[:, par, 1, :], ALU.mult).then_inc(h2_scaled, 1)
                    pool.wait_ge(h2_scaled, r * TPC + i + 1)
                    nc.gpsimd.tensor_tensor(h2[:, par, i, :], h2[:, par, i, :], bc[:, par, 0, :], ALU.add).then_inc(h2_ready, 1)

            def low(q, m):
                pool.wait_ge(ahi_ready, q * FC + m + 1)
                nc.gpsimd.tensor_tensor(alo[:, m, :], sq[:, m % 2, :], ahi[:, m, :].bitcast(f32), ALU.subtract).then_inc(alo_ready, 1)

            def send(r, par):
                pool.wait_ge(slots_ready, r + 1)
                apart(pool)
                for c in range(2):
                    for j in range(TPC):
                        nc.gpsimd.indirect_dma_start(out=K.xs, out_offset=bass.IndirectOffsetOnAxis(ap=slotu[:, par, c, j:j + 1], axis=0),
                                                     in_=h2[:, par, j, :], in_offset=None).then_inc(sent[par], 16)

            def first():
                for j in range(TPC + 1):
                    norm(0, 0, j, 0)
                send(0, 0)

            def chunk(q, par, nxt, b, half):
                for m in range(FC):
                    if nxt and m % 2 == 0:
                        norm(q + 1, 1 - par, m // 2, b)
                    low(q, m)
                if nxt:
                    norm(q + 1, 1 - par, TPC, b)
                for j in range(TPC):
                    pool.wait_ge(y_scaled, q * TPC + j + 1)
                    nc.gpsimd.tensor_tensor(y[:, j % 2, :], y[:, j % 2, :], xb[:, par, j, :], ALU.add).then_inc(y_ready, 1)
                if nxt:
                    send(q + 1, 1 - par)

            rounds(pool, first, chunk)
            for i in range(2):
                pool.wait_ge(sent[i], NCH * TPC * 16)

        @block.scalar
        def _(act):
            def high(r, par, j):
                act.wait_ge(t_done, r * TPC + j + 1)
                nc.scalar.activation(thi[:, par, :, j * P:(j + 1) * P], tp[j % 2][:, :, :], ACT.Copy).then_inc(thi_ready, 1)

            def sigmoid(r):
                act.wait_ge(lg_ready, r * TPC + TPC)
                nc.scalar.activation(s_[:, :, :], lg[:, :, :], ACT.Sigmoid).then_inc(s_ready, 1)

            def first():
                for j in range(TPC):
                    high(0, 0, j)
                sigmoid(0)

            def chunk(q, par, nxt, b, half):
                for m in range(FC + 1):
                    if m < FC:
                        act.wait_ge(up_done, q * FC + m + 1)
                        if m >= 2:
                            act.wait_ge(sq_ready, q * FC + m - 1)
                        else:
                            act.wait_ge(sq_ready, q * FC)
                        nc.scalar.activation(relu[:, m % 2, :], upb[m % 2][:, :], ACT.Relu).then_inc(relu_ready, 1)
                    if m >= 1:
                        act.wait_ge(sq_ready, q * FC + m)
                        nc.scalar.activation(ahi[:, m - 1, :], sq[:, (m - 1) % 2, :], ACT.Copy).then_inc(ahi_ready, 1)
                    if nxt and m % 2 == 0 and m:
                        high(q + 1, 1 - par, m // 2 - 1)
                if nxt:
                    sigmoid(q + 1)

            rounds(act, first, chunk)

        @block.vector
        def _(dve):
            STEPS_R = 32

            def ln(r, par, j, b):
                if j < TPC:
                    if j == 0:
                        dve.wait_ge(xb_in[par], b * 16 + 16)
                    nc.vector.bn_stats(stats[:, j % 2, :], xb[:, par, j, :]).then_inc(bn, 1)
                    dve.wait_ge(bn, r * TPC + j + 1)
                    apart(dve)
                    nc.vector.bn_aggr(mv[:, j % 2, :], stats[:, j % 2, :]).then_inc(mv_ready, 1)
                if j >= 1:
                    i = j - 1
                    dve.wait_ge(rstd_ready, r * TPC + i + 1)
                    nc.vector.tensor_scalar(h2[:, par, i, :], xb[:, par, i, :], mv[:, i % 2, 0:1], rstd[:, i % 2, 1:2],
                                            ALU.subtract, ALU.mult).then_inc(xn_ready, 1)

            def low(r, par, j):
                dve.wait_ge(thi_ready, r * TPC + j + 1)
                nc.vector.tensor_tensor(tlo[:, par, :, j * P:(j + 1) * P], tp[j % 2][:, :, :],
                                        thi[:, par, :, j * P:(j + 1) * P].bitcast(f32), ALU.subtract).then_inc(tlo_ready, 1)

            def logits(r, j):
                dve.wait_ge(r_done, r * TPC + j + 1)
                nc.vector.tensor_copy(lg[:, j, :], rp[:, 0:E]).then_inc(lg_ready, 1)

            n = [0]

            def step_of(r):
                def then(ins):
                    n[0] += 1
                    ins.then_inc(step, 1)
                    dve.wait_ge(step, r * STEPS_R + n[0])
                return then

            def route(r, par):
                n[0] = 0
                then = step_of(r)
                tt, ts, red = nc.vector.tensor_tensor, nc.vector.tensor_scalar, nc.vector.tensor_reduce
                dve.wait_ge(s_ready, r + 1)
                then(tt(sbias[:, :, :], s_[:, :, :], K.ebias[:, :].unsqueeze(1).broadcast_to([P, TPC, E]), ALU.add))
                v = sbias[:, :, :].rearrange("p t (g a b) -> p t g a b", a=2, b=2)
                tt(g2[:, 0, :, :], v[:, :, :, 0, 0], v[:, :, :, 0, 1], ALU.max)
                tt(g2[:, 1, :, :], v[:, :, :, 1, 0], v[:, :, :, 1, 1], ALU.max)
                tt(g2[:, 2, :, :], v[:, :, :, 0, 0], v[:, :, :, 0, 1], ALU.min)
                then(tt(g2[:, 3, :, :], v[:, :, :, 1, 0], v[:, :, :, 1, 1], ALU.min))
                tt(g2[:, 4, :, :], g2[:, 0, :, :], g2[:, 1, :, :], ALU.min)
                tt(g2[:, 5, :, :], g2[:, 2, :, :], g2[:, 3, :, :], ALU.max)
                then(tt(g2[:, 0, :, :], g2[:, 0, :, :], g2[:, 1, :, :], ALU.max))
                then(tt(g2[:, 1, :, :], g2[:, 4, :, :], g2[:, 5, :, :], ALU.max))
                then(tt(g2[:, 2, :, :], g2[:, 0, :, :], g2[:, 1, :, :], ALU.add))
                gi = g2[:, 2, :, :].unsqueeze(2).broadcast_to([P, TPC, NG, NG])
                gj = g2[:, 2, :, :].unsqueeze(3).broadcast_to([P, TPC, NG, NG])
                tt(cmp[:, 0], gi, gj, ALU.is_gt)
                then(tt(cmp[:, 1], gi, gj, ALU.is_equal))
                then(tt(cmp[:, 1], cmp[:, 1], K.gtri[:, :, :].unsqueeze(1).broadcast_to([P, TPC, NG, NG]), ALU.mult))
                then(tt(cmp[:, 0], cmp[:, 0], cmp[:, 1], ALU.add))
                then(red(rank[:, :, :], cmp[:, 0], AX.X, ALU.add))
                then(ts(rank[:, :, :], rank[:, :, :], float(2), None, ALU.is_lt))
                masked = m16[:, 0, :, :]
                then(tt(masked.rearrange("p t (g i) -> p t g i", i=GSZ), sbias[:, :, :].rearrange("p t (g i) -> p t g i", i=GSZ),
                        rank[:, :, :].unsqueeze(3).broadcast_to([P, TPC, NG, GSZ]), ALU.mult))
                order = K.order[:, :].unsqueeze(1).broadcast_to([P, TPC, E])
                for c in range(2):
                    then(red(top[:, 0, :, 0], masked, AX.X, ALU.max))
                    then(tt(m16[:, 1, :, :], masked, top[:, 0, :, :].broadcast_to([P, TPC, E]), ALU.is_equal))
                    then(tt(m16[:, 1, :, :], m16[:, 1, :, :], order, ALU.mult))
                    then(red(top[:, 1, :, 0], m16[:, 1, :, :], AX.X, ALU.max))
                    nc.vector.tensor_copy(K.choice[:, c, bass.ds(r * TPC, TPC)], top[:, 1, :, 0])
                    then(tt(oh[:, c, :, :], order, top[:, 1, :, :].broadcast_to([P, TPC, E]), ALU.is_equal))
                    if c == 0:
                        then(nc.vector.scalar_tensor_tensor(m16[:, 0, :, :], oh[:, 0, :, :], -3e38, masked, ALU.mult, ALU.add))
                nc.vector.tensor_tensor(chosen[:, :, :], oh[:, 0, :, :], oh[:, 1, :, :], ALU.add).then_inc(chosen_ready, 1)
                for c in range(2):
                    last = tt(m16[:, 1 + c, :, :], oh[:, c, :, :], s_[:, :, :], ALU.mult)
                then(last)
                red(ws[:, 0, :], m16[:, 1, :, :], AX.X, ALU.add)
                then(red(ws[:, 1, :], m16[:, 2, :, :], AX.X, ALU.add))
                then(tt(ws[:, 2, :], ws[:, 0, :], ws[:, 1, :], ALU.add))
                then(ts(ws[:, 2, :], ws[:, 2, :], 1e-20, None, ALU.add))
                then(nc.vector.reciprocal(ws[:, 3, :], ws[:, 2, :]))
                for c in range(2):
                    tt(K.wts[:, c, bass.ds(r * TPC, TPC)], ws[:, c, :], ws[:, 3, :], ALU.mult)

            def place_rows(r, par):
                then = step_of(r)
                tt, red = nc.vector.tensor_tensor, nc.vector.tensor_reduce
                dve.wait_ge(place_done, r + 1)
                then(tt(place[:, :, :], pl[:, 0:TPC * E].rearrange("p (t e) -> p t e", e=E),
                        K.count[:, :].unsqueeze(1).broadcast_to([P, TPC, E]), ALU.add))
                then(tt(K.count[:, :], K.count[:, :], pl[:, TPC * E:(TPC + 1) * E], ALU.add))
                then(tt(place[:, :, :], place[:, :, :], K.region[:, :].unsqueeze(1).broadcast_to([P, TPC, E]), ALU.add))
                for c in range(2):
                    last = tt(m16[:, 1 + c, :, :], place[:, :, :], oh[:, c, :, :], ALU.mult)
                then(last)
                for c in range(2):
                    last = red(slotf[:, c, :], m16[:, 1 + c, :, :], AX.X, ALU.add)
                then(last)
                nc.vector.tensor_copy(K.slots[:, :, bass.ds(r * TPC, TPC)], slotf[:, :, :])
                nc.vector.tensor_copy(slotu[:, par, :, :], slotf[:, :, :]).then_inc(slots_ready, 1)
                assert n[0] == STEPS_R, n[0]

            def square(q, m):
                dve.wait_ge(relu_ready, q * FC + m + 1)
                if m >= 2:
                    dve.wait_ge(alo_ready, q * FC + m - 1)
                else:
                    dve.wait_ge(alo_ready, q * FC)
                nc.vector.tensor_tensor(sq[:, m % 2, :], relu[:, m % 2, :], relu[:, m % 2, :], ALU.mult).then_inc(sq_ready, 1)

            def scaled(q, par, j):
                dve.wait_ge(dn_done, q * TPC + j + 1)
                dve.wait_ge(y_out[j % 2], q * (TPC // 2 * 16) + j // 2 * 16)
                nc.vector.tensor_tensor(y[:, j % 2, :], dnb[j % 2][:, :], bc[:, par, 2, :], ALU.mult).then_inc(y_scaled, 1)

            def first():
                for j in range(TPC + 1):
                    ln(0, 0, j, 0)
                for j in range(TPC):
                    low(0, 0, j)
                    if j >= 1:
                        logits(0, j - 1)
                logits(0, TPC - 1)
                route(0, 0)
                place_rows(0, 0)

            def chunk(q, par, nxt, b, half):
                if nxt:
                    dve.wait_ge(sent[1 - par], b * (TPC * 2 * 16))
                for m in range(FC):
                    if nxt and m % 2 == 0:
                        ln(q + 1, 1 - par, m // 2, b)
                    if nxt and m == 7:
                        ln(q + 1, 1 - par, TPC, b)
                    square(q, m)
                    if nxt and m >= 3 and m % 2:
                        low(q + 1, 1 - par, (m - 3) // 2)
                        if m >= 5:
                            logits(q + 1, (m - 5) // 2)
                if nxt:
                    logits(q + 1, TPC - 2)
                    low(q + 1, 1 - par, TPC - 1)
                scaled(q, par, 0)
                if nxt:
                    logits(q + 1, TPC - 1)
                    route(q + 1, 1 - par)
                scaled(q, par, 1)
                scaled(q, par, 2)
                if nxt:
                    place_rows(q + 1, 1 - par)
                scaled(q, par, 3)

            rounds(dve, first, chunk)

        @block.tensor
        def _(pe):
            def transposes(r, par, j):
                pe.wait_ge(h2_ready, r * TPC + j + 1)
                if j >= 2:
                    pe.wait_ge(tlo_ready, r * TPC + j - 1)
                else:
                    pe.wait_ge(tlo_ready, r * TPC)
                for k in range(KC):
                    last = nc.tensor.transpose(tp[j % 2][:, k, :], h2[:, par, j, k * P:(k + 1) * P], K.ident[:, :])
                last.then_inc(t_done, 1)

            def router(r, par, j):
                pe.wait_ge(tlo_ready, r * TPC + j + 1)
                pe.wait_ge(lg_ready, r * TPC + j)
                terms = [(x_, w_, k) for k in range(KC) for x_, w_ in ((thi, K.rwhi), (thi, K.rwlo), (tlo, K.rwhi))]
                for n, (x_, w_, k) in enumerate(terms):
                    last = nc.tensor.matmul(rp[:, 0:E], x_[:, par, k, j * P:(j + 1) * P], w_[:, k, :],
                                            start=(n == 0), stop=(n == len(terms) - 1))
                last.then_inc(r_done, 1)

            def places(r):
                pe.wait_ge(chosen_ready, r + 1)
                for j in range(TPC + 1):
                    o = pl[:, j * E:(j + 1) * E]
                    for i in range(j):
                        last = nc.tensor.matmul(o, K.ones[:, :], chosen[:, i, :], start=(i == 0), stop=(i == j - 1 and j == TPC))
                    if j < TPC:
                        last = nc.tensor.matmul(o, K.tri[:, :], chosen[:, j, :], start=(j == 0), stop=True)
                last.then_inc(place_done, 1)

            def up(q, par, m):
                if m >= 2:
                    pe.wait_ge(relu_ready, q * FC + m - 1)
                else:
                    pe.wait_ge(relu_ready, q * FC)
                terms = [(w_, x_, k) for k in range(KC) for w_, x_ in ((K.uphi, thi), (K.uphi, tlo), (K.uplo, thi))]
                for n, (w_, x_, k) in enumerate(terms):
                    last = nc.tensor.matmul(upb[m % 2][:, :], w_[:, k, m * P:(m + 1) * P], x_[:, par, k, :],
                                            start=(n == 0), stop=(n == len(terms) - 1))
                last.then_inc(up_done, 1)

            def down(q, j):
                if j >= 2:
                    pe.wait_ge(y_scaled, q * TPC + j - 1)
                else:
                    pe.wait_ge(y_scaled, q * TPC)
                for k in range(FC):
                    if j == 0:
                        pe.wait_ge(alo_ready, q * FC + k + 1)
                    for n, (a_, w_) in enumerate(((ahi, K.dnhi), (ahi, K.dnlo), (alo, K.dnhi))):
                        last = nc.tensor.matmul(dnb[j % 2][:, :], a_[:, k, j * P:(j + 1) * P], w_[:, k, :],
                                                start=(k == 0 and n == 0), stop=(k == FC - 1 and n == 2))
                last.then_inc(dn_done, 1)

            def first():
                for j in range(TPC):
                    transposes(0, 0, j)
                    if j >= 1:
                        router(0, 0, j - 1)
                router(0, 0, TPC - 1)
                places(0)

            def chunk(q, par, nxt, b, half):
                for m in range(FC):
                    up(q, par, m)
                    if nxt and m % 2 == 0 and m >= 2:
                        if m >= 4:
                            router(q + 1, 1 - par, m // 2 - 2)
                        transposes(q + 1, 1 - par, m // 2 - 1)
                down(q, 0)
                if nxt:
                    router(q + 1, 1 - par, TPC - 2)
                    transposes(q + 1, 1 - par, TPC - 1)
                down(q, 1)
                if nxt:
                    router(q + 1, 1 - par, TPC - 1)
                down(q, 2)
                if nxt:
                    places(q + 1)
                down(q, 3)

            rounds(pe, first, chunk)


def program_c(nc, K, ctx):
    f32, f32r, bf16 = mybir.dt.float32, mybir.dt.float32r, mybir.dt.bfloat16
    with ExitStack() as a:
        sb = lambda n, s, d=f32: a.enter_context(nc.sbuf_tensor(n, s, d))
        K.uphi = sb("uphi", [P, KC, F], f32r)
        K.uplo = sb("uplo", [P, KC, F], f32r)
        K.dnhi = sb("dnhi", [P, FC, D], f32r)
        K.dnlo = sb("dnlo", [P, FC, D], f32r)
        K.rwhi = sb("rwhi", [P, KC, E], f32r)
        K.rwlo = sb("rwlo", [P, KC, E], f32r)
        K.ebias = sb("ebias", [P, E])
        K.order = sb("order", [P, E])
        K.region = sb("region", [P, E])
        K.gtri = sb("gtri", [P, NG, NG])
        K.tri = sb("tri", [P, P], bf16)
        K.ones = sb("ones", [P, P], bf16)
        shared_setup(nc, K)
        shared_phase(nc, K)

AHEAD = 3
XR = 4


def expert_setup(nc, K):
    f32, i32 = mybir.dt.float32, mybir.dt.int32
    ALU, AX = mybir.AluOpType, mybir.AxisListType
    ctx = ExitStack()
    with ctx:
        sb = lambda n, s, d=f32: ctx.enter_context(nc.sbuf_tensor(n, s, d))
        sem = lambda n: ctx.enter_context(nc.semaphore(n))
        zero = sb("zero_rows", [P, D])
        k_i, j_i, e_i = sb("k_i", [P, NTILE], i32), sb("j_i", [P, NET], i32), sb("e_i", [P, E], i32)
        kf, jf, ef = sb("kf", [P, NTILE]), sb("jf", [P, NET]), sb("ef", [P, E])
        more = sb("more", [P, E, NTILE])
        ntile = sb("ntile", [P, E])
        ones = sb("ones_e", [P, E])
        ends = sb("ends", [P, E])
        starts = sb("starts", [P, E])
        base = sb("base", [P, E])
        inside = sb("inside", [P, NET, E])
        other = sb("other", [P, NET, E])
        rowf = sb("rowf", [P, 4, NET])
        padf = sb("padf", [P, E])
        order, shift = sb("order_e", [P, E]), sb("shift", [P, E])
        mine = sb("mine", [P, 2 * NTILE, E])
        moved = sb("moved", [P, 2 * NTILE])
        padi = sb("padi", [P, E], i32)
        iotas, zeroed, step, tables = sem("iotas"), sem("rows_zeroed"), sem("table_step"), sem("tables")
        w_in, padded = sem("we_in"), sem("padded")
        block = ctx.enter_context(nc.Block())

        @block.sync
        def _(sp):
            for e in range(E):
                sp.dma_start(K.wu[:, e * KC * EI:(e + 1) * KC * EI].rearrange("p (k n) -> p k n", k=KC),
                             K.wup[e, :, :].rearrange("(k p) n -> p k n", p=P)).then_inc(w_in, 16)
            sp.wait_ge(tables, 1)
            sp.wait_ge(zeroed, 1)
            for e in range(E):
                row = sp.value_load(padi[0:1, e:e + 1], min_val=e * REGION, max_val=e * REGION + T)
                sp.dma_start(K.xs[bass.ds(row, P), :], zero[:, :]).then_inc(padded, 16)
            sp.wait_ge(padded, 16 * E)
            sp.wait_ge(w_in, 16 * 2 * E)

        @block.scalar
        def _(act):
            for e in range(E):
                act.dma_start(K.wd[:, e * EC * D:(e + 1) * EC * D].rearrange("p (k n) -> p k n", k=EC),
                              K.wdn[e, :, :].rearrange("(k p) n -> p k n", p=P)).then_inc(w_in, 16)

        @block.gpsimd
        def _(pool):
            nc.gpsimd.memset(zero[:, :], 0.0).then_inc(zeroed, 1)
            nc.gpsimd.iota(k_i[:, :], pattern=[[P, NTILE]], base=0, channel_multiplier=0).then_inc(iotas, 1)
            nc.gpsimd.iota(j_i[:, :], pattern=[[1, NET]], base=0, channel_multiplier=0).then_inc(iotas, 1)
            nc.gpsimd.iota(e_i[:, :], pattern=[[1, E]], base=0, channel_multiplier=0).then_inc(iotas, 1)

        @block.vector
        def _(dve):
            n = [0]

            def then(ins):
                n[0] += 1
                ins.then_inc(step, 1)
                dve.wait_ge(step, n[0])

            tt, ts, red = nc.vector.tensor_tensor, nc.vector.tensor_scalar, nc.vector.tensor_reduce
            dve.wait_ge(iotas, 3)
            nc.vector.memset(ones[:, :], 1.0)
            nc.vector.tensor_copy(kf[:, :], k_i[:, :])
            nc.vector.tensor_copy(jf[:, :], j_i[:, :])
            then(nc.vector.tensor_copy(ef[:, :], e_i[:, :]))
            then(tt(more[:, :, :], K.count[:, :].unsqueeze(2).broadcast_to([P, E, NTILE]),
                    kf[:, :].unsqueeze(1).broadcast_to([P, E, NTILE]), ALU.is_gt))
            then(red(ntile[:, :], more[:, :, :], AX.X, ALU.add))
            then(nc.vector.tensor_tensor_scan(ends[:, :], ones[:, :], ntile[:, :], 0.0, ALU.mult, ALU.add))
            then(tt(starts[:, :], ends[:, :], ntile[:, :], ALU.subtract))
            then(ts(base[:, :], starts[:, :], -float(P), -float(DUMMY), ALU.mult, ALU.add))
            ts(padf[:, :], ef[:, :], float(REGION), None, ALU.mult)
            then(nc.vector.scalar_tensor_tensor(base[:, :], ef[:, :], float(REGION), base[:, :], ALU.mult, ALU.add))
            then(tt(padf[:, :], padf[:, :], K.count[:, :], ALU.add))
            nc.vector.tensor_copy(padi[:, :], padf[:, :])
            bj = jf[:, :].unsqueeze(2).broadcast_to([P, NET, E])
            be = lambda a: a[:, :].unsqueeze(1).broadcast_to([P, NET, E])
            bc = K.choice[:, :, :].rearrange("p c t -> p (c t)").unsqueeze(2).broadcast_to([P, 2 * NTILE, E])
            bx = lambda a: a[:, :].unsqueeze(1).broadcast_to([P, 2 * NTILE, E])
            ts(order[:, :], ef[:, :], -1.0, float(E), ALU.mult, ALU.add)
            then(ts(shift[:, :], base[:, :], float(DUMMY), None, ALU.add))
            then(tt(mine[:, :, :], bc, bx(order), ALU.is_equal))
            then(tt(mine[:, :, :], mine[:, :, :], bx(shift), ALU.mult))
            then(red(moved[:, :], mine[:, :, :], AX.X, ALU.add))
            then(tt(moved[:, :], K.slots[:, :, :].rearrange("p c t -> p (c t)"), moved[:, :], ALU.subtract))
            nc.vector.tensor_copy(K.rows[:, :, :].rearrange("p c t -> p (c t)"), moved[:, :])
            tt(inside[:, :, :], be(starts), bj, ALU.is_le)
            then(tt(other[:, :, :], be(ends), bj, ALU.is_le))
            then(tt(inside[:, :, :], inside[:, :, :], other[:, :, :], ALU.subtract))
            red(rowf[:, 0, :], inside[:, :, :], AX.X, ALU.add)
            then(tt(other[:, :, :], inside[:, :, :], be(base), ALU.mult))
            then(red(rowf[:, 1, :], other[:, :, :], AX.X, ALU.add))
            then(tt(other[:, :, :], inside[:, :, :], be(ef), ALU.mult))
            then(red(rowf[:, 2, :], other[:, :, :], AX.X, ALU.add))
            nc.vector.tensor_copy(K.eid[:, :], rowf[:, 2, :])
            then(ts(rowf[:, 3, :], jf[:, :], float(P), None, ALU.mult))
            then(tt(rowf[:, 3, :], rowf[:, 3, :], rowf[:, 0, :], ALU.mult))
            then(tt(rowf[:, 3, :], rowf[:, 3, :], rowf[:, 1, :], ALU.add))
            then(ts(rowf[:, 0, :], rowf[:, 3, :], float(DUMMY), None, ALU.add))
            nc.vector.tensor_copy(K.xrow[:, :], rowf[:, 0, :]).then_inc(tables, 1)


def expert_phase(nc, K):
    f32 = mybir.dt.float32
    ALU, ACT = mybir.AluOpType, mybir.ActivationFunctionType
    ctx = ExitStack()
    with ctx:
        sb = lambda n, s, d=f32: ctx.enter_context(nc.sbuf_tensor(n, s, d))
        pb = lambda n, s: ctx.enter_context(nc.psum_tensor(n, s, f32))
        sem = lambda n: ctx.enter_context(nc.semaphore(n))
        x = sb("x_e", [P, XR, D])
        xT = sb("xT_e", [P, 2, KC, P])
        r = sb("r_e", [P, 2, EI])
        a = sb("a_e", [P, 2, EI])
        aT = sb("aT_e", [P, 2, EC, P])
        y = sb("y_e", [P, XR, D])
        txb = [pb(f"tx{i}", [P, KC, P]) for i in range(2)]
        ub = [pb(f"ue{i}", [P, 512]) for i in range(2)]
        tab = [pb(f"ta{i}", [P, 512]) for i in range(2)]
        db = [pb(f"de{i}", [P, D]) for i in range(2)]
        x_in = [sem(f"xe_in{i}") for i in range(XR)]
        y_out = [sem(f"ye_out{i}") for i in range(XR)]
        tx_done, xT_ready, u_done, r_ready, a_ready, ta_done, aT_ready, d_done, y_ready = (sem(n) for n in
            ("tx_done", "xT_ready", "ue_done", "re_ready", "ae_ready", "ta_done", "aT_ready", "de_done", "ye_ready"))
        block = ctx.enter_context(nc.Block())
        FULL = (NET - AHEAD) // XR * XR

        def rounds(eng, round_):
            for j in range(-AHEAD, XR):
                round_(j, j % XR)
            with eng.Fori(1, FULL // XR) as i:
                for s in range(XR):
                    round_(i * XR + s, s)
            for j in range(FULL, NET):
                round_(j, j % XR)

        def known(j):
            return isinstance(j, int)

        def has(j):
            return not known(j) or 0 <= j < NET

        def wait(eng, s, value):
            if not (known(value) and value <= 0):
                eng.wait_ge(s, value)

        @block.sync
        def _(sp):
            def load(j, k, s):
                if has(j + k if known(j) else j):
                    t = j + k
                    wait(sp, tx_done, t - XR + 1)
                    row = sp.value_load(K.xrow[0:1, t:t + 1] if known(t) else K.xrow[0:1, bass.ds(t, 1)], min_val=0, max_val=ROWS - P)
                    sp.dma_start(x[:, (s + k) % XR, :], K.xs[bass.ds(row, P), :]).then_inc(x_in[(s + k) % XR], 16)

            def store(j, s):
                if has(j):
                    wait(sp, y_ready, j + 1)
                    sp.dma_start(K.ys[bass.ds(j * P, P), :], y[:, s, :]).then_inc(y_out[s], 16)

            for t in range(AHEAD):
                load(t - 2 * AHEAD, 2 * AHEAD, (t - 2 * AHEAD) % XR)
            for j in range(-AHEAD, 0):
                load(j, 2 * AHEAD, j % XR)
            L = (NET - 2 * AHEAD) // XR * XR
            with sp.Fori(0, L // XR) as i:
                for s in range(XR):
                    load(i * XR + s, 2 * AHEAD, s)
                    store(i * XR + s, s)
            for j in range(L, NET):
                load(j, 2 * AHEAD, j % XR)
                store(j, j % XR)
            for s in range(XR):
                sp.wait_ge(y_out[s], 16 * len(range(s, NET, XR)))

        @block.scalar
        def _(act):
            def round_(j, s):
                if has(j + 3 if known(j) else j):
                    act.wait_ge(tx_done, j + 4)
                    wait(act, u_done, j + 2)
                    nc.scalar.activation(xT[:, (s + 3) % 2, :, :], txb[(s + 3) % 2][:, :, :], ACT.Copy).then_inc(xT_ready, 1)
                if has(j + 2 if known(j) else j):
                    act.wait_ge(u_done, j + 3)
                    wait(act, a_ready, j + 1)
                    nc.scalar.activation(r[:, s % 2, :], ub[s % 2][:, 0:EI], ACT.Relu).then_inc(r_ready, 1)

            rounds(act, round_)

        @block.vector
        def _(dve):
            def round_(j, s):
                if has(j + 2 if known(j) else j):
                    dve.wait_ge(r_ready, j + 3)
                    wait(dve, ta_done, j + 1)
                    nc.vector.tensor_tensor(a[:, s % 2, :], r[:, s % 2, :], r[:, s % 2, :], ALU.mult).then_inc(a_ready, 1)
                if has(j + 1 if known(j) else j):
                    dve.wait_ge(ta_done, j + 2)
                    wait(dve, d_done, j)
                    nc.vector.tensor_copy(aT[:, (s + 1) % 2, :, :], tab[(s + 1) % 2][:, 0:EC * P]).then_inc(aT_ready, 1)
                if has(j):
                    dve.wait_ge(d_done, j + 1)
                    if known(j):
                        wait(dve, y_out[s], j // XR * 16)
                    else:
                        dve.wait_ge(y_out[s], (j - s) * (16 // XR))
                    nc.vector.tensor_copy(y[:, s, :], db[s % 2][:, :]).then_inc(y_ready, 1)

            rounds(dve, round_)

        @block.tensor
        def _(pe):
            def expert(t):
                return pe.value_load(K.eid[0:1, t:t + 1] if known(t) else K.eid[0:1, bass.ds(t, 1)], min_val=0, max_val=E - 1)

            def round_(j, s):
                if has(j + 3 if known(j) else j):
                    t, z = j + 3, (s + 3) % XR
                    pe.wait_ge(x_in[z], t // XR * 16 + 16 if known(t) else (j - s) * (16 // XR) + ((s + 3) // XR + 1) * 16)
                    wait(pe, xT_ready, j + 2)
                    for k in range(KC):
                        last = nc.tensor.transpose(txb[z % 2][:, k, :], x[:, z, k * P:(k + 1) * P], K.ident[:, :])
                    last.then_inc(tx_done, 1)
                if has(j + 2 if known(j) else j):
                    e = expert(j + 2)
                    pe.wait_ge(xT_ready, j + 3)
                    wait(pe, r_ready, j + 1)
                    for k in range(KC):
                        last = nc.tensor.matmul(ub[s % 2][:, 0:EI], xT[:, s % 2, k, :], K.wu[:, bass.ds(e * (KC * EI) + k * EI, EI)],
                                                start=(k == 0), stop=(k == KC - 1))
                    last.then_inc(u_done, 1)
                if has(j + 1 if known(j) else j):
                    pe.wait_ge(a_ready, j + 2)
                    wait(pe, aT_ready, j)
                    for k in range(EC):
                        last = nc.tensor.transpose(tab[(s + 1) % 2][:, k * P:(k + 1) * P], a[:, (s + 1) % 2, k * P:(k + 1) * P], K.ident[:, :])
                    last.then_inc(ta_done, 1)
                if has(j):
                    e = expert(j)
                    pe.wait_ge(aT_ready, j + 1)
                    wait(pe, y_ready, j - 1)
                    for k in range(EC):
                        last = nc.tensor.matmul(db[s % 2][:, :], aT[:, s % 2, k, :], K.wd[:, bass.ds(e * (EC * D) + k * D, D)],
                                                start=(k == 0), stop=(k == EC - 1))
                    last.then_inc(d_done, 1)

            rounds(pe, round_)


def combine_phase(nc, K):
    f32, u32 = mybir.dt.float32, mybir.dt.uint32
    ALU = mybir.AluOpType
    ctx = ExitStack()
    with ctx:
        sb = lambda n, s, d=f32: ctx.enter_context(nc.sbuf_tensor(n, s, d))
        sem = lambda n: ctx.enter_context(nc.semaphore(n))
        gb = sb("gb_f", [P, 2, D])
        base = sb("base_f", [P, 2, TPC, D])
        g = sb("g_f", [P, 2, TPC, 2, D])
        z = sb("z_f", [P, 2, TPC, D])
        idx = sb("idx_f", [P, 2, 2, TPC], u32)
        w = sb("w_f", [P, 2, 2, TPC])
        gb_in = [sem(f"gb_in{i}") for i in range(2)]
        base_in = [sem(f"base_in{i}") for i in range(2)]
        g_in = [[sem(f"g_in{i}_{j}") for j in range(TPC)] for i in range(2)]
        out_sent = [sem(f"out_sent{i}") for i in range(2)]
        idx_ready, first_done, both_done, gated, z_ready = (sem(n) for n in ("idx_ready", "first_done", "both_done", "gated", "z_ready"))
        block = ctx.enter_context(nc.Block())

        @block.sync
        def _(sp):
            def load(c, par, b, done):
                if done is not None:
                    sp.wait_ge(z_ready, done)
                sp.dma_start(gb[:, par, :], K.modd[bass.ds(b, 1), GB, :].broadcast_to([P, D])).then_inc(gb_in[par], 16)
                sp.dma_start(base[:, par, :, :], K.part[bass.ds(c * CH, CH), :].rearrange("(j p) d -> p j d", p=P)).then_inc(base_in[par], 16)

            def store(c, par):
                for j in range(TPC):
                    sp.wait_ge(z_ready, c * TPC + j + 1)
                    sp.dma_start(K.out[bass.ds(c * CH + j * P, P), :], z[:, par, j, :]).then_inc(out_sent[par], 16)

            load(0, 0, 0, None)
            load(1, 1, 0, None)
            with sp.Fori(0, NB - 1) as b:
                for par in range(2):
                    store(2 * b + par, par)
                    load(2 * b + par + 2, par, b + 1, (2 * b + par + 1) * TPC)
            for par in range(2):
                store(NCH - 2 + par, par)
            for par in range(2):
                sp.wait_ge(out_sent[par], NCH // 2 * TPC * 16)

        @block.gpsimd
        def _(pool):
            with pool.Fori(0, NB) as b:
                for par in range(2):
                    pool.wait_ge(idx_ready, 2 * b + par + 1)
                    apart(pool)
                    for j in range(TPC):
                        for c in range(2):
                            nc.gpsimd.indirect_dma_start(out=g[:, par, j, c, :], out_offset=None, in_=K.ys,
                                                         in_offset=bass.IndirectOffsetOnAxis(ap=idx[:, par, c, j:j + 1], axis=0))\
                                .then_inc(g_in[par][j], 16)

        @block.vector
        def _(dve):
            def indices(c, par):
                nc.vector.tensor_copy(w[:, par, :, :], K.wts[:, :, bass.ds(c * TPC, TPC)])
                nc.vector.tensor_copy(idx[:, par, :, :], K.rows[:, :, bass.ds(c * TPC, TPC)]).then_inc(idx_ready, 1)

            def chunk(b, par):
                c = 2 * b + par
                dve.wait_ge(gb_in[par], b * 16 + 16)
                dve.wait_ge(base_in[par], b * 16 + 16)
                dve.wait_ge(out_sent[par], b * (TPC * 16))
                for j in range(TPC):
                    n = c * TPC + j
                    dve.wait_ge(g_in[par][j], b * 32 + 32)
                    zj = z[:, par, j, :]
                    nc.vector.tensor_scalar(zj, g[:, par, j, 0, :], w[:, par, 0, j:j + 1], None, ALU.mult).then_inc(first_done, 1)
                    dve.wait_ge(first_done, n + 1)
                    nc.vector.scalar_tensor_tensor(zj, g[:, par, j, 1, :], w[:, par, 1, j:j + 1], zj, ALU.mult, ALU.add).then_inc(both_done, 1)
                    dve.wait_ge(both_done, n + 1)
                    nc.vector.tensor_tensor(zj, zj, gb[:, par, :], ALU.mult).then_inc(gated, 1)
                    dve.wait_ge(gated, n + 1)
                    nc.vector.tensor_tensor(zj, zj, base[:, par, j, :], ALU.add).then_inc(z_ready, 1)

            indices(0, 0)
            with dve.Fori(0, NB - 1) as b:
                indices(2 * b + 1, 1)
                chunk(b, 0)
                indices(2 * b + 2, 0)
                chunk(b, 1)
            indices(NCH - 1, 1)
            chunk(NB - 1, 0)
            chunk(NB - 1, 1)


def program_e(nc, K, ctx):
    f32, i32 = mybir.dt.float32, mybir.dt.int32
    with ExitStack() as a:
        sb = lambda n, s, d=f32: a.enter_context(nc.sbuf_tensor(n, s, d))
        K.wu = sb("wu_e", [P, E * KC * EI])
        K.wd = sb("wd_e", [P, E * EC * D])
        K.eid = sb("eid", [P, NET], i32)
        K.xrow = sb("xrow", [P, NET], i32)
        expert_setup(nc, K)
        expert_phase(nc, K)
    combine_phase(nc, K)


def block_kernel(nc, x, Wqkv, bqkv, Wo, bo, rw, eb, wup, wdn, sup, sdn, c, wmod, out):
    f32, u32 = mybir.dt.float32, mybir.dt.uint32
    K = Kept()
    K.x = x.rearrange("b s d -> (b s) d")
    K.out = out.rearrange("b s d -> (b s) d")
    K.Wqkv, K.bqkv, K.Wo, K.bo, K.rw, K.eb, K.wup, K.wdn, K.sup, K.sdn, K.c, K.wmod = (
        Wqkv, bqkv, Wo, bo, rw, eb, wup, wdn, sup, sdn, c, wmod)
    K.modd = nc.dram_tensor("modd", [NB, 7, D], f32, kind="Internal").ap()
    K.x1d = nc.dram_tensor("x1d", [T, D], f32, kind="Internal").ap()
    K.part = nc.dram_tensor("part", [T, D], f32, kind="Internal").ap()
    K.xs = nc.dram_tensor("xs", [ROWS, D], f32, kind="Internal").ap()
    K.ys = nc.dram_tensor("ys", [NET * P, D], f32, kind="Internal").ap()
    with ExitStack() as ctx:
        K.count = ctx.enter_context(nc.sbuf_tensor("count", [P, E], f32))
        K.wts = ctx.enter_context(nc.sbuf_tensor("wts", [P, 2, NTILE], f32))
        K.slots = ctx.enter_context(nc.sbuf_tensor("slots", [P, 2, NTILE], f32))
        K.choice = ctx.enter_context(nc.sbuf_tensor("choice", [P, 2, NTILE], f32))
        K.rows = ctx.enter_context(nc.sbuf_tensor("rows", [P, 2, NTILE], u32))
        program_a(nc, K, ctx)
        program_c(nc, K, ctx)
        program_e(nc, K, ctx)


_INS = ['L0_attn_x', 'L0_attn_Wqkv', 'L0_attn_bqkv', 'L0_attn_Wo', 'L0_attn_bo', 'L0_ffn_router_weight', 'L0_ffn_e_bias',
        'L0_ffn_w_up', 'L0_ffn_w_down', 'L0_ffn_shared_up', 'L0_ffn_shared_down', 'L0_c', 'L0_wmod']
_OUTS = [((4, 1024, 512), 'float32')]


def kernel(**inputs):
    import numpy as _np
    import concourse.bacc as _bacc
    from concourse import mybir as _mybir
    from concourse.bass_utils import run_bass_kernel_spmd as _run

    nc = _bacc.Bacc("TRN2", target_bir_lowering=False, num_devices=1)
    arrays, args = {}, []
    for name in _INS:
        a = _np.ascontiguousarray(inputs[name])
        arrays[f"in_{name}_dram"] = a
        args.append(nc.dram_tensor(f"in_{name}_dram", a.shape, _mybir.dt.from_np(a.dtype), kind="ExternalInput").ap())
    for i, (shape, dtype) in enumerate(_OUTS):
        dt = _mybir.dt.from_np(_np.dtype(dtype))
        args.append(nc.dram_tensor(f"out_{i}_dram", shape, dt, kind="ExternalOutput").ap())
    block_kernel(nc, *args)
    r = _run(nc, [arrays], core_ids=[0])
    got = tuple(r.results[0][f"out_{i}_dram"] for i in range(len(_OUTS)))
    return got[0]
```

```python
import concourse.bass as bass
from concourse import mybir
from contextlib import ExitStack

P = 128
D = 512
KC = D // P
H, DH = 16, 32
NB, S = 4, 1024
T = NB * S
NT = S // P
SCALE = float(DH) ** -0.5
MASKED = -10000.0 / SCALE
NEG = -1e30
EPS = 1e-5
SA, CA1, GA, SB, CB1, GB, GABO = range(7)


def setup_phase(nc, K):
    f32, f32r, bf16 = mybir.dt.float32, mybir.dt.float32r, mybir.dt.bfloat16
    ALU, ACT = mybir.AluOpType, mybir.ActivationFunctionType
    ctx = ExitStack()
    with ctx:
        sb = lambda n, s, d=f32: ctx.enter_context(nc.sbuf_tensor(n, s, d))
        sem = lambda n: ctx.enter_context(nc.semaphore(n))
        wraw = sb("wraw", [P, KC, 3 * D])
        wmod = sb("wmod_sb", [P, KC, 6 * D])
        cT = sb("cT", [P, KC, NB])
        sig = sb("sig", [P, KC, NB])
        silu = sb("silu", [P, KC, NB])
        bv4 = sb("bv4", [P, KC, NB])
        bo4 = sb("bo4", [NB, D])
        modr = sb("modr", [NB, 7, D])
        sgn = sb("sgn", [NB, 2, D])
        mag = sb("mag", [NB, 2, D])
        pm = [ctx.enter_context(nc.psum_tensor(f"pmod{i}", [P, 512], f32)) for i in range(7)]
        small_in, w_in, wmod_in = sem("small_in"), sem("w_in"), sem("wmod_in")
        sig_done, silu_done, mod_mm, bo_mm = sem("sig_done"), sem("silu_done"), sem("mod_mm"), sem("bo_mm")
        hi_done, step, mod_stored, zeroed, consts = sem("w_hi_done"), sem("setup_step"), sem("mod_stored"), sem("c_zeroed"), sem("consts")
        bv_done, mag_done = sem("bv_done"), sem("mag_done")
        block = ctx.enter_context(nc.Block())

        @block.sync
        def _(sp):
            with nc.allow_non_contiguous_dma(reason="small vectors by partition"):
                for k in range(KC):
                    sp.dma_start(cT[:, k, :], K.c[:, k * P:(k + 1) * P].rearrange("b p -> p b")).then_inc(small_in, 16)
                sp.dma_start(K.bias[:, :], K.bqkv.rearrange("(g p) -> p g", p=P)).then_inc(small_in, 16)
            sp.dma_start(bo4[:, :], K.bo.rearrange("(a n) -> a n", a=1).broadcast_to([NB, D])).then_inc(small_in, 16)
            sp.dma_start(wmod[:, :, :], K.wmod.rearrange("(k p) n -> p k n", p=P)).then_inc(wmod_in, 16)
            sp.dma_start(K.wo[:, :, :], K.Wo.rearrange("(k p) n -> p k n", p=P)).then_inc(w_in, 16)
            sp.dma_start(wraw[:, :, :], K.Wqkv.rearrange("(k p) n -> p k n", p=P)).then_inc(w_in, 16)
            sp.wait_ge(step, 9)
            sp.dma_start(K.modd, modr[:, :, :]).then_inc(mod_stored, 16)
            sp.wait_ge(mod_stored, 16)

        @block.gpsimd
        def _(pool):
            nc.gpsimd.memset(K.expo[:, :], -0.5).then_inc(zeroed, 1)
            nc.gpsimd.memset(K.ident[:, :], 0.0).then_inc(zeroed, 1)
            nc.gpsimd.memset(K.identb[:, :], 0.0).then_inc(zeroed, 1)
            nc.gpsimd.memset(K.mask_qk[:, :], 0.0).then_inc(zeroed, 1)
            nc.gpsimd.memset(K.mask_kq[:, :], 0.0).then_inc(zeroed, 1)
            nc.gpsimd.memset(K.V[:, NT * D:NT * D + DH], 1.0).then_inc(zeroed, 1)
            nc.gpsimd.memset(K.S[:, :, :], 0.0).then_inc(zeroed, 1)
            nc.gpsimd.memset(K.ones_row[:, :], 1.0).then_inc(zeroed, 1)
            pool.wait_ge(zeroed, 8)
            for m in (K.ident, K.identb):
                nc.gpsimd.affine_select(out=m[:, :], in_=m[:, :], compare_op=ALU.not_equal, fill=1.0, base=0,
                                        pattern=[[-1, P]], channel_multiplier=1).then_inc(consts, 1)
            nc.gpsimd.affine_select(out=K.mask_qk[:, :], in_=K.mask_qk[:, :], compare_op=ALU.is_ge, fill=NEG, base=0,
                                    pattern=[[-1, P]], channel_multiplier=1).then_inc(consts, 1)
            nc.gpsimd.affine_select(out=K.mask_kq[:, :], in_=K.mask_kq[:, :], compare_op=ALU.is_ge, fill=NEG, base=0,
                                    pattern=[[1, P]], channel_multiplier=-1).then_inc(consts, 1)
            for k in range(KC):
                pool.wait_ge(hi_done, k + 1)
                nc.gpsimd.tensor_tensor(K.wlo[:, k, :], wraw[:, k, :], K.whi[:, k, :].bitcast(f32), ALU.subtract).then_inc(consts, 1)
            pool.wait_ge(consts, 4 + KC)

        @block.scalar
        def _(act):
            act.wait_ge(small_in, 96)
            nc.scalar.activation(sig[:, :, :], cT[:, :, :], ACT.Sigmoid).then_inc(sig_done, 1)
            act.wait_ge(mod_mm, 6)
            for i, src in ((0, 2), (1, 5)):
                nc.scalar.activation(mag[:, i, :], pm[src][0:NB, :], ACT.Abs, scale=2.0).then_inc(mag_done, 1)
            act.wait_ge(w_in, 32)
            for k in range(KC):
                nc.scalar.activation(K.whi[:, k, :], wraw[:, k, :], ACT.Copy).then_inc(hi_done, 1)

        @block.vector
        def _(dve):
            dve.wait_ge(zeroed, 8)
            for s in range(2):
                for e in range(2):
                    for n in range(4):
                        nc.vector.tensor_copy(K.stk[96:128, s, 1, e, n * (S // 4):(n + 1) * (S // 4)], K.ones_row[96:128, :])
            dve.wait_ge(sig_done, 1)
            nc.vector.tensor_tensor(silu[:, :, :], cT[:, :, :], sig[:, :, :], ALU.mult).then_inc(silu_done, 1)
            for i in range(NB):
                last = nc.vector.tensor_copy(bv4[:, :, i], K.bias[:, 2 * KC:3 * KC])
            last.then_inc(bv_done, 1)
            dve.wait_ge(mod_mm, 6)
            for kind, src, add in ((SA, 0, 0.0), (CA1, 1, 1.0), (SB, 3, 0.0), (CB1, 4, 1.0)):
                nc.vector.tensor_scalar(modr[:, kind, :], pm[src][0:NB, :], add, None, ALU.add).then_inc(step, 1)
            for i, src in ((0, 2), (1, 5)):
                dve.wait_ge(mag_done, i + 1)
                nc.vector.tensor_scalar(sgn[:, i, :], pm[src][0:NB, :], 0.0, 0.5, ALU.is_ge, ALU.subtract).then_inc(step, 1)
            dve.wait_ge(step, 6)
            for i, kind in ((0, GA), (1, GB)):
                nc.vector.scalar_tensor_tensor(modr[:, kind, :], mag[:, i, :], 0.5, sgn[:, i, :], ALU.max, ALU.mult)\
                    .then_inc(step, 1)
            dve.wait_ge(bo_mm, 1)
            nc.vector.tensor_tensor(bo4[:, :], pm[6][0:NB, :], bo4[:, :], ALU.add).then_inc(bo_mm, 1)
            dve.wait_ge(bo_mm, 2)
            dve.wait_ge(step, 8)
            nc.vector.tensor_tensor(modr[:, GABO, :], modr[:, GA, :], bo4[:, :], ALU.mult).then_inc(step, 1)

        @block.tensor
        def _(pe):
            pe.wait_ge(silu_done, 1)
            pe.wait_ge(wmod_in, 16)
            for n in range(6):
                for k in range(KC):
                    last = nc.tensor.matmul(pm[n][0:NB, :], silu[:, k, :], wmod[:, k, n * D:(n + 1) * D],
                                            start=(k == 0), stop=(k == KC - 1))
                last.then_inc(mod_mm, 1)
            pe.wait_ge(bv_done, 1)
            pe.wait_ge(w_in, 32)
            for k in range(KC):
                last = nc.tensor.matmul(pm[6][0:NB, :], bv4[:, k, :], K.wo[:, k, :], start=(k == 0), stop=(k == KC - 1))
            last.then_inc(bo_mm, 1)


M_FROM, M_RATE = 4, 3


def attention_phase(nc, K):
    f32, f32r, bf16 = mybir.dt.float32, mybir.dt.float32r, mybir.dt.bfloat16
    ALU, ACT, AX = mybir.AluOpType, mybir.ActivationFunctionType, mybir.AxisListType
    NPAIR = H // 2
    NHG = H // 4
    CH = 512
    CHUNKS = (1, 0)
    STEPS = [(c, i) for c in CHUNKS for i in range(4 * c + 4)]
    TURN = 4 * CHUNKS[0] + 4
    NST = len(STEPS)
    MUSES = []
    for qt in range(NT):
        first = min((qt + 1) * P, CH)
        rest = (qt + 1) * P - first
        for n, k0, part in ((first, 0, 0), (rest, CH, 1)):
            if not n:
                continue
            if 2 * n <= CH:
                MUSES.append(((0, 1), qt, k0, n, part))
            else:
                MUSES += [((e,), qt, k0, n, part) for e in range(2)]
    NM = len(MUSES)
    M_DUE = [min(NM, max(0, M_RATE * (s - M_FROM + 1))) for s in range(NST + 1)]
    M_DUE[NST] = NM
    ring = []
    for j in range(NT):
        ring.append("hT")
        if j >= 1:
            ring.append("v")
    ring.append("v")
    ring += ["p"] * 4 + ["m"] * NM + ["mt"] * 2
    for p in range(NPAIR):
        if p + 1 < NPAIR:
            ring += ["m"] * NM
            if p % 2 == 0 and p + 2 < NPAIR:
                ring += ["p"] * 4
            ring += ["mt"] * 2
    ring += ["w"] * NT
    TOTAL = {k: ring.count(k) for k in set(ring)}
    assert len(ring) % 3 == 0, len(ring)

    ctx = ExitStack()
    with ctx:
        sb = lambda n, s, d=f32: ctx.enter_context(nc.sbuf_tensor(n, s, d))
        sem = lambda n: ctx.enter_context(nc.semaphore(n))
        mod_t = sb("mod_t", [P, 2, KC])
        ga_bc = sb("ga_bc", [P, D])
        gabo_bc = sb("gabo_bc", [P, D])
        xa = sb("xa", [P, 2, D])
        stats = sb("stats", [P, 2, 6])
        mv = sb("mv", [P, 2, 2])
        rstd = sb("rstd", [P, 2, 2])
        h = sb("h", [P, 2, KC, P])
        hhi = sb("hhi", [P, KC, S], f32r)
        hlo = sb("hlo", [P, KC, S], f32r)
        st = sb("st", [P, 4, S], f32r)
        V, S_t = K.V, K.S
        mx = sb("mx", [P, 2, NT, 2])
        negm = sb("negm", [P, NT, 2])
        mhi = sb("mhi", [P, NT, 2], f32r)
        pr = sb("pr", [P, 3, 2, CH])
        oV = sb("oV", [P, 2, CH])
        oD = sb("oD", [P, 2, CH])
        oT = sb("oT", [P, KC, S])
        xr = xa
        u = h[:, :, :, :].rearrange("p a k t -> p a (k t)")
        pb = lambda n, s: ctx.enter_context(nc.psum_tensor(n, s, f32))
        rb = [pb(f"ring{i}", [P, 512]) for i in range(3)]
        sc = [pb(f"sc{i}", [P, 2, 512]) for i in range(2)]
        O = pb("O", [P, 512])

        mod_in, mod2_in = sem("mod_in"), sem("mod2_in")
        xa_in = [sem(f"xa_in{i}") for i in range(2)]
        xr_in = [sem(f"xr_in{i}") for i in range(2)]
        x1_out = [sem(f"x1_out{i}") for i in range(2)]
        stk_in = [sem(f"stk_in{i}") for i in range(2)]
        bn, mv_ready, rstd_ready, xn_ready = sem("bn"), sem("mv_ready"), sem("rstd_ready"), sem("xn_ready")
        var_eps = sem("var_eps")
        t_done, h_ready, hhi_ready, hlo_ready = sem("t_done"), sem("h_ready"), sem("hhi_ready"), sem("hlo_ready")
        v_done, v_ready = sem("v_done"), sem("v_ready")
        p_done, p_hi, p_lo = sem("p_done"), sem("p_hi"), sem("p_lo")
        m_done, m_red, mstep, s_ready = sem("m_done"), sem("m_red"), sem("mstep"), sem("s_ready")
        mt_done, mt_ready = sem("mt_done"), sem("mt_ready")
        sc_done, exp_done, pv_done = sem("sc_done"), sem("exp_done"), sem("pv_done")
        o_copied, o_rec, o_norm = sem("o_copied"), sem("o_rec"), sem("o_norm")
        w_done, u_ready, xg_ready, x1_ready = sem("w_done"), sem("u_ready"), sem("xg_ready"), sem("x1_ready")
        freed = {"hT": h_ready, "v": v_ready, "p": p_lo, "m": m_red, "mt": mt_ready, "w": u_ready}
        positions = {}
        for at, kind in enumerate(ring):
            positions.setdefault(kind, []).append(at)

        def ring_at(kind, n):
            return positions[kind][n]

        block = ctx.enter_context(nc.Block())

        @block.sync
        def _(sp):
            with sp.Fori(0, NB) as b:
                sp.wait_ge(h_ready, b * NT)
                with nc.allow_non_contiguous_dma(reason="512 numbers by partition"):
                    for i, kind in ((0, SA), (1, CA1)):
                        for k in range(KC):
                            sp.dma_start(mod_t[:, i, k:k + 1], K.modd[bass.ds(b, 1), kind, k * P:(k + 1) * P].rearrange("a p -> p a"))\
                                .then_inc(mod_in, 16)
                sp.wait_ge(u_ready, b * NT)
                sp.dma_start(ga_bc[:, :], K.modd[bass.ds(b, 1), GA, :].broadcast_to([P, D])).then_inc(mod2_in, 16)
                sp.wait_ge(x1_ready, b * NT)
                sp.dma_start(gabo_bc[:, :], K.modd[bass.ds(b, 1), GABO, :].broadcast_to([P, D])).then_inc(mod2_in, 16)
                for j in range(NT):
                    if j >= 2:
                        sp.wait_ge(t_done, b * NT + j - 1)
                    else:
                        sp.wait_ge(x1_ready, b * NT)
                    sp.dma_start(xa[:, j % 2, :], K.x[bass.ds(b * S + j * P, P), :]).then_inc(xa_in[j % 2], 16)
                for p in range(NPAIR):
                    if p >= 2:
                        sp.wait_ge(pv_done, b * (NPAIR * NST) + NST * (p - 1))
                        apart(sp)
                    sp.wait_ge(p_lo, b * 16 + 4 * (p // 2) + 4)
                    for e in range(2):
                        r = 2 * (p % 2) + e
                        rows = slice(DH * r, DH * r + DH)
                        for n, parts in enumerate((slice(0, 3, 2), slice(1, 3), slice(0, 4, 3))):
                            sp.dma_start(K.stk[DH * n:DH * n + DH, p % 2, :, e, :].bitcast(f32), st[rows, parts, :].bitcast(f32))\
                                .then_inc(stk_in[p % 2], 16)
                for j in range(NT):
                    if j < 2:
                        sp.wait_ge(t_done, b * NT + NT)
                    else:
                        sp.wait_ge(x1_ready, b * NT + j - 1)
                    sp.dma_start(xr[:, j % 2, :], K.x[bass.ds(b * S + j * P, P), :]).then_inc(xr_in[j % 2], 16)
                    if j >= 1:
                        sp.wait_ge(x1_ready, b * NT + j)
                        sp.dma_start(K.x1d[bass.ds(b * S + (j - 1) * P, P), :], u[:, (j - 1) % 2, :]).then_inc(x1_out[(j - 1) % 2], 16)
                sp.wait_ge(x1_ready, b * NT + NT)
                sp.dma_start(K.x1d[bass.ds(b * S + (NT - 1) * P, P), :], u[:, (NT - 1) % 2, :]).then_inc(x1_out[(NT - 1) % 2], 16)
            for i in range(2):
                sp.wait_ge(x1_out[i], NB * NT // 2 * 16)

        @block.gpsimd
        def _(pool):
            def split_low(b, j):
                pool.wait_ge(h_ready, b * NT + j + 1)
                pool.wait_ge(hhi_ready, b * NT + j + 1)
                nc.gpsimd.tensor_tensor(hlo[:, :, j * P:(j + 1) * P], h[:, j % 2, :, :],
                                        hhi[:, :, j * P:(j + 1) * P].bitcast(f32), ALU.subtract).then_inc(hlo_ready, 1)

            with pool.Fori(0, NB) as b:
                for j in range(NT):
                    pool.wait_ge(mv_ready, b * NT + j + 1)
                    apart(pool)
                    nc.gpsimd.tensor_scalar(rstd[:, j % 2, 0:1], mv[:, j % 2, 1:2], EPS, None, ALU.add).then_inc(var_eps, 1)
                    pool.wait_ge(var_eps, b * NT + j + 1)
                    nc.gpsimd.tensor_tensor(rstd[:, j % 2, 1:2], rstd[:, j % 2, 0:1], K.expo[:, 0:1], ALU.pow).then_inc(rstd_ready, 1)
                    if j >= 2:
                        split_low(b, j - 2)
                split_low(b, NT - 2)
                split_low(b, NT - 1)
                for n in range(2 * NHG):
                    hg, c = n // 2, CHUNKS[n % 2]
                    pool.wait_ge(o_rec, b * 8 + n + 1)
                    nc.gpsimd.tensor_tensor(oT[:, hg, c * CH:(c + 1) * CH], oV[:, c, :], oD[:, c, :], ALU.mult).then_inc(o_norm, 1)
                pool.wait_ge(mod2_in, b * 32 + 32)
                for j in range(NT):
                    pool.wait_ge(xr_in[j % 2], b * (NT // 2 * 16) + (j // 2 + 1) * 16)
                    nc.gpsimd.tensor_tensor(xr[:, j % 2, :], xr[:, j % 2, :], gabo_bc[:, :], ALU.add).then_inc(xg_ready, 1)
                    pool.wait_ge(xg_ready, b * NT + j + 1)
                    pool.wait_ge(u_ready, b * NT + j + 1)
                    nc.gpsimd.tensor_tensor(u[:, j % 2, :], u[:, j % 2, :], xr[:, j % 2, :], ALU.add).then_inc(x1_ready, 1)

        @block.scalar
        def _(act):
            def p_evac(b, hg):
                for n in range(4):
                    which, c = n // 2, n % 2
                    if n == 0 and hg >= 1:
                        for s in range(2):
                            act.wait_ge(stk_in[s], b * 4 * 96 + hg * 96)
                    elif n == 0:
                        for s in range(2):
                            act.wait_ge(stk_in[s], b * 4 * 96)
                    u_ = ring_at("p", 4 * hg + n)
                    act.wait_ge(p_done, b * 16 + 4 * hg + n + 1)
                    nc.scalar.activation(st[:, 2 * which, c * CH:(c + 1) * CH], rb[u_ % 3][:, :], ACT.Identity,
                                         bias=K.bias[:, which * KC + hg:which * KC + hg + 1]).then_inc(p_hi, 1)

            def mt_evac(b, p):
                if p >= 2:
                    act.wait_ge(pv_done, b * NPAIR * NST + NST * (p - 1))
                for z, c in enumerate(CHUNKS):
                    act.wait_ge(mt_done, b * 16 + 2 * p + z + 1)
                    bank = rb[ring_at("mt", 2 * p + z) % 3]
                    for e in range(2):
                        last = nc.scalar.activation(K.stk[96:128, p % 2, 0, e, c * CH:(c + 1) * CH], bank[32 * e:32 * e + 32, :], ACT.Copy)
                    last.then_inc(mt_ready, 1)

            def exp(b, p, s):
                c, i = STEPS[s]
                off = max(0, i * P - c * CH)
                g = p * NST + s
                act.wait_ge(sc_done, b * NPAIR * NST + g + 1)
                if g >= 3:
                    act.wait_ge(pv_done, b * NPAIR * NST + g - 2)
                nc.scalar.activation(pr[:, g % 3, :, off:], sc[g % 2][:, :, off:], ACT.Exp, scale=SCALE).then_inc(exp_done, 1)

            def o_copy(b, n):
                act.wait_ge(pv_done, b * NPAIR * NST + (n // 2) * NST + (TURN, NST)[n % 2])
                p, c = n // 2, CHUNKS[n % 2]
                if p % 2 == 0 and p >= 2:
                    act.wait_ge(o_norm, b * 8 + p - 2 + n % 2 + 1)
                elif p == 0:
                    act.wait_ge(o_norm, b * 8)
                z = 64 * (p % 2)
                nc.scalar.activation(oV[z:z + 64, c, :], O[z:z + 64, :], ACT.Copy)
                nc.scalar.activation(oD[z:z + 64, c, :], O[64 - z:128 - z, :], ACT.Copy).then_inc(o_copied, 1)

            with act.Fori(0, NB) as b:
                act.wait_ge(mod_in, b * 128 + 128)
                for j in range(NT + 1):
                    if j < NT:
                        act.wait_ge(t_done, b * NT + j + 1)
                        if j >= 2:
                            act.wait_ge(hlo_ready, b * NT + j - 1)
                        else:
                            act.wait_ge(x1_out[j % 2], b * (NT // 2 * 16))
                        bank = rb[ring_at("hT", j) % 3]
                        for k in range(KC):
                            last = nc.scalar.activation(h[:, j % 2, k, :], bank[:, k * P:(k + 1) * P], ACT.Identity,
                                                        scale=mod_t[:, 1, k:k + 1], bias=mod_t[:, 0, k:k + 1])
                        last.then_inc(h_ready, 1)
                    if j >= 1:
                        act.wait_ge(v_done, b * NT + j)
                        nc.scalar.activation(V[:, (j - 1) * D:j * D], rb[ring_at("v", j - 1) % 3][:, :], ACT.Copy).then_inc(v_ready, 1)
                p_evac(b, 0)
                mt_evac(b, 0)
                for p in range(NPAIR):
                    for s in range(NST):
                        exp(b, p, s)
                        if s == TURN:
                            o_copy(b, 2 * p)
                    o_copy(b, 2 * p + 1)
                    if p % 2 == 0 and p + 2 < NPAIR:
                        p_evac(b, (p + 2) // 2)
                    if p + 1 < NPAIR:
                        mt_evac(b, p + 1)

        @block.vector
        def _(dve):

            def ln_stats(b, j):
                dve.wait_ge(xa_in[j % 2], b * (NT // 2 * 16) + (j // 2 + 1) * 16)
                nc.vector.bn_stats(stats[:, j % 2, :], xa[:, j % 2, :]).then_inc(bn, 1)
                if j >= 2:
                    dve.wait_ge(rstd_ready, b * NT + j - 1)
                dve.wait_ge(bn, b * NT + j + 1)
                apart(dve)
                nc.vector.bn_aggr(mv[:, j % 2, :], stats[:, j % 2, :]).then_inc(mv_ready, 1)

            def ln_norm(b, j):
                dve.wait_ge(rstd_ready, b * NT + j + 1)
                nc.vector.tensor_scalar(xa[:, j % 2, :], xa[:, j % 2, :], mv[:, j % 2, 0:1], rstd[:, j % 2, 1:2],
                                        ALU.subtract, ALU.mult).then_inc(xn_ready, 1)

            def split_high(b, j):
                dve.wait_ge(h_ready, b * NT + j + 1)
                nc.vector.tensor_copy(hhi[:, :, j * P:(j + 1) * P], h[:, j % 2, :, :]).then_inc(hhi_ready, 1)

            def p_low(b, hg):
                for n in range(4):
                    which, c = n // 2, n % 2
                    bank = rb[ring_at("p", 4 * hg + n) % 3]
                    dve.wait_ge(p_hi, b * 16 + 4 * hg + n + 1)
                    nc.vector.scalar_tensor_tensor(st[:, 2 * which + 1, c * CH:(c + 1) * CH], bank[:, :],
                                                   K.bias[:, which * KC + hg:which * KC + hg + 1],
                                                   st[:, 2 * which, c * CH:(c + 1) * CH].bitcast(f32),
                                                   ALU.add, ALU.subtract).then_inc(p_lo, 1)

            def m_reduce(b, p, n):
                heads, qt, k0, w, part = MUSES[n]
                bank = rb[ring_at("m", NM * p + n) % 3]
                dve.wait_ge(m_done, b * NPAIR * NM + p * NM + n + 1)
                nc.vector.tensor_reduce(mx[:, heads[0]:heads[-1] + 1, qt, part],
                                        bank[:, 0:len(heads) * w].rearrange("p (e k) -> p e k", e=len(heads)),
                                        AX.X, ALU.max).then_inc(m_red, 1)

            def m_rows(b, p):
                base = b * NPAIR * 3 + p * 3
                dve.wait_ge(m_red, b * NPAIR * NM + (p + 1) * NM)
                nc.vector.tensor_tensor(mx[:, :, 4:NT, 0], mx[:, :, 4:NT, 0], mx[:, :, 4:NT, 1], ALU.max).then_inc(mstep, 1)
                dve.wait_ge(mstep, base + 1)
                nc.vector.tensor_scalar(negm[:, :, :], mx[:, :, :, 0].rearrange("p e t -> p t e"), MASKED, -1.0, ALU.max, ALU.mult)\
                    .then_inc(mstep, 1)
                dve.wait_ge(mstep, base + 2)
                nc.vector.tensor_copy(mhi[:, :, :], negm[:, :, :]).then_inc(mstep, 1)
                dve.wait_ge(mstep, base + 3)
                dve.wait_ge(mt_done, b * 16 + 2 * p)
                nc.vector.tensor_copy(S_t[:, :, 0::32], mhi[:, :, :].bitcast(f32))
                nc.vector.tensor_tensor(S_t[:, :, 1::32], negm[:, :, :], mhi[:, :, :].bitcast(f32), ALU.subtract).then_inc(s_ready, 1)

            def o_recip(b, n):
                hg, c = n // 2, CHUNKS[n % 2]
                dve.wait_ge(o_copied, b * 16 + 4 * hg + 3 + n % 2)
                nc.vector.reciprocal(oD[:, c, :], oD[:, c, :]).then_inc(o_rec, 1)

            with dve.Fori(0, NB) as b:
                ln_stats(b, 0)
                for j in range(NT):
                    if j + 1 < NT:
                        ln_stats(b, j + 1)
                    ln_norm(b, j)
                    if j >= 1:
                        split_high(b, j - 1)
                split_high(b, NT - 1)
                p_low(b, 0)
                for n in range(NM):
                    m_reduce(b, 0, n)
                m_rows(b, 0)
                for p in range(NPAIR):
                    n = 0
                    for s in range(NST + 1):
                        if p + 1 < NPAIR:
                            while n < M_DUE[s]:
                                m_reduce(b, p + 1, n)
                                n += 1
                        if s == TURN + 1 and p % 2:
                            o_recip(b, p - 1)
                    if p + 1 < NPAIR:
                        m_rows(b, p + 1)
                    if p % 2 == 0 and p + 2 < NPAIR:
                        p_low(b, (p + 2) // 2)
                    if p % 2:
                        o_recip(b, p)
                dve.wait_ge(mod2_in, b * 32 + 32)
                for j in range(NT):
                    bank = rb[ring_at("w", j) % 3]
                    dve.wait_ge(w_done, b * NT + j + 1)
                    dve.wait_ge(x1_out[j % 2], b * (NT // 2 * 16) + (j // 2) * 16)
                    nc.vector.tensor_tensor(u[:, j % 2, :], bank[:, :], ga_bc[:, :], ALU.mult).then_inc(u_ready, 1)

        @block.tensor
        def _(pe):

            def bank_for(b, kind, n):
                at = ring_at(kind, n)
                if at < 3:
                    pe.wait_ge(u_ready, b * NT)
                else:
                    before = ring[at - 3]
                    pe.wait_ge(freed[before], b * TOTAL[before] + positions[before].index(at - 3) + 1)
                return rb[at % 3]

            def transposes(b, j):
                bank = bank_for(b, "hT", j)
                pe.wait_ge(xn_ready, b * NT + j + 1)
                for k in range(KC):
                    last = nc.tensor.transpose(bank[:, k * P:(k + 1) * P], xa[:, j % 2, k * P:(k + 1) * P], K.ident[:, :])
                last.then_inc(t_done, 1)

            def values(b, j):
                bank = bank_for(b, "v", j)
                pe.wait_ge(hlo_ready, b * NT + j + 1)
                terms = [(x_, w_, k) for k in range(KC) for x_, w_ in ((hhi, K.whi), (hhi, K.wlo), (hlo, K.whi))]
                for n, (x_, w_, k) in enumerate(terms):
                    last = nc.tensor.matmul(bank[:, :], x_[:, k, j * P:(j + 1) * P], w_[:, k, 2 * D:3 * D],
                                            start=(n == 0), stop=(n == len(terms) - 1))
                last.then_inc(v_done, 1)

            def project(b, hg):
                for n in range(4):
                    which, c = n // 2, n % 2
                    bank = bank_for(b, "p", 4 * hg + n)
                    cols = slice(which * D + hg * P, which * D + (hg + 1) * P)
                    terms = [(w_, x_, k) for k in range(KC) for w_, x_ in ((K.whi, hhi), (K.whi, hlo), (K.wlo, hhi))]
                    for t, (w_, x_, k) in enumerate(terms):
                        last = nc.tensor.matmul(bank[:, :], w_[:, k, cols], x_[:, k, c * CH:(c + 1) * CH],
                                                start=(t == 0), stop=(t == len(terms) - 1))
                    last.then_inc(p_done, 1)

            def m_scores(b, p, n):
                heads, qt, k0, w, part = MUSES[n]
                bank = bank_for(b, "m", NM * p + n)
                diag = k0 <= qt * P < k0 + w
                for x_, e in enumerate(heads):
                    o = bank[:, x_ * w:(x_ + 1) * w]
                    last = nc.tensor.matmul(o, K.stk[0:96, p % 2, 0, e, qt * P:(qt + 1) * P], K.stk[0:96, p % 2, 1, e, k0:k0 + w],
                                            start=True, stop=not diag)
                    if diag:
                        last = nc.tensor.matmul(o[:, qt * P - k0:qt * P - k0 + P], K.identb[:, :], K.mask_qk[:, :],
                                                start=False, stop=True)
                last.then_inc(m_done, 1)

            def m_transpose(b, p):
                for z, c in enumerate(CHUNKS):
                    bank = bank_for(b, "mt", 2 * p + z)
                    pe.wait_ge(s_ready, b * NPAIR + p + 1)
                    apart(pe)
                    for t in range(4):
                        last = nc.tensor.transpose(bank[0:64, t * P:(t + 1) * P], S_t[:, 4 * c + t, :], K.ident[:, :])
                    last.then_inc(mt_done, 1)

            def scores(b, p, s):
                c, i = STEPS[s]
                off = max(0, i * P - c * CH)
                g = p * NST + s
                if g >= 2:
                    pe.wait_ge(exp_done, b * NPAIR * NST + g - 1)
                else:
                    pe.wait_ge(exp_done, b * NPAIR * NST)
                pe.wait_ge(mt_ready, b * 16 + 2 * p + CHUNKS.index(c) + 1)
                diag = i * P >= c * CH
                for e in range(2):
                    last = nc.tensor.matmul(sc[g % 2][:, e, off:], K.stk[:, p % 2, 1, e, i * P:(i + 1) * P],
                                            K.stk[:, p % 2, 0, e, c * CH + off:(c + 1) * CH], start=True, stop=not diag)
                    if diag:
                        last = nc.tensor.matmul(sc[g % 2][:, e, off:off + P], K.identb[:, :], K.mask_kq[:, :], start=False, stop=True)
                last.then_inc(sc_done, 1)

            def weighted(b, p, s):
                c, i = STEPS[s]
                off = max(0, i * P - c * CH)
                g = p * NST + s
                n = 2 * p + CHUNKS.index(c)
                if i == 0:
                    pe.wait_ge(o_copied, b * 16 + n)
                pe.wait_ge(exp_done, b * NPAIR * NST + g + 1)
                for e in range(2):
                    at = i * D + (2 * p + e) * DH
                    for z, col in ((p % 2, at), (1 - p % 2, NT * D)):
                        row = 64 * z + 32 * e
                        last = nc.tensor.matmul(O[row:row + 32, off:], V[:, col:col + DH], pr[:, g % 3, e, off:],
                                                start=(i == 0), stop=(i == 4 * c + 3))
                last.then_inc(pv_done, 1)

            def output(b, j):
                bank = bank_for(b, "w", j)
                pe.wait_ge(o_norm, b * 8 + 8)
                for k in range(KC):
                    last = nc.tensor.matmul(bank[:, :], oT[:, k, j * P:(j + 1) * P], K.wo[:, k, :], start=(k == 0), stop=(k == KC - 1))
                last.then_inc(w_done, 1)

            with pe.Fori(0, NB) as b:
                for j in range(NT):
                    transposes(b, j)
                    if j >= 1:
                        values(b, j - 1)
                values(b, NT - 1)
                project(b, 0)
                pe.wait_ge(stk_in[0], b * 4 * 96 + 96)
                for n in range(NM):
                    m_scores(b, 0, n)
                m_transpose(b, 0)
                for p in range(NPAIR):
                    n = 0
                    for s in range(NST + 1):
                        if s < NST:
                            scores(b, p, s)
                        if p + 1 < NPAIR:
                            if n == 0 and M_DUE[s]:
                                pe.wait_ge(stk_in[(p + 1) % 2], b * 4 * 96 + ((p + 1) // 2 + 1) * 96)
                            while n < M_DUE[s]:
                                m_scores(b, p + 1, n)
                                n += 1
                        if s >= 1:
                            weighted(b, p, s - 1)
                    if p % 2 == 0 and p + 2 < NPAIR:
                        project(b, (p + 2) // 2)
                    if p + 1 < NPAIR:
                        m_transpose(b, p + 1)
                for j in range(NT):
                    output(b, j)


def apart(eng):
    eng.nop(nofuse=True)


class Kept:
    pass


def program_a(nc, K, ctx):
    f32, f32r, bf16 = mybir.dt.float32, mybir.dt.float32r, mybir.dt.bfloat16
    sb = lambda n, s, d=f32: ctx.enter_context(nc.sbuf_tensor(n, s, d))
    K.ident = sb("ident", [P, P])
    K.expo = sb("expo", [P, 4])
    a = ExitStack()
    with a:
        sb = lambda n, s, d=f32: a.enter_context(nc.sbuf_tensor(n, s, d))
        K.whi = sb("whi", [P, KC, 3 * D], f32r)
        K.wlo = sb("wlo", [P, KC, 3 * D], f32r)
        K.wo = sb("wo_sb", [P, KC, D])
        K.bias = sb("bias", [P, 3 * KC])
        K.identb = sb("identb", [P, P], bf16)
        K.mask_qk = sb("mask_qk", [P, P], bf16)
        K.mask_kq = sb("mask_kq", [P, P], bf16)
        K.V = sb("V", [P, NT * D + DH])
        K.S = sb("S", [P, NT, 64])
        K.stk = sb("stk", [P, 2, 2, 2, S], f32r)
        with nc.sbuf_tensor("ones_row", [P, S // 4], f32) as K.ones_row:
            setup_phase(nc, K)
        attention_phase(nc, K)

E = 16
NG, GSZ = 4, 4
F = 1024
FC = F // P
EI = 256
EC = EI // P
CH = 512
TPC = CH // P
NCH = T // CH
T_FROM = FC - TPC
NTILE = T // P
REGION = T + P
NET = (2 * T + E * (P - 1)) // P
DUMMY = E * REGION
ROWS = DUMMY + P


def shared_setup(nc, K):
    f32, f32r, bf16 = mybir.dt.float32, mybir.dt.float32r, mybir.dt.bfloat16
    ALU, ACT = mybir.AluOpType, mybir.ActivationFunctionType
    ctx = ExitStack()
    with ctx:
        sb = lambda n, s, d=f32: ctx.enter_context(nc.sbuf_tensor(n, s, d))
        sem = lambda n: ctx.enter_context(nc.semaphore(n))
        up_raw = sb("up_raw", [P, KC, F])
        dn_raw = sb("dn_raw", [P, FC, D])
        rw_raw = sb("rw_raw", [E, D])
        zero = sb("zero", [P, D])
        pt = ctx.enter_context(nc.psum_tensor("pt_rw", [P, KC, E], f32))
        raw_in, rw_in, hi_done, lo_done, rw_t, rw_hi, rw_lo = (sem(n) for n in
            ("c_raw_in", "rw_in", "c_hi_done", "c_lo_done", "rw_t", "rw_hi", "rw_lo"))
        zeroed, consts, zero_out = sem("c_zeroed2"), sem("c_consts"), sem("zero_out")
        block = ctx.enter_context(nc.Block())

        @block.sync
        def _(sp):
            sp.dma_start(rw_raw[:, :], K.rw).then_inc(rw_in, 16)
            sp.dma_start(K.ebias[:, :], K.eb.rearrange("(a n) -> a n", a=1).broadcast_to([P, E])).then_inc(rw_in, 16)
            for k in range(KC):
                sp.dma_start(up_raw[:, k, :], K.sup[k * P:(k + 1) * P, :]).then_inc(raw_in, 16)
            sp.dma_start(dn_raw[:, :, :], K.sdn.rearrange("(k p) n -> p k n", p=P)).then_inc(raw_in, 16)
            sp.wait_ge(zeroed, 1)
            sp.dma_start(K.xs[DUMMY:DUMMY + P, :], zero[:, :]).then_inc(zero_out, 16)
            sp.wait_ge(zero_out, 16)

        @block.gpsimd
        def _(pool):
            nc.gpsimd.memset(zero[:, :], 0.0).then_inc(zeroed, 1)
            nc.gpsimd.memset(K.tri[:, :], 1.0).then_inc(zeroed, 1)
            nc.gpsimd.memset(K.ones[:, :], 1.0)
            nc.gpsimd.memset(K.expo[:, :], -0.5)
            pool.wait_ge(zeroed, 2)
            nc.gpsimd.affine_select(out=K.tri[:, :], in_=K.tri[:, :], compare_op=ALU.is_gt, fill=0.0, base=0,
                                    pattern=[[1, P]], channel_multiplier=-1).then_inc(consts, 1)
            pool.wait_ge(consts, 1)
            pool.wait_ge(hi_done, 2)
            nc.gpsimd.tensor_tensor(K.dnlo[:, :, :], dn_raw[:, :, :], K.dnhi[:, :, :].bitcast(f32), ALU.subtract).then_inc(lo_done, 1)
            pool.wait_ge(lo_done, 1)

        @block.scalar
        def _(act):
            act.wait_ge(raw_in, 16 * (KC + 1))
            nc.scalar.activation(K.uphi[:, :, :], up_raw[:, :, :], ACT.Copy).then_inc(hi_done, 1)
            nc.scalar.activation(K.dnhi[:, :, :], dn_raw[:, :, :], ACT.Copy).then_inc(hi_done, 1)

        @block.vector
        def _(dve):
            for e in range(E):
                nc.vector.memset(K.order[:, e:e + 1], float(E - e))
                nc.vector.memset(K.region[:, e:e + 1], float(e * REGION))
            for i in range(NG):
                for j in range(NG):
                    nc.vector.memset(K.gtri[:, j, i:i + 1], 1.0 if i < j else 0.0)
            nc.vector.memset(K.count[:, :], 0.0)
            dve.wait_ge(rw_t, 1)
            nc.vector.tensor_copy(K.rwhi[:, :, :], pt[:, :, :]).then_inc(rw_hi, 1)
            dve.wait_ge(rw_hi, 1)
            nc.vector.tensor_tensor(K.rwlo[:, :, :], pt[:, :, :], K.rwhi[:, :, :].bitcast(f32), ALU.subtract)
            dve.wait_ge(hi_done, 1)
            nc.vector.tensor_tensor(K.uplo[:, :, :], up_raw[:, :, :], K.uphi[:, :, :].bitcast(f32), ALU.subtract).then_inc(rw_lo, 1)
            dve.wait_ge(rw_lo, 1)

        @block.tensor
        def _(pe):
            pe.wait_ge(rw_in, 32)
            for k in range(KC):
                last = nc.tensor.transpose(pt[:, k, :], rw_raw[:, k * P:(k + 1) * P], K.ident[0:E, 0:E])
            last.then_inc(rw_t, 1)


def shared_phase(nc, K):
    f32, f32r, bf16, u32 = mybir.dt.float32, mybir.dt.float32r, mybir.dt.bfloat16, mybir.dt.uint32
    ALU, ACT, AX = mybir.AluOpType, mybir.ActivationFunctionType, mybir.AxisListType
    ctx = ExitStack()
    with ctx:
        sb = lambda n, s, d=f32: ctx.enter_context(nc.sbuf_tensor(n, s, d))
        pb = lambda n, s: ctx.enter_context(nc.psum_tensor(n, s, f32))
        sem = lambda n: ctx.enter_context(nc.semaphore(n))
        xb = sb("xb", [P, 2, TPC, D])
        h2 = sb("h2", [P, 2, TPC, D])
        bc = sb("bc", [P, 2, 3, D])
        stats = sb("stats2", [P, TPC, 6])
        mv = sb("mv2", [P, TPC, 2])
        rstd = sb("rstd2", [P, 2, TPC])
        thi = sb("thi", [P, 2, KC, CH], f32r)
        tlo = sb("tlo", [P, 2, KC, CH], f32r)
        relu = sb("relu", [P, 2, CH])
        sq = sb("sq", [P, 2, CH])
        ahi = sb("ahi", [P, FC, CH], f32r)
        alo = sb("alo", [P, FC, CH], f32r)
        y = sb("y_sh", [P, 2, D])
        s_ = sb("s_", [P, TPC, E])
        sbias = sb("sbias", [P, TPC, E])
        g2 = sb("g2", [P, 6, TPC, NG])
        cmp = sb("cmp", [P, 3, TPC, NG, NG])
        rank = sb("rank", [P, TPC, NG])
        m16 = sb("m16", [P, 3, TPC, E])
        top = sb("top", [P, 2, TPC, 1])
        oh = sb("oh", [P, 2, TPC, E])
        chosen = sb("chosen", [P, TPC, E], bf16)
        ws = sb("ws", [P, 4, TPC])
        place = sb("place", [P, TPC, E])
        slotf = sb("slotf", [P, 2, TPC])
        slotu = sb("slotu", [P, 2, 2, TPC], u32)
        tp = [pb(f"tp{i}", [P, KC, P]) for i in range(2)]
        rp = pb("rp", [P, 512])
        pl = pb("pl", [P, 512])
        upb = [pb(f"up{i}", [P, CH]) for i in range(2)]
        dnb = [pb(f"dn{i}", [P, D]) for i in range(2)]

        xb_in = [sem(f"xb_in{i}") for i in range(2)]
        bc_in = [sem(f"bc_in{i}") for i in range(2)]
        bn, mv_ready, var_eps, rstd_ready = sem("bn2"), sem("mv2_ready"), sem("var_eps2"), sem("rstd2_ready")
        h2_scaled, h2_ready = sem("h2_scaled"), sem("h2_ready")
        t_done, thi_ready, tlo_ready = sem("t2_done"), sem("thi_ready"), sem("tlo_ready")
        r_done, s_ready, step = sem("r_done"), sem("sig_ready"), sem("route_step")
        chosen_ready, place_done, slots_ready = sem("chosen_ready"), sem("place_done"), sem("slots_ready")
        sent = [sem(f"sent{i}") for i in range(2)]
        up_done, relu_ready, sq_ready, ahi_ready, alo_ready = (sem(n) for n in
            ("up_done", "relu_ready", "sq_ready", "ahi_ready", "alo_ready"))
        dn_done, y_scaled, y_ready = sem("dn_done"), sem("y_scaled"), sem("y_ready")
        y_out = [sem(f"y_out{i}") for i in range(2)]
        block = ctx.enter_context(nc.Block())

        def rounds(first, loop, chunk):
            first()
            with loop as i:
                chunk(2 * i, 0, i)
                chunk(2 * i + 1, 1, i + 1)
            chunk(NCH - 2, 0, NB - 1)
            chunk(NCH - 1, 1, None)

        @block.sync
        def _(sp):
            def load_tile(r, par, j):
                sp.dma_start(xb[:, par, j, :], K.x1d[bass.ds(r * CH + j * P, P), :]).then_inc(xb_in[par], 16)

            def load_rows(b, par):
                sp.dma_start(bc[:, par, :, :], K.modd[bass.ds(b, 1), SB:GB + 1, :].broadcast_to([P, 3, D])).then_inc(bc_in[par], 16)

            def first():
                for r in range(2):
                    for j in range(TPC):
                        load_tile(r, r, j)
                    load_rows(0, r)

            def chunk(q, par, b):
                more = not isinstance(q, int)
                for j in range(TPC):
                    sp.wait_ge(y_ready, q * TPC + j + 1)
                    sp.dma_start(K.part[bass.ds(q * CH + j * P, P), :], y[:, j % 2, :]).then_inc(y_out[j % 2], 16)
                    if more:
                        load_tile(q + 2, par, j)
                if more:
                    load_rows(b + 1 - par, par)

            rounds(first, sp.Fori(0, NCH // 2 - 1), chunk)
            for i in range(2):
                sp.wait_ge(y_out[i], NCH * TPC // 2 * 16)

        @block.gpsimd
        def _(pool):

            def inverse_deviation(r):
                pool.wait_ge(mv_ready, r * TPC + TPC)
                apart(pool)
                nc.gpsimd.tensor_scalar(rstd[:, 0, :], mv[:, :, 1], EPS, None, ALU.add).then_inc(var_eps, 1)
                pool.wait_ge(var_eps, r + 1)
                nc.gpsimd.tensor_tensor(rstd[:, 1, :], rstd[:, 0, :], K.expo[:, 0:TPC], ALU.pow).then_inc(rstd_ready, 1)

            def low(q, m):
                pool.wait_ge(ahi_ready, q * FC + m + 1)
                nc.gpsimd.tensor_tensor(alo[:, m, :], sq[:, m % 2, :], ahi[:, m, :].bitcast(f32), ALU.subtract).then_inc(alo_ready, 1)

            def send(par, n):
                c, j = n // TPC, n % TPC
                nc.gpsimd.indirect_dma_start(out=K.xs, out_offset=bass.IndirectOffsetOnAxis(ap=slotu[:, par, c, j:j + 1], axis=0),
                                             in_=h2[:, par, j, :], in_offset=None).then_inc(sent[par], 16)

            def chunk(q, par, b):
                for m in range(FC):
                    low(q, m)
                    if m == 1 and b is not None:
                        inverse_deviation(q + 1)
                    if m == 0:
                        pool.wait_ge(slots_ready, q + 1)
                        apart(pool)
                    send(par, m)
                for j in range(TPC):
                    pool.wait_ge(y_scaled, q * TPC + j + 1)
                    nc.gpsimd.tensor_tensor(y[:, j % 2, :], y[:, j % 2, :], xb[:, par, j, :], ALU.add).then_inc(y_ready, 1)

            rounds(lambda: inverse_deviation(0), pool.Fori(0, NCH // 2 - 1), chunk)
            for i in range(2):
                pool.wait_ge(sent[i], NCH * TPC * 16)

        @block.scalar
        def _(act):
            def high(r, par, j):
                act.wait_ge(t_done, r * TPC + j + 1)
                nc.scalar.activation(thi[:, par, :, j * P:(j + 1) * P], tp[j % 2][:, :, :], ACT.Copy).then_inc(thi_ready, 1)

            def sigmoid(r):
                act.wait_ge(r_done, r + 1)
                nc.scalar.activation(s_[:, :, :], rp[:, 0:TPC * E].rearrange("p (t e) -> p t e", e=E), ACT.Sigmoid).then_inc(s_ready, 1)

            def first():
                for j in range(TPC):
                    high(0, 0, j)
                sigmoid(0)

            def chunk(q, par, b):
                for m in range(FC + 1):
                    if m < FC:
                        act.wait_ge(up_done, q * FC + m + 1)
                        if m >= 2:
                            act.wait_ge(sq_ready, q * FC + m - 1)
                        else:
                            act.wait_ge(sq_ready, q * FC)
                        nc.scalar.activation(relu[:, m % 2, :], upb[m % 2][:, :], ACT.Relu).then_inc(relu_ready, 1)
                    if m >= 1:
                        act.wait_ge(sq_ready, q * FC + m)
                        nc.scalar.activation(ahi[:, m - 1, :], sq[:, (m - 1) % 2, :], ACT.Copy).then_inc(ahi_ready, 1)
                    if b is not None and T_FROM <= m < T_FROM + TPC:
                        high(q + 1, 1 - par, m - T_FROM)
                if b is not None:
                    sigmoid(q + 1)

            rounds(first, act.Fori(0, NCH // 2 - 1), chunk)

        @block.vector
        def _(dve):
            STEPS_R = 32

            def ln_stats(r, par, b):
                dve.wait_ge(xb_in[par], b * (TPC * 16) + TPC * 16)
                for j in range(TPC):
                    nc.vector.bn_stats(stats[:, j, :], xb[:, par, j, :]).then_inc(bn, 1)
                dve.wait_ge(bn, r * TPC + TPC)
                apart(dve)
                for j in range(TPC):
                    nc.vector.bn_aggr(mv[:, j, :], stats[:, j, :]).then_inc(mv_ready, 1)

            def ln_norm(r, par, b, j):
                hj = h2[:, par, j, :]
                if j == 0:
                    dve.wait_ge(rstd_ready, r + 1)
                    dve.wait_ge(bc_in[par], b * 16 + 16)
                nc.vector.scalar_tensor_tensor(hj, xb[:, par, j, :], mv[:, j, 0:1], bc[:, par, 1, :], ALU.subtract, ALU.mult)\
                    .then_inc(h2_scaled, 1)
                dve.wait_ge(h2_scaled, r * TPC + j + 1)
                nc.vector.scalar_tensor_tensor(hj, hj, rstd[:, 1, j:j + 1], bc[:, par, 0, :], ALU.mult, ALU.add).then_inc(h2_ready, 1)

            def low(r, par, j):
                dve.wait_ge(thi_ready, r * TPC + j + 1)
                nc.vector.tensor_tensor(tlo[:, par, :, j * P:(j + 1) * P], tp[j % 2][:, :, :],
                                        thi[:, par, :, j * P:(j + 1) * P].bitcast(f32), ALU.subtract).then_inc(tlo_ready, 1)

            n = [0]

            def step_of(r):
                def then(ins):
                    n[0] += 1
                    ins.then_inc(step, 1)
                    dve.wait_ge(step, r * STEPS_R + n[0])
                return then

            def route(r, par):
                n[0] = 0
                then = step_of(r)
                tt, ts, red = nc.vector.tensor_tensor, nc.vector.tensor_scalar, nc.vector.tensor_reduce
                dve.wait_ge(s_ready, r + 1)
                then(tt(sbias[:, :, :], s_[:, :, :], K.ebias[:, :].unsqueeze(1).broadcast_to([P, TPC, E]), ALU.add))
                v = sbias[:, :, :].rearrange("p t (g a b) -> p t g a b", a=2, b=2)
                tt(g2[:, 0, :, :], v[:, :, :, 0, 0], v[:, :, :, 0, 1], ALU.max)
                tt(g2[:, 1, :, :], v[:, :, :, 1, 0], v[:, :, :, 1, 1], ALU.max)
                tt(g2[:, 2, :, :], v[:, :, :, 0, 0], v[:, :, :, 0, 1], ALU.min)
                then(tt(g2[:, 3, :, :], v[:, :, :, 1, 0], v[:, :, :, 1, 1], ALU.min))
                tt(g2[:, 4, :, :], g2[:, 0, :, :], g2[:, 1, :, :], ALU.min)
                tt(g2[:, 5, :, :], g2[:, 2, :, :], g2[:, 3, :, :], ALU.max)
                then(tt(g2[:, 0, :, :], g2[:, 0, :, :], g2[:, 1, :, :], ALU.max))
                then(tt(g2[:, 1, :, :], g2[:, 4, :, :], g2[:, 5, :, :], ALU.max))
                then(tt(g2[:, 2, :, :], g2[:, 0, :, :], g2[:, 1, :, :], ALU.add))
                gi = g2[:, 2, :, :].unsqueeze(2).broadcast_to([P, TPC, NG, NG])
                gj = g2[:, 2, :, :].unsqueeze(3).broadcast_to([P, TPC, NG, NG])
                tt(cmp[:, 0], gi, gj, ALU.is_gt)
                then(tt(cmp[:, 1], gi, gj, ALU.is_equal))
                then(tt(cmp[:, 1], cmp[:, 1], K.gtri[:, :, :].unsqueeze(1).broadcast_to([P, TPC, NG, NG]), ALU.mult))
                then(tt(cmp[:, 0], cmp[:, 0], cmp[:, 1], ALU.add))
                then(red(rank[:, :, :], cmp[:, 0], AX.X, ALU.add))
                then(ts(rank[:, :, :], rank[:, :, :], float(2), None, ALU.is_lt))
                masked = m16[:, 0, :, :]
                then(tt(masked.rearrange("p t (g i) -> p t g i", i=GSZ), sbias[:, :, :].rearrange("p t (g i) -> p t g i", i=GSZ),
                        rank[:, :, :].unsqueeze(3).broadcast_to([P, TPC, NG, GSZ]), ALU.mult))
                order = K.order[:, :].unsqueeze(1).broadcast_to([P, TPC, E])
                for c in range(2):
                    then(red(top[:, 0, :, 0], masked, AX.X, ALU.max))
                    then(tt(m16[:, 1, :, :], masked, top[:, 0, :, :].broadcast_to([P, TPC, E]), ALU.is_equal))
                    then(tt(m16[:, 1, :, :], m16[:, 1, :, :], order, ALU.mult))
                    then(red(top[:, 1, :, 0], m16[:, 1, :, :], AX.X, ALU.max))
                    nc.vector.tensor_copy(K.choice[:, c, bass.ds(r * TPC, TPC)], top[:, 1, :, 0])
                    then(tt(oh[:, c, :, :], order, top[:, 1, :, :].broadcast_to([P, TPC, E]), ALU.is_equal))
                    if c == 0:
                        then(nc.vector.scalar_tensor_tensor(m16[:, 0, :, :], oh[:, 0, :, :], -3e38, masked, ALU.mult, ALU.add))
                nc.vector.tensor_tensor(chosen[:, :, :], oh[:, 0, :, :], oh[:, 1, :, :], ALU.add).then_inc(chosen_ready, 1)
                for c in range(2):
                    last = tt(m16[:, 1 + c, :, :], oh[:, c, :, :], s_[:, :, :], ALU.mult)
                then(last)
                red(ws[:, 0, :], m16[:, 1, :, :], AX.X, ALU.add)
                then(red(ws[:, 1, :], m16[:, 2, :, :], AX.X, ALU.add))
                then(tt(ws[:, 2, :], ws[:, 0, :], ws[:, 1, :], ALU.add))
                then(ts(ws[:, 2, :], ws[:, 2, :], 1e-20, None, ALU.add))
                then(nc.vector.reciprocal(ws[:, 3, :], ws[:, 2, :]))
                for c in range(2):
                    tt(K.wts[:, c, bass.ds(r * TPC, TPC)], ws[:, c, :], ws[:, 3, :], ALU.mult)

            def place_rows(r, par):
                then = step_of(r)
                tt, red = nc.vector.tensor_tensor, nc.vector.tensor_reduce
                dve.wait_ge(place_done, r + 1)
                then(tt(place[:, :, :], pl[:, 0:TPC * E].rearrange("p (t e) -> p t e", e=E),
                        K.count[:, :].unsqueeze(1).broadcast_to([P, TPC, E]), ALU.add))
                then(tt(K.count[:, :], K.count[:, :], pl[:, TPC * E:(TPC + 1) * E], ALU.add))
                then(tt(place[:, :, :], place[:, :, :], K.region[:, :].unsqueeze(1).broadcast_to([P, TPC, E]), ALU.add))
                for c in range(2):
                    last = tt(m16[:, 1 + c, :, :], place[:, :, :], oh[:, c, :, :], ALU.mult)
                then(last)
                for c in range(2):
                    last = red(slotf[:, c, :], m16[:, 1 + c, :, :], AX.X, ALU.add)
                then(last)
                nc.vector.tensor_copy(K.slots[:, :, bass.ds(r * TPC, TPC)], slotf[:, :, :])
                nc.vector.tensor_copy(slotu[:, par, :, :], slotf[:, :, :]).then_inc(slots_ready, 1)
                assert n[0] == STEPS_R, n[0]

            def square(q, m):
                dve.wait_ge(relu_ready, q * FC + m + 1)
                if m >= 2:
                    dve.wait_ge(alo_ready, q * FC + m - 1)
                else:
                    dve.wait_ge(alo_ready, q * FC)
                nc.vector.tensor_tensor(sq[:, m % 2, :], relu[:, m % 2, :], relu[:, m % 2, :], ALU.mult).then_inc(sq_ready, 1)

            def scaled(q, par, j):
                dve.wait_ge(dn_done, q * TPC + j + 1)
                dve.wait_ge(y_out[j % 2], q * (TPC // 2 * 16) + j // 2 * 16)
                nc.vector.tensor_tensor(y[:, j % 2, :], dnb[j % 2][:, :], bc[:, par, 2, :], ALU.mult).then_inc(y_scaled, 1)

            def first():
                ln_stats(0, 0, 0)
                for j in range(TPC):
                    ln_norm(0, 0, 0, j)
                for j in range(TPC):
                    low(0, 0, j)
                route(0, 0)
                place_rows(0, 0)

            def chunk(q, par, b):
                for m in range(FC):
                    square(q, m)
                    if b is not None:
                        if m == 1:
                            ln_stats(q + 1, 1 - par, b)
                            dve.wait_ge(sent[1 - par], b * (TPC * 2 * 16))
                        if T_FROM - 2 <= m < T_FROM - 2 + TPC:
                            ln_norm(q + 1, 1 - par, b, m - (T_FROM - 2))
                        if T_FROM <= m:
                            low(q + 1, 1 - par, m - T_FROM)
                scaled(q, par, 0)
                if b is not None:
                    route(q + 1, 1 - par)
                scaled(q, par, 1)
                scaled(q, par, 2)
                if b is not None:
                    place_rows(q + 1, 1 - par)
                scaled(q, par, 3)

            rounds(first, dve.Fori(0, NCH // 2 - 1), chunk)

        @block.tensor
        def _(pe):
            def transposes(r, par, j):
                pe.wait_ge(h2_ready, r * TPC + j + 1)
                if j >= 2:
                    pe.wait_ge(tlo_ready, r * TPC + j - 1)
                else:
                    pe.wait_ge(tlo_ready, r * TPC)
                for k in range(KC):
                    last = nc.tensor.transpose(tp[j % 2][:, k, :], h2[:, par, j, k * P:(k + 1) * P], K.ident[:, :])
                last.then_inc(t_done, 1)

            def router(r, par, j):
                pe.wait_ge(tlo_ready, r * TPC + j + 1)
                if j == 0:
                    pe.wait_ge(s_ready, r)
                terms = [(x_, w_, k) for k in range(KC) for x_, w_ in ((thi, K.rwhi), (thi, K.rwlo), (tlo, K.rwhi))]
                for n, (x_, w_, k) in enumerate(terms):
                    last = nc.tensor.matmul(rp[:, j * E:(j + 1) * E], x_[:, par, k, j * P:(j + 1) * P], w_[:, k, :],
                                            start=(n == 0), stop=(n == len(terms) - 1))
                if j == TPC - 1:
                    last.then_inc(r_done, 1)

            def places(r):
                pe.wait_ge(chosen_ready, r + 1)
                for j in range(TPC + 1):
                    o = pl[:, j * E:(j + 1) * E]
                    for i in range(j):
                        last = nc.tensor.matmul(o, K.ones[:, :], chosen[:, i, :], start=(i == 0), stop=(i == j - 1 and j == TPC))
                    if j < TPC:
                        last = nc.tensor.matmul(o, K.tri[:, :], chosen[:, j, :], start=(j == 0), stop=True)
                last.then_inc(place_done, 1)

            def up(q, par, m):
                if m >= 2:
                    pe.wait_ge(relu_ready, q * FC + m - 1)
                else:
                    pe.wait_ge(relu_ready, q * FC)
                terms = [(w_, x_, k) for k in range(KC) for w_, x_ in ((K.uphi, thi), (K.uphi, tlo), (K.uplo, thi))]
                for n, (w_, x_, k) in enumerate(terms):
                    last = nc.tensor.matmul(upb[m % 2][:, :], w_[:, k, m * P:(m + 1) * P], x_[:, par, k, :],
                                            start=(n == 0), stop=(n == len(terms) - 1))
                last.then_inc(up_done, 1)

            def down(q, j):
                if j >= 2:
                    pe.wait_ge(y_scaled, q * TPC + j - 1)
                else:
                    pe.wait_ge(y_scaled, q * TPC)
                for k in range(FC):
                    if j == 0:
                        pe.wait_ge(alo_ready, q * FC + k + 1)
                    for n, (a_, w_) in enumerate(((ahi, K.dnhi), (ahi, K.dnlo), (alo, K.dnhi))):
                        last = nc.tensor.matmul(dnb[j % 2][:, :], a_[:, k, j * P:(j + 1) * P], w_[:, k, :],
                                                start=(k == 0 and n == 0), stop=(k == FC - 1 and n == 2))
                last.then_inc(dn_done, 1)

            def first():
                for j in range(TPC):
                    transposes(0, 0, j)
                for j in range(TPC):
                    router(0, 0, j)
                places(0)

            def chunk(q, par, b):
                for m in range(FC):
                    up(q, par, m)
                    if b is not None and m >= T_FROM:
                        transposes(q + 1, 1 - par, m - T_FROM)
                if b is not None:
                    router(q + 1, 1 - par, 0)
                    router(q + 1, 1 - par, 1)
                down(q, 0)
                if b is not None:
                    router(q + 1, 1 - par, 2)
                    router(q + 1, 1 - par, 3)
                down(q, 1)
                down(q, 2)
                if b is not None:
                    places(q + 1)
                down(q, 3)

            rounds(first, pe.Fori(0, NCH // 2 - 1), chunk)


def program_c(nc, K, ctx):
    f32, f32r, bf16 = mybir.dt.float32, mybir.dt.float32r, mybir.dt.bfloat16
    with ExitStack() as a:
        sb = lambda n, s, d=f32: a.enter_context(nc.sbuf_tensor(n, s, d))
        K.uphi = sb("uphi", [P, KC, F], f32r)
        K.uplo = sb("uplo", [P, KC, F], f32r)
        K.dnhi = sb("dnhi", [P, FC, D], f32r)
        K.dnlo = sb("dnlo", [P, FC, D], f32r)
        K.rwhi = sb("rwhi", [P, KC, E], f32r)
        K.rwlo = sb("rwlo", [P, KC, E], f32r)
        K.ebias = sb("ebias", [P, E])
        K.order = sb("order", [P, E])
        K.region = sb("region", [P, E])
        K.gtri = sb("gtri", [P, NG, NG])
        K.tri = sb("tri", [P, P], bf16)
        K.ones = sb("ones", [P, P], bf16)
        shared_setup(nc, K)
        shared_phase(nc, K)

AHEAD = 3
XR = 4


def expert_setup(nc, K):
    f32, i32 = mybir.dt.float32, mybir.dt.int32
    ALU, AX = mybir.AluOpType, mybir.AxisListType
    ctx = ExitStack()
    with ctx:
        sb = lambda n, s, d=f32: ctx.enter_context(nc.sbuf_tensor(n, s, d))
        sem = lambda n: ctx.enter_context(nc.semaphore(n))
        zero = sb("zero_rows", [P, D])
        k_i, j_i, e_i = sb("k_i", [P, NTILE], i32), sb("j_i", [P, NET], i32), sb("e_i", [P, E], i32)
        kf, jf, ef = sb("kf", [P, NTILE]), sb("jf", [P, NET]), sb("ef", [P, E])
        more = sb("more", [P, E, NTILE])
        ntile = sb("ntile", [P, E])
        ones = sb("ones_e", [P, E])
        ends = sb("ends", [P, E])
        starts = sb("starts", [P, E])
        base = sb("base", [P, E])
        inside = sb("inside", [P, NET, E])
        other = sb("other", [P, NET, E])
        rowf = sb("rowf", [P, 4, NET])
        padf = sb("padf", [P, E])
        order, shift = sb("order_e", [P, E]), sb("shift", [P, E])
        mine = sb("mine", [P, 2 * NTILE, E])
        moved = sb("moved", [P, 2 * NTILE])
        padi = sb("padi", [P, E], i32)
        iotas, zeroed, step, tables = sem("iotas"), sem("rows_zeroed"), sem("table_step"), sem("tables")
        w_in, padded = sem("we_in"), sem("padded")
        block = ctx.enter_context(nc.Block())

        @block.sync
        def _(sp):
            for e in range(E):
                sp.dma_start(K.wu[:, e * KC * EI:(e + 1) * KC * EI].rearrange("p (k n) -> p k n", k=KC),
                             K.wup[e, :, :].rearrange("(k p) n -> p k n", p=P)).then_inc(w_in, 16)
            sp.wait_ge(tables, 1)
            sp.wait_ge(zeroed, 1)
            for e in range(E):
                row = sp.value_load(padi[0:1, e:e + 1], min_val=e * REGION, max_val=e * REGION + T)
                sp.dma_start(K.xs[bass.ds(row, P), :], zero[:, :]).then_inc(padded, 16)
            sp.wait_ge(padded, 16 * E)
            sp.wait_ge(w_in, 16 * 2 * E)

        @block.scalar
        def _(act):
            for e in range(E):
                act.dma_start(K.wd[:, e * EC * D:(e + 1) * EC * D].rearrange("p (k n) -> p k n", k=EC),
                              K.wdn[e, :, :].rearrange("(k p) n -> p k n", p=P)).then_inc(w_in, 16)

        @block.gpsimd
        def _(pool):
            nc.gpsimd.memset(zero[:, :], 0.0).then_inc(zeroed, 1)
            nc.gpsimd.iota(k_i[:, :], pattern=[[P, NTILE]], base=0, channel_multiplier=0).then_inc(iotas, 1)
            nc.gpsimd.iota(j_i[:, :], pattern=[[1, NET]], base=0, channel_multiplier=0).then_inc(iotas, 1)
            nc.gpsimd.iota(e_i[:, :], pattern=[[1, E]], base=0, channel_multiplier=0).then_inc(iotas, 1)

        @block.vector
        def _(dve):
            n = [0]

            def then(ins):
                n[0] += 1
                ins.then_inc(step, 1)
                dve.wait_ge(step, n[0])

            tt, ts, red = nc.vector.tensor_tensor, nc.vector.tensor_scalar, nc.vector.tensor_reduce
            dve.wait_ge(iotas, 3)
            nc.vector.memset(ones[:, :], 1.0)
            nc.vector.tensor_copy(kf[:, :], k_i[:, :])
            nc.vector.tensor_copy(jf[:, :], j_i[:, :])
            then(nc.vector.tensor_copy(ef[:, :], e_i[:, :]))
            then(tt(more[:, :, :], K.count[:, :].unsqueeze(2).broadcast_to([P, E, NTILE]),
                    kf[:, :].unsqueeze(1).broadcast_to([P, E, NTILE]), ALU.is_gt))
            then(red(ntile[:, :], more[:, :, :], AX.X, ALU.add))
            then(nc.vector.tensor_tensor_scan(ends[:, :], ones[:, :], ntile[:, :], 0.0, ALU.mult, ALU.add))
            then(tt(starts[:, :], ends[:, :], ntile[:, :], ALU.subtract))
            then(ts(base[:, :], starts[:, :], -float(P), -float(DUMMY), ALU.mult, ALU.add))
            ts(padf[:, :], ef[:, :], float(REGION), None, ALU.mult)
            then(nc.vector.scalar_tensor_tensor(base[:, :], ef[:, :], float(REGION), base[:, :], ALU.mult, ALU.add))
            then(tt(padf[:, :], padf[:, :], K.count[:, :], ALU.add))
            nc.vector.tensor_copy(padi[:, :], padf[:, :])
            bj = jf[:, :].unsqueeze(2).broadcast_to([P, NET, E])
            be = lambda a: a[:, :].unsqueeze(1).broadcast_to([P, NET, E])
            bc = K.choice[:, :, :].rearrange("p c t -> p (c t)").unsqueeze(2).broadcast_to([P, 2 * NTILE, E])
            bx = lambda a: a[:, :].unsqueeze(1).broadcast_to([P, 2 * NTILE, E])
            ts(order[:, :], ef[:, :], -1.0, float(E), ALU.mult, ALU.add)
            then(ts(shift[:, :], base[:, :], float(DUMMY), None, ALU.add))
            then(tt(mine[:, :, :], bc, bx(order), ALU.is_equal))
            then(tt(mine[:, :, :], mine[:, :, :], bx(shift), ALU.mult))
            then(red(moved[:, :], mine[:, :, :], AX.X, ALU.add))
            then(tt(moved[:, :], K.slots[:, :, :].rearrange("p c t -> p (c t)"), moved[:, :], ALU.subtract))
            nc.vector.tensor_copy(K.rows[:, :, :].rearrange("p c t -> p (c t)"), moved[:, :])
            tt(inside[:, :, :], be(starts), bj, ALU.is_le)
            then(tt(other[:, :, :], be(ends), bj, ALU.is_le))
            then(tt(inside[:, :, :], inside[:, :, :], other[:, :, :], ALU.subtract))
            red(rowf[:, 0, :], inside[:, :, :], AX.X, ALU.add)
            then(tt(other[:, :, :], inside[:, :, :], be(base), ALU.mult))
            then(red(rowf[:, 1, :], other[:, :, :], AX.X, ALU.add))
            then(tt(other[:, :, :], inside[:, :, :], be(ef), ALU.mult))
            then(red(rowf[:, 2, :], other[:, :, :], AX.X, ALU.add))
            nc.vector.tensor_copy(K.eid[:, :], rowf[:, 2, :])
            then(ts(rowf[:, 3, :], jf[:, :], float(P), None, ALU.mult))
            then(tt(rowf[:, 3, :], rowf[:, 3, :], rowf[:, 0, :], ALU.mult))
            then(tt(rowf[:, 3, :], rowf[:, 3, :], rowf[:, 1, :], ALU.add))
            then(ts(rowf[:, 0, :], rowf[:, 3, :], float(DUMMY), None, ALU.add))
            nc.vector.tensor_copy(K.xrow[:, :], rowf[:, 0, :]).then_inc(tables, 1)


def expert_phase(nc, K):
    f32 = mybir.dt.float32
    ALU, ACT = mybir.AluOpType, mybir.ActivationFunctionType
    ctx = ExitStack()
    with ctx:
        sb = lambda n, s, d=f32: ctx.enter_context(nc.sbuf_tensor(n, s, d))
        pb = lambda n, s: ctx.enter_context(nc.psum_tensor(n, s, f32))
        sem = lambda n: ctx.enter_context(nc.semaphore(n))
        x = sb("x_e", [P, XR, D])
        xT = sb("xT_e", [P, 2, KC, P])
        r = sb("r_e", [P, 2, EI])
        a = sb("a_e", [P, 2, EI])
        aT = sb("aT_e", [P, 2, EC, P])
        y = sb("y_e", [P, XR, D])
        txb = [pb(f"tx{i}", [P, KC, P]) for i in range(2)]
        ub = [pb(f"ue{i}", [P, 512]) for i in range(2)]
        tab = [pb(f"ta{i}", [P, 512]) for i in range(2)]
        db = [pb(f"de{i}", [P, D]) for i in range(2)]
        x_in = [sem(f"xe_in{i}") for i in range(XR)]
        y_out = [sem(f"ye_out{i}") for i in range(XR)]
        tx_done, xT_ready, u_done, r_ready, a_ready, ta_done, aT_ready, d_done, y_ready = (sem(n) for n in
            ("tx_done", "xT_ready", "ue_done", "re_ready", "ae_ready", "ta_done", "aT_ready", "de_done", "ye_ready"))
        block = ctx.enter_context(nc.Block())
        FULL = (NET - AHEAD) // XR * XR

        def rounds(eng, round_):
            for j in range(-AHEAD, XR):
                round_(j, j % XR)
            with eng.Fori(1, FULL // XR) as i:
                for s in range(XR):
                    round_(i * XR + s, s)
            for j in range(FULL, NET):
                round_(j, j % XR)

        def known(j):
            return isinstance(j, int)

        def has(j):
            return not known(j) or 0 <= j < NET

        def wait(eng, s, value):
            if not (known(value) and value <= 0):
                eng.wait_ge(s, value)

        @block.sync
        def _(sp):
            def load(j, k, s):
                if has(j + k if known(j) else j):
                    t = j + k
                    wait(sp, tx_done, t - XR + 1)
                    row = sp.value_load(K.xrow[0:1, t:t + 1] if known(t) else K.xrow[0:1, bass.ds(t, 1)], min_val=0, max_val=ROWS - P)
                    sp.dma_start(x[:, (s + k) % XR, :], K.xs[bass.ds(row, P), :]).then_inc(x_in[(s + k) % XR], 16)

            def store(j, s):
                if has(j):
                    wait(sp, y_ready, j + 1)
                    sp.dma_start(K.ys[bass.ds(j * P, P), :], y[:, s, :]).then_inc(y_out[s], 16)

            for t in range(AHEAD):
                load(t - 2 * AHEAD, 2 * AHEAD, (t - 2 * AHEAD) % XR)
            for j in range(-AHEAD, 0):
                load(j, 2 * AHEAD, j % XR)
            L = (NET - 2 * AHEAD) // XR * XR
            with sp.Fori(0, L // XR) as i:
                for s in range(XR):
                    load(i * XR + s, 2 * AHEAD, s)
                    store(i * XR + s, s)
            for j in range(L, NET):
                load(j, 2 * AHEAD, j % XR)
                store(j, j % XR)
            for s in range(XR):
                sp.wait_ge(y_out[s], 16 * len(range(s, NET, XR)))

        @block.scalar
        def _(act):
            def round_(j, s):
                if has(j + 3 if known(j) else j):
                    act.wait_ge(tx_done, j + 4)
                    wait(act, u_done, j + 2)
                    nc.scalar.activation(xT[:, (s + 3) % 2, :, :], txb[(s + 3) % 2][:, :, :], ACT.Copy).then_inc(xT_ready, 1)
                if has(j + 2 if known(j) else j):
                    act.wait_ge(u_done, j + 3)
                    wait(act, a_ready, j + 1)
                    nc.scalar.activation(r[:, s % 2, :], ub[s % 2][:, 0:EI], ACT.Relu).then_inc(r_ready, 1)

            rounds(act, round_)

        @block.vector
        def _(dve):
            def round_(j, s):
                if has(j + 2 if known(j) else j):
                    dve.wait_ge(r_ready, j + 3)
                    wait(dve, ta_done, j + 1)
                    nc.vector.tensor_tensor(a[:, s % 2, :], r[:, s % 2, :], r[:, s % 2, :], ALU.mult).then_inc(a_ready, 1)
                if has(j + 1 if known(j) else j):
                    dve.wait_ge(ta_done, j + 2)
                    wait(dve, d_done, j)
                    nc.vector.tensor_copy(aT[:, (s + 1) % 2, :, :], tab[(s + 1) % 2][:, 0:EC * P]).then_inc(aT_ready, 1)
                if has(j):
                    dve.wait_ge(d_done, j + 1)
                    if known(j):
                        wait(dve, y_out[s], j // XR * 16)
                    else:
                        dve.wait_ge(y_out[s], (j - s) * (16 // XR))
                    nc.vector.tensor_copy(y[:, s, :], db[s % 2][:, :]).then_inc(y_ready, 1)

            rounds(dve, round_)

        @block.tensor
        def _(pe):
            def expert(t):
                return pe.value_load(K.eid[0:1, t:t + 1] if known(t) else K.eid[0:1, bass.ds(t, 1)], min_val=0, max_val=E - 1)

            def round_(j, s):
                if has(j + 3 if known(j) else j):
                    t, z = j + 3, (s + 3) % XR
                    pe.wait_ge(x_in[z], t // XR * 16 + 16 if known(t) else (j - s) * (16 // XR) + ((s + 3) // XR + 1) * 16)
                    wait(pe, xT_ready, j + 2)
                    for k in range(KC):
                        last = nc.tensor.transpose(txb[z % 2][:, k, :], x[:, z, k * P:(k + 1) * P], K.ident[:, :])
                    last.then_inc(tx_done, 1)
                if has(j + 2 if known(j) else j):
                    e = expert(j + 2)
                    pe.wait_ge(xT_ready, j + 3)
                    wait(pe, r_ready, j + 1)
                    for k in range(KC):
                        last = nc.tensor.matmul(ub[s % 2][:, 0:EI], xT[:, s % 2, k, :], K.wu[:, bass.ds(e * (KC * EI) + k * EI, EI)],
                                                start=(k == 0), stop=(k == KC - 1))
                    last.then_inc(u_done, 1)
                if has(j + 1 if known(j) else j):
                    pe.wait_ge(a_ready, j + 2)
                    wait(pe, aT_ready, j)
                    for k in range(EC):
                        last = nc.tensor.transpose(tab[(s + 1) % 2][:, k * P:(k + 1) * P], a[:, (s + 1) % 2, k * P:(k + 1) * P], K.ident[:, :])
                    last.then_inc(ta_done, 1)
                if has(j):
                    e = expert(j)
                    pe.wait_ge(aT_ready, j + 1)
                    wait(pe, y_ready, j - 1)
                    for k in range(EC):
                        last = nc.tensor.matmul(db[s % 2][:, :], aT[:, s % 2, k, :], K.wd[:, bass.ds(e * (EC * D) + k * D, D)],
                                                start=(k == 0), stop=(k == EC - 1))
                    last.then_inc(d_done, 1)

            rounds(pe, round_)


def combine_phase(nc, K):
    f32, u32 = mybir.dt.float32, mybir.dt.uint32
    ALU = mybir.AluOpType
    ctx = ExitStack()
    with ctx:
        sb = lambda n, s, d=f32: ctx.enter_context(nc.sbuf_tensor(n, s, d))
        sem = lambda n: ctx.enter_context(nc.semaphore(n))
        gb = sb("gb_f", [P, 2, D])
        base = sb("base_f", [P, 2, TPC, D])
        g = sb("g_f", [P, 2, TPC, 2, D])
        z = sb("z_f", [P, 2, TPC, D])
        idx = sb("idx_f", [P, 2, 2, TPC], u32)
        w = sb("w_f", [P, 2, 2, TPC])
        gb_in = [sem(f"gb_in{i}") for i in range(2)]
        base_in = [sem(f"base_in{i}") for i in range(2)]
        g_in = [[sem(f"g_in{i}_{j}") for j in range(TPC)] for i in range(2)]
        out_sent = [sem(f"out_sent{i}") for i in range(2)]
        idx_ready, first_done, both_done, gated, z_ready = (sem(n) for n in ("idx_ready", "first_done", "both_done", "gated", "z_ready"))
        block = ctx.enter_context(nc.Block())

        @block.sync
        def _(sp):
            def load(c, par, b, done):
                if done is not None:
                    sp.wait_ge(z_ready, done)
                sp.dma_start(gb[:, par, :], K.modd[bass.ds(b, 1), GB, :].broadcast_to([P, D])).then_inc(gb_in[par], 16)
                sp.dma_start(base[:, par, :, :], K.part[bass.ds(c * CH, CH), :].rearrange("(j p) d -> p j d", p=P)).then_inc(base_in[par], 16)

            def store(c, par):
                for j in range(TPC):
                    sp.wait_ge(z_ready, c * TPC + j + 1)
                    sp.dma_start(K.out[bass.ds(c * CH + j * P, P), :], z[:, par, j, :]).then_inc(out_sent[par], 16)

            load(0, 0, 0, None)
            load(1, 1, 0, None)
            with sp.Fori(0, NB - 1) as b:
                for par in range(2):
                    store(2 * b + par, par)
                    load(2 * b + par + 2, par, b + 1, (2 * b + par + 1) * TPC)
            for par in range(2):
                store(NCH - 2 + par, par)
            for par in range(2):
                sp.wait_ge(out_sent[par], NCH // 2 * TPC * 16)

        @block.gpsimd
        def _(pool):
            with pool.Fori(0, NB) as b:
                for par in range(2):
                    pool.wait_ge(idx_ready, 2 * b + par + 1)
                    apart(pool)
                    for j in range(TPC):
                        for c in range(2):
                            nc.gpsimd.indirect_dma_start(out=g[:, par, j, c, :], out_offset=None, in_=K.ys,
                                                         in_offset=bass.IndirectOffsetOnAxis(ap=idx[:, par, c, j:j + 1], axis=0))\
                                .then_inc(g_in[par][j], 16)

        @block.vector
        def _(dve):
            def indices(c, par):
                nc.vector.tensor_copy(w[:, par, :, :], K.wts[:, :, bass.ds(c * TPC, TPC)])
                nc.vector.tensor_copy(idx[:, par, :, :], K.rows[:, :, bass.ds(c * TPC, TPC)]).then_inc(idx_ready, 1)

            def chunk(b, par):
                c = 2 * b + par
                dve.wait_ge(gb_in[par], b * 16 + 16)
                dve.wait_ge(base_in[par], b * 16 + 16)
                dve.wait_ge(out_sent[par], b * (TPC * 16))
                for j in range(TPC):
                    n = c * TPC + j
                    dve.wait_ge(g_in[par][j], b * 32 + 32)
                    zj = z[:, par, j, :]
                    nc.vector.tensor_scalar(zj, g[:, par, j, 0, :], w[:, par, 0, j:j + 1], None, ALU.mult).then_inc(first_done, 1)
                    dve.wait_ge(first_done, n + 1)
                    nc.vector.scalar_tensor_tensor(zj, g[:, par, j, 1, :], w[:, par, 1, j:j + 1], zj, ALU.mult, ALU.add).then_inc(both_done, 1)
                    dve.wait_ge(both_done, n + 1)
                    nc.vector.tensor_tensor(zj, zj, gb[:, par, :], ALU.mult).then_inc(gated, 1)
                    dve.wait_ge(gated, n + 1)
                    nc.vector.tensor_tensor(zj, zj, base[:, par, j, :], ALU.add).then_inc(z_ready, 1)

            indices(0, 0)
            with dve.Fori(0, NB - 1) as b:
                indices(2 * b + 1, 1)
                chunk(b, 0)
                indices(2 * b + 2, 0)
                chunk(b, 1)
            indices(NCH - 1, 1)
            chunk(NB - 1, 0)
            chunk(NB - 1, 1)


def program_e(nc, K, ctx):
    f32, i32 = mybir.dt.float32, mybir.dt.int32
    with ExitStack() as a:
        sb = lambda n, s, d=f32: a.enter_context(nc.sbuf_tensor(n, s, d))
        K.wu = sb("wu_e", [P, E * KC * EI])
        K.wd = sb("wd_e", [P, E * EC * D])
        K.eid = sb("eid", [P, NET], i32)
        K.xrow = sb("xrow", [P, NET], i32)
        expert_setup(nc, K)
        expert_phase(nc, K)
    combine_phase(nc, K)


def block_kernel(nc, x, Wqkv, bqkv, Wo, bo, rw, eb, wup, wdn, sup, sdn, c, wmod, out):
    f32, u32 = mybir.dt.float32, mybir.dt.uint32
    K = Kept()
    K.x = x.rearrange("b s d -> (b s) d")
    K.out = out.rearrange("b s d -> (b s) d")
    K.Wqkv, K.bqkv, K.Wo, K.bo, K.rw, K.eb, K.wup, K.wdn, K.sup, K.sdn, K.c, K.wmod = (
        Wqkv, bqkv, Wo, bo, rw, eb, wup, wdn, sup, sdn, c, wmod)
    K.modd = nc.dram_tensor("modd", [NB, 7, D], f32, kind="Internal").ap()
    K.x1d = nc.dram_tensor("x1d", [T, D], f32, kind="Internal").ap()
    K.part = nc.dram_tensor("part", [T, D], f32, kind="Internal").ap()
    K.xs = nc.dram_tensor("xs", [ROWS, D], f32, kind="Internal").ap()
    K.ys = nc.dram_tensor("ys", [NET * P, D], f32, kind="Internal").ap()
    with ExitStack() as ctx:
        K.count = ctx.enter_context(nc.sbuf_tensor("count", [P, E], f32))
        K.wts = ctx.enter_context(nc.sbuf_tensor("wts", [P, 2, NTILE], f32))
        K.slots = ctx.enter_context(nc.sbuf_tensor("slots", [P, 2, NTILE], f32))
        K.choice = ctx.enter_context(nc.sbuf_tensor("choice", [P, 2, NTILE], f32))
        K.rows = ctx.enter_context(nc.sbuf_tensor("rows", [P, 2, NTILE], u32))
        program_a(nc, K, ctx)
        program_c(nc, K, ctx)
        program_e(nc, K, ctx)


_INS = ['L0_attn_x', 'L0_attn_Wqkv', 'L0_attn_bqkv', 'L0_attn_Wo', 'L0_attn_bo', 'L0_ffn_router_weight', 'L0_ffn_e_bias',
        'L0_ffn_w_up', 'L0_ffn_w_down', 'L0_ffn_shared_up', 'L0_ffn_shared_down', 'L0_c', 'L0_wmod']
_OUTS = [((4, 1024, 512), 'float32')]


def kernel(**inputs):
    import numpy as _np
    import concourse.bacc as _bacc
    from concourse import mybir as _mybir
    from concourse.bass_utils import run_bass_kernel_spmd as _run

    nc = _bacc.Bacc("TRN2", target_bir_lowering=False, num_devices=1)
    arrays, args = {}, []
    for name in _INS:
        a = _np.ascontiguousarray(inputs[name])
        arrays[f"in_{name}_dram"] = a
        args.append(nc.dram_tensor(f"in_{name}_dram", a.shape, _mybir.dt.from_np(a.dtype), kind="ExternalInput").ap())
    for i, (shape, dtype) in enumerate(_OUTS):
        dt = _mybir.dt.from_np(_np.dtype(dtype))
        args.append(nc.dram_tensor(f"out_{i}_dram", shape, dt, kind="ExternalOutput").ap())
    block_kernel(nc, *args)
    r = _run(nc, [arrays], core_ids=[0])
    got = tuple(r.results[0][f"out_{i}_dram"] for i in range(len(_OUTS)))
    return got[0]
```

```python
import concourse.bass as bass
from concourse import mybir
from contextlib import ExitStack

P = 128
D = 512
KC = D // P
H, DH = 16, 32
NB, S = 4, 1024
T = NB * S
NT = S // P
SCALE = float(DH) ** -0.5
MASKED = -10000.0 / SCALE
NEG = -1e30
EPS = 1e-5
PRIMED = 1
SA, CA1, GA, SB, CB1, GB, GABO = range(7)


def setup_phase(nc, K):
    f32 = mybir.dt.float32
    ALU, ACT = mybir.AluOpType, mybir.ActivationFunctionType
    ctx = ExitStack()
    with ctx:
        sb = lambda n, s, d=f32: ctx.enter_context(nc.sbuf_tensor(n, s, d))
        sem = lambda n: ctx.enter_context(nc.semaphore(n))
        wraw = sb("wraw", [P, KC, 3 * D])
        wmod = sb("wmod_sb", [P, KC, 6 * D])
        cT = sb("cT", [P, KC, NB])
        sig = sb("sig", [P, KC, NB])
        silu = sb("silu", [P, KC, NB])
        bv4 = sb("bv4", [P, KC, NB])
        bo4 = sb("bo4", [NB, D])
        modr = sb("modr", [NB, 7, D])
        sgn = sb("sgn", [NB, 2, D])
        mag = sb("mag", [NB, 2, D])
        pm = [ctx.enter_context(nc.psum_tensor(f"pmod{i}", [P, 512], f32)) for i in range(7)]
        small_in, w_in = sem("small_in"), sem("w_in")
        wmod_in, wraw_in = [sem(f"wmod_in{n}") for n in range(6)], [sem(f"wraw_in{k}") for k in range(KC)]
        sig_done, silu_done, mod_mm, bo_mm = sem("sig_done"), sem("silu_done"), sem("mod_mm"), sem("bo_mm")
        hi_done, step, mod_stored, zeroed, consts = sem("w_hi_done"), sem("setup_step"), sem("mod_stored"), sem("c_zeroed"), sem("consts")
        mag_done, bv_done = sem("mag_done"), sem("bv_done")
        block = ctx.enter_context(nc.Block())

        @block.sync
        def _(sp):
            with nc.allow_non_contiguous_dma(reason="small vectors by partition"):
                for k in range(KC):
                    sp.dma_start(cT[:, k, :], K.c[:, k * P:(k + 1) * P].rearrange("b p -> p b")).then_inc(small_in, 16)
                sp.dma_start(K.bias[:, :], K.bqkv.rearrange("(g p) -> p g", p=P)).then_inc(small_in, 16)
            for n in range(6):
                sp.dma_start(wmod[:, :, n * D:(n + 1) * D], K.wmod[:, n * D:(n + 1) * D].rearrange("(k p) n -> p k n", p=P)).then_inc(wmod_in[n], 16)
            sp.dma_start(bo4[:, :], K.bo.rearrange("(a n) -> a n", a=1).broadcast_to([NB, D])).then_inc(w_in, 16)
            sp.dma_start(K.wo[:, :, :], K.Wo.rearrange("(k p) n -> p k n", p=P)).then_inc(w_in, 16)
            for k in range(KC):
                sp.dma_start(wraw[:, k, :], K.Wqkv[k * P:(k + 1) * P, :]).then_inc(wraw_in[k], 16)
            sp.wait_ge(step, 9)
            sp.dma_start(K.modd, modr[:, :, :]).then_inc(mod_stored, 16)
            sp.wait_ge(mod_stored, 16)

        @block.gpsimd
        def _(pool):
            nc.gpsimd.memset(K.expo[:, :], -0.5).then_inc(zeroed, 1)
            nc.gpsimd.memset(K.ident[:, :], 0.0).then_inc(zeroed, 1)
            nc.gpsimd.memset(K.identb[:, :], 0.0).then_inc(zeroed, 1)
            nc.gpsimd.memset(K.mask_qk[:, :], 0.0).then_inc(zeroed, 1)
            nc.gpsimd.memset(K.mask_kq[:, :], 0.0).then_inc(zeroed, 1)
            nc.gpsimd.memset(K.V[:, NT * D:NT * D + DH], 1.0).then_inc(zeroed, 1)
            nc.gpsimd.memset(K.S[:, :, :], 0.0).then_inc(zeroed, 1)
            nc.gpsimd.memset(K.ones_row[:, :], 1.0).then_inc(zeroed, 1)
            pool.wait_ge(zeroed, 8)
            for m in (K.ident, K.identb):
                nc.gpsimd.affine_select(out=m[:, :], in_=m[:, :], compare_op=ALU.not_equal, fill=1.0, base=0,
                                        pattern=[[-1, P]], channel_multiplier=1).then_inc(consts, 1)
            nc.gpsimd.affine_select(out=K.mask_qk[:, :], in_=K.mask_qk[:, :], compare_op=ALU.is_ge, fill=NEG, base=0,
                                    pattern=[[-1, P]], channel_multiplier=1).then_inc(consts, 1)
            nc.gpsimd.affine_select(out=K.mask_kq[:, :], in_=K.mask_kq[:, :], compare_op=ALU.is_ge, fill=NEG, base=0,
                                    pattern=[[1, P]], channel_multiplier=-1).then_inc(consts, 1)
            pool.wait_ge(consts, 4)

        @block.scalar
        def _(act):
            act.wait_ge(small_in, 80)
            nc.scalar.activation(sig[:, :, :], cT[:, :, :], ACT.Sigmoid).then_inc(sig_done, 1)
            act.wait_ge(mod_mm, 6)
            for i, src in ((0, 2), (1, 5)):
                nc.scalar.activation(mag[:, i, :], pm[src][0:NB, :], ACT.Abs, scale=2.0).then_inc(mag_done, 1)
            for k in range(KC):
                act.wait_ge(wraw_in[k], 16)
                nc.scalar.activation(K.whi[:, k, :], wraw[:, k, :], ACT.Copy).then_inc(hi_done, 1)

        @block.vector
        def _(dve):
            dve.wait_ge(zeroed, 8)
            for s in range(2):
                for e in range(2):
                    for n in range(4):
                        nc.vector.tensor_copy(K.stk[96:128, s, 1, e, n * (S // 4):(n + 1) * (S // 4)], K.ones_row[96:128, :])
            dve.wait_ge(sig_done, 1)
            nc.vector.tensor_tensor(silu[:, :, :], cT[:, :, :], sig[:, :, :], ALU.mult).then_inc(silu_done, 1)
            for i in range(NB):
                last = nc.vector.tensor_copy(bv4[:, :, i], K.bias[:, 2 * KC:3 * KC])
            last.then_inc(bv_done, 1)
            dve.wait_ge(mod_mm, 6)
            for kind, src, add in ((SA, 0, 0.0), (CA1, 1, 1.0), (SB, 3, 0.0), (CB1, 4, 1.0)):
                nc.vector.tensor_scalar(modr[:, kind, :], pm[src][0:NB, :], add, None, ALU.add).then_inc(step, 1)
            for i, src in ((0, 2), (1, 5)):
                dve.wait_ge(mag_done, i + 1)
                nc.vector.tensor_scalar(sgn[:, i, :], pm[src][0:NB, :], 0.0, 0.5, ALU.is_ge, ALU.subtract).then_inc(step, 1)
            dve.wait_ge(step, 6)
            for i, kind in ((0, GA), (1, GB)):
                nc.vector.scalar_tensor_tensor(modr[:, kind, :], mag[:, i, :], 0.5, sgn[:, i, :], ALU.max, ALU.mult)\
                    .then_inc(step, 1)
            dve.wait_ge(bo_mm, 1)
            nc.vector.tensor_tensor(bo4[:, :], pm[6][0:NB, :], bo4[:, :], ALU.add).then_inc(bo_mm, 1)
            dve.wait_ge(bo_mm, 2)
            dve.wait_ge(step, 8)
            nc.vector.tensor_tensor(modr[:, GABO, :], modr[:, GA, :], bo4[:, :], ALU.mult).then_inc(step, 1)
            for k in range(KC):
                dve.wait_ge(hi_done, k + 1)
                nc.vector.tensor_tensor(K.wlo[:, k, :], wraw[:, k, :], K.whi[:, k, :].bitcast(f32), ALU.subtract)

        @block.tensor
        def _(pe):
            pe.wait_ge(silu_done, 1)
            for n in range(6):
                pe.wait_ge(wmod_in[n], 16)
                for k in range(KC):
                    last = nc.tensor.matmul(pm[n][0:NB, :], silu[:, k, :], wmod[:, k, n * D:(n + 1) * D],
                                            start=(k == 0), stop=(k == KC - 1))
                last.then_inc(mod_mm, 1)
            pe.wait_ge(bv_done, 1)
            pe.wait_ge(w_in, 32)
            for k in range(KC):
                last = nc.tensor.matmul(pm[6][0:NB, :], bv4[:, k, :], K.wo[:, k, :], start=(k == 0), stop=(k == KC - 1))
            last.then_inc(bo_mm, 1)


M_FROM, M_RATE = 4, 3


def attention_phase(nc, K):
    f32, f32r = mybir.dt.float32, mybir.dt.float32r
    ALU, ACT, AX = mybir.AluOpType, mybir.ActivationFunctionType, mybir.AxisListType
    NPAIR = H // 2
    NHG = H // 4
    OUT = [*range(NT // 2, NT), *range(NT // 2)]
    STACKED = 2 * 3 * 16
    V_LAG = 3
    CH = 512
    CHUNKS = (1, 0)
    STEPS = [(c, i) for c in CHUNKS for i in range(4 * c + 4)]
    TURN = 4 * CHUNKS[0] + 4
    NST = len(STEPS)
    MUSES = []
    for qt in reversed(range(NT)):
        first = min((qt + 1) * P, CH)
        rest = (qt + 1) * P - first
        for n, k0, part in ((first, 0, 0), (rest, CH, 1)):
            if not n:
                continue
            if 2 * n <= CH:
                MUSES.append(((0, 1), qt, k0, n, part))
            else:
                MUSES += [((e,), qt, k0, n, part) for e in range(2)]
    NM = len(MUSES)
    M_DUE = [min(NM, max(0, M_RATE * (s - M_FROM + 1))) for s in range(NST + 1)]
    M_DUE[NST] = NM
    ring = []
    for j in range(NT):
        ring.append("hT")
        if j >= V_LAG:
            ring.append("v")
    ring += ["p"] * 4 + ["v"] * V_LAG + ["m"] * NM + ["mt"] * 2
    for p in range(NPAIR):
        if p + 1 < NPAIR:
            ring += ["m"] * NM
            if p % 2 == 0 and p + 2 < NPAIR:
                ring += ["p"] * 4
            ring += ["mt"] * 2
    ring += ["w"] * NT
    TOTAL = {k: ring.count(k) for k in set(ring)}
    assert len(ring) % 3 == 0, len(ring)

    ctx = ExitStack()
    with ctx:
        sb = lambda n, s, d=f32: ctx.enter_context(nc.sbuf_tensor(n, s, d))
        sem = lambda n: ctx.enter_context(nc.semaphore(n))
        mod_t = sb("mod_t", [P, 2, KC])
        ga_bc = sb("ga_bc", [P, D])
        gabo_bc = sb("gabo_bc", [P, D])
        xr = sb("xr", [P, 2, D])
        stats = sb("stats", [P, 2, 6])
        mv = sb("mv", [P, 2, 2])
        rstd = sb("rstd", [P, 2, 2])
        h = sb("h", [P, 2, KC, P])
        hhi = sb("hhi", [P, KC, S], f32r)
        hlo = sb("hlo", [P, KC, S], f32r)
        st = sb("st", [P, 4, S], f32r)
        V, S_t = K.V, K.S
        mx = sb("mx", [P, 2, NT, 2])
        negm = sb("negm", [P, NT, 2])
        mhi = sb("mhi", [P, NT, 2], f32r)
        pr = sb("pr", [P, 3, 2, CH])
        oV = sb("oV", [P, 2, CH])
        oD = sb("oD", [P, 2, CH])
        oT = sb("oT", [P, KC, S])
        xt = oT[:, :, :].rearrange("p k s -> p (k s)").rearrange("p (j d) -> p j d", d=D)
        u = h[:, :, :, :].rearrange("p a k t -> p a (k t)")
        pb = lambda n, s: ctx.enter_context(nc.psum_tensor(n, s, f32))
        rb = [pb(f"ring{i}", [P, 512]) for i in range(3)]
        sc = [pb(f"sc{i}", [P, 2, 512]) for i in range(2)]
        O = pb("O", [P, 512])

        mod_in, mod2_in = sem("mod_in"), sem("mod2_in")
        xt_in = [sem(f"xt_in{i}") for i in range(NT // 2)]
        xr_in = [sem(f"xr_in{i}") for i in range(2)]
        x1_out = [sem(f"x1_out{i}") for i in range(2)]
        stk_in = [sem(f"stk_in{i}") for i in range(2)]
        bn, mv_ready, rstd_ready, xn_ready = sem("bn"), sem("mv_ready"), sem("rstd_ready"), sem("xn_ready")
        var_eps = sem("var_eps")
        t_done, h_ready, hhi_ready, hlo_ready = sem("t_done"), sem("h_ready"), sem("hhi_ready"), sem("hlo_ready")
        v_done, v_ready = sem("v_done"), sem("v_ready")
        p_done, p_hi, p_lo = sem("p_done"), sem("p_hi"), sem("p_lo")
        m_done, m_red, mstep, s_ready = sem("m_done"), sem("m_red"), sem("mstep"), sem("s_ready")
        mt_done, mt_ready = sem("mt_done"), sem("mt_ready")
        sc_done, exp_done, pv_done = sem("sc_done"), sem("exp_done"), sem("pv_done")
        o_copied, o_rec, o_norm = sem("o_copied"), sem("o_rec"), sem("o_norm")
        w_done, u_ready, xg_ready, x1_ready = sem("w_done"), sem("u_ready"), sem("xg_ready"), sem("x1_ready")
        freed = {"hT": h_ready, "v": v_ready, "p": p_lo, "m": m_red, "mt": mt_ready, "w": u_ready}
        positions = {}
        for at, kind in enumerate(ring):
            positions.setdefault(kind, []).append(at)

        def ring_at(kind, n):
            return positions[kind][n]

        with nc.Block() as priming:
            @priming.sync
            def _(sp):
                for s in (h_ready, u_ready, x1_ready, w_done, t_done, hlo_ready, pv_done, o_norm, exp_done, mt_done, o_copied, *x1_out, *stk_in):
                    sp.sem_inc(s, PRIMED)

        block = ctx.enter_context(nc.Block())

        @block.sync
        def _(sp):
            with sp.Fori(0, NB) as b:
                sp.wait_ge(u_ready, b * NT + PRIMED)
                sp.dma_start(ga_bc[:, :], K.modd[bass.ds(b, 1), GA, :].broadcast_to([P, D])).then_inc(mod2_in, 16)
                sp.wait_ge(x1_ready, b * NT + PRIMED)
                sp.dma_start(gabo_bc[:, :], K.modd[bass.ds(b, 1), GABO, :].broadcast_to([P, D])).then_inc(mod2_in, 16)
                for p in range(NPAIR):
                    if p >= 2:
                        sp.wait_ge(pv_done, b * (NPAIR * NST) + NST * (p - 1) + PRIMED)
                        apart(sp)
                    sp.wait_ge(p_lo, b * 16 + 4 * (p // 2) + 4)
                    for e in range(2):
                        r = 2 * (p % 2) + e
                        rows = slice(DH * r, DH * r + DH)
                        for n, parts in enumerate((slice(0, 3, 2), slice(1, 3), slice(0, 4, 3))):
                            sp.dma_start(K.stk[DH * n:DH * n + DH, p % 2, :, e, :].bitcast(f32), st[rows, parts, :].bitcast(f32))\
                                .then_inc(stk_in[p % 2], 16)
                for j in range(NT):
                    if j < 2:
                        sp.wait_ge(x1_ready, b * NT + PRIMED)
                    else:
                        sp.wait_ge(x1_ready, b * NT + j - 1 + PRIMED)
                    sp.dma_start(xr[:, j % 2, :], K.x[bass.ds(b * S + OUT[j] * P, P), :]).then_inc(xr_in[j % 2], 16)
                    if j >= 1:
                        sp.wait_ge(x1_ready, b * NT + j + PRIMED)
                        sp.dma_start(K.x1d[bass.ds(b * S + OUT[j - 1] * P, P), :], u[:, (j - 1) % 2, :]).then_inc(x1_out[(j - 1) % 2], 16)
                sp.wait_ge(x1_ready, b * NT + NT + PRIMED)
                sp.dma_start(K.x1d[bass.ds(b * S + OUT[NT - 1] * P, P), :], u[:, (NT - 1) % 2, :]).then_inc(x1_out[(NT - 1) % 2], 16)
            for i in range(2):
                sp.wait_ge(x1_out[i], NB * NT // 2 * 16 + PRIMED)

        @block.gpsimd
        def _(pool):
            def split_low(b, j):
                pool.wait_ge(h_ready, b * NT + j + 1 + PRIMED)
                pool.wait_ge(hhi_ready, b * NT + j + 1)
                nc.gpsimd.tensor_tensor(hlo[:, :, j * P:(j + 1) * P], h[:, j % 2, :, :],
                                        hhi[:, :, j * P:(j + 1) * P].bitcast(f32), ALU.subtract).then_inc(hlo_ready, 1)

            with pool.Fori(0, NB) as b:
                for j in range(NT):
                    pool.wait_ge(mv_ready, b * NT + j + 1)
                    apart(pool)
                    nc.gpsimd.tensor_scalar(rstd[:, j % 2, 0:1], mv[:, j % 2, 1:2], EPS, None, ALU.add).then_inc(var_eps, 1)
                    pool.wait_ge(var_eps, b * NT + j + 1)
                    nc.gpsimd.tensor_tensor(rstd[:, j % 2, 1:2], rstd[:, j % 2, 0:1], K.expo[:, 0:1], ALU.pow).then_inc(rstd_ready, 1)
                    if j >= 2:
                        split_low(b, j - 2)
                split_low(b, NT - 2)
                split_low(b, NT - 1)
                for n in range(2 * NHG):
                    hg, c = n // 2, CHUNKS[n % 2]
                    pool.wait_ge(o_rec, b * 8 + n + 1)
                    nc.gpsimd.tensor_tensor(oT[:, hg, c * CH:(c + 1) * CH], oV[:, c, :], oD[:, c, :], ALU.mult).then_inc(o_norm, 1)
                pool.wait_ge(mod2_in, b * 32 + 32)
                for j in range(NT):
                    pool.wait_ge(xr_in[j % 2], b * (NT // 2 * 16) + (j // 2 + 1) * 16)
                    nc.gpsimd.tensor_tensor(xr[:, j % 2, :], xr[:, j % 2, :], gabo_bc[:, :], ALU.add).then_inc(xg_ready, 1)
                    pool.wait_ge(xg_ready, b * NT + j + 1)
                    pool.wait_ge(u_ready, b * NT + j + 1 + PRIMED)
                    nc.gpsimd.tensor_tensor(u[:, j % 2, :], u[:, j % 2, :], xr[:, j % 2, :], ALU.add).then_inc(x1_ready, 1)

        @block.scalar
        def _(act):
            def p_evac(b, hg):
                for n in range(4):
                    which, c = n // 2, n % 2
                    if n == 0:
                        for s in range(2):
                            act.wait_ge(stk_in[s], (b * NHG + hg) * STACKED + PRIMED)
                    u_ = ring_at("p", 4 * hg + n)
                    act.wait_ge(p_done, b * 16 + 4 * hg + n + 1)
                    nc.scalar.activation(st[:, 2 * which, c * CH:(c + 1) * CH], rb[u_ % 3][:, :], ACT.Identity,
                                         bias=K.bias[:, which * KC + hg:which * KC + hg + 1]).then_inc(p_hi, 1)

            def v_evac(b, j):
                act.wait_ge(v_done, b * NT + j + 1)
                nc.scalar.activation(V[:, j * D:(j + 1) * D], rb[ring_at("v", j) % 3][:, :], ACT.Copy).then_inc(v_ready, 1)

            def mt_evac(b, p):
                if p >= 2:
                    act.wait_ge(pv_done, b * NPAIR * NST + NST * (p - 1) + PRIMED)
                for z, c in enumerate(CHUNKS):
                    act.wait_ge(mt_done, b * 16 + 2 * p + z + 1 + PRIMED)
                    bank = rb[ring_at("mt", 2 * p + z) % 3]
                    for e in range(2):
                        last = nc.scalar.activation(K.stk[96:128, p % 2, 0, e, c * CH:(c + 1) * CH], bank[32 * e:32 * e + 32, :], ACT.Copy)
                    last.then_inc(mt_ready, 1)

            def exp(b, p, s):
                c, i = STEPS[s]
                off = max(0, i * P - c * CH)
                g = p * NST + s
                act.wait_ge(sc_done, b * NPAIR * NST + g + 1)
                if g >= 3:
                    act.wait_ge(pv_done, b * NPAIR * NST + g - 2 + PRIMED)
                nc.scalar.activation(pr[:, g % 3, :, off:], sc[g % 2][:, :, off:], ACT.Exp, scale=SCALE).then_inc(exp_done, 1)

            def o_copy(b, n):
                act.wait_ge(pv_done, b * NPAIR * NST + (n // 2) * NST + (TURN, NST)[n % 2] + PRIMED)
                p, c = n // 2, CHUNKS[n % 2]
                if p % 2 == 0 and p >= 2:
                    act.wait_ge(o_norm, b * 8 + p - 2 + n % 2 + 1 + PRIMED)
                elif p == 0:
                    act.wait_ge(o_norm, b * 8 + PRIMED)
                z = 64 * (p % 2)
                nc.scalar.activation(oV[z:z + 64, c, :], O[z:z + 64, :], ACT.Copy)
                nc.scalar.activation(oD[z:z + 64, c, :], O[64 - z:128 - z, :], ACT.Copy).then_inc(o_copied, 1)

            with act.Fori(0, NB) as b:
                act.wait_ge(h_ready, b * NT + PRIMED)
                with nc.allow_non_contiguous_dma(reason="512 numbers by partition"):
                    for i, kind in ((0, SA), (1, CA1)):
                        for k in range(KC):
                            act.dma_start(mod_t[:, i, k:k + 1], K.modd[bass.ds(b, 1), kind, k * P:(k + 1) * P].rearrange("a p -> p a"))\
                                .then_inc(mod_in, 16)
                act.wait_ge(w_done, b * NT + PRIMED)
                for i in range(NT // 2):
                    act.dma_start(xt[:, 2 * i:2 * i + 2, :], K.x[bass.ds(b * S + i * 2 * P, 2 * P), :].rearrange("(j p) d -> p j d", p=P))\
                        .then_inc(xt_in[i], 16)
                act.wait_ge(mod_in, b * 128 + 128)
                for j in range(NT):
                    act.wait_ge(t_done, b * NT + j + 1 + PRIMED)
                    if j >= 2:
                        act.wait_ge(hlo_ready, b * NT + j - 1 + PRIMED)
                    else:
                        act.wait_ge(x1_out[j % 2], b * (NT // 2 * 16) + PRIMED)
                    bank = rb[ring_at("hT", j) % 3]
                    for k in range(KC):
                        last = nc.scalar.activation(h[:, j % 2, k, :], bank[:, k * P:(k + 1) * P], ACT.Identity,
                                                    scale=mod_t[:, 1, k:k + 1], bias=mod_t[:, 0, k:k + 1])
                    last.then_inc(h_ready, 1)
                    if j >= V_LAG:
                        v_evac(b, j - V_LAG)
                p_evac(b, 0)
                for j in range(NT - V_LAG, NT):
                    v_evac(b, j)
                mt_evac(b, 0)
                for p in range(NPAIR):
                    for s in range(NST):
                        exp(b, p, s)
                        if s == TURN:
                            o_copy(b, 2 * p)
                    o_copy(b, 2 * p + 1)
                    if p % 2 == 0 and p + 2 < NPAIR:
                        p_evac(b, (p + 2) // 2)
                    if p + 1 < NPAIR:
                        mt_evac(b, p + 1)

        @block.vector
        def _(dve):

            def ln_stats(b, j):
                if j % 2 == 0:
                    dve.wait_ge(xt_in[j // 2], b * 16 + 16)
                nc.vector.bn_stats(stats[:, j % 2, :], xt[:, j, :]).then_inc(bn, 1)
                if j >= 2:
                    dve.wait_ge(rstd_ready, b * NT + j - 1)
                dve.wait_ge(bn, b * NT + j + 1)
                apart(dve)
                nc.vector.bn_aggr(mv[:, j % 2, :], stats[:, j % 2, :]).then_inc(mv_ready, 1)

            def ln_norm(b, j):
                dve.wait_ge(rstd_ready, b * NT + j + 1)
                nc.vector.tensor_scalar(xt[:, j, :], xt[:, j, :], mv[:, j % 2, 0:1], rstd[:, j % 2, 1:2],
                                        ALU.subtract, ALU.mult).then_inc(xn_ready, 1)

            def split_high(b, j):
                dve.wait_ge(h_ready, b * NT + j + 1 + PRIMED)
                nc.vector.tensor_copy(hhi[:, :, j * P:(j + 1) * P], h[:, j % 2, :, :]).then_inc(hhi_ready, 1)

            def p_low(b, hg):
                for n in range(4):
                    which, c = n // 2, n % 2
                    bank = rb[ring_at("p", 4 * hg + n) % 3]
                    dve.wait_ge(p_hi, b * 16 + 4 * hg + n + 1)
                    nc.vector.scalar_tensor_tensor(st[:, 2 * which + 1, c * CH:(c + 1) * CH], bank[:, :],
                                                   K.bias[:, which * KC + hg:which * KC + hg + 1],
                                                   st[:, 2 * which, c * CH:(c + 1) * CH].bitcast(f32),
                                                   ALU.add, ALU.subtract).then_inc(p_lo, 1)

            def m_reduce(b, p, n):
                heads, qt, k0, w, part = MUSES[n]
                bank = rb[ring_at("m", NM * p + n) % 3]
                dve.wait_ge(m_done, b * NPAIR * NM + p * NM + n + 1)
                nc.vector.tensor_reduce(mx[:, heads[0]:heads[-1] + 1, qt, part],
                                        bank[:, 0:len(heads) * w].rearrange("p (e k) -> p e k", e=len(heads)),
                                        AX.X, ALU.max).then_inc(m_red, 1)

            def m_rows(b, p):
                base = b * NPAIR * 3 + p * 3
                dve.wait_ge(m_red, b * NPAIR * NM + (p + 1) * NM)
                nc.vector.tensor_tensor(mx[:, :, 4:NT, 0], mx[:, :, 4:NT, 0], mx[:, :, 4:NT, 1], ALU.max).then_inc(mstep, 1)
                dve.wait_ge(mstep, base + 1)
                nc.vector.tensor_scalar(negm[:, :, :], mx[:, :, :, 0].rearrange("p e t -> p t e"), MASKED, -1.0, ALU.max, ALU.mult)\
                    .then_inc(mstep, 1)
                dve.wait_ge(mstep, base + 2)
                nc.vector.tensor_copy(mhi[:, :, :], negm[:, :, :]).then_inc(mstep, 1)
                dve.wait_ge(mstep, base + 3)
                dve.wait_ge(mt_done, b * 16 + 2 * p + PRIMED)
                nc.vector.tensor_copy(S_t[:, :, 0::32], mhi[:, :, :].bitcast(f32))
                nc.vector.tensor_tensor(S_t[:, :, 1::32], negm[:, :, :], mhi[:, :, :].bitcast(f32), ALU.subtract).then_inc(s_ready, 1)

            def o_recip(b, n):
                hg, c = n // 2, CHUNKS[n % 2]
                dve.wait_ge(o_copied, b * 16 + 4 * hg + 3 + n % 2 + PRIMED)
                nc.vector.reciprocal(oD[:, c, :], oD[:, c, :]).then_inc(o_rec, 1)

            with dve.Fori(0, NB) as b:
                ln_stats(b, 0)
                for j in range(NT):
                    if j + 1 < NT:
                        ln_stats(b, j + 1)
                    ln_norm(b, j)
                    if j >= 1:
                        split_high(b, j - 1)
                split_high(b, NT - 1)
                p_low(b, 0)
                for n in range(NM):
                    m_reduce(b, 0, n)
                m_rows(b, 0)
                for p in range(NPAIR):
                    n = 0
                    for s in range(NST + 1):
                        if p + 1 < NPAIR:
                            while n < M_DUE[s]:
                                m_reduce(b, p + 1, n)
                                n += 1
                        if s == TURN + 1 and p == NPAIR - 1:
                            o_recip(b, p - 1)
                    if p + 1 < NPAIR:
                        m_rows(b, p + 1)
                    if p % 2 == 0 and p + 2 < NPAIR:
                        p_low(b, (p + 2) // 2)
                    if p % 2:
                        if p < NPAIR - 1:
                            o_recip(b, p - 1)
                        o_recip(b, p)
                dve.wait_ge(mod2_in, b * 32 + 32)
                for j in range(NT):
                    bank = rb[ring_at("w", j) % 3]
                    dve.wait_ge(w_done, b * NT + j + 1 + PRIMED)
                    dve.wait_ge(x1_out[j % 2], b * (NT // 2 * 16) + (j // 2) * 16 + PRIMED)
                    nc.vector.tensor_tensor(u[:, j % 2, :], bank[:, :], ga_bc[:, :], ALU.mult).then_inc(u_ready, 1)

        @block.tensor
        def _(pe):

            def bank_for(b, kind, n):
                at = ring_at(kind, n)
                if at < 3:
                    pe.wait_ge(u_ready, b * NT + PRIMED)
                else:
                    before = ring[at - 3]
                    primed = PRIMED if freed[before] in (h_ready, u_ready) else 0
                    pe.wait_ge(freed[before], b * TOTAL[before] + positions[before].index(at - 3) + 1 + primed)
                return rb[at % 3]

            def transposes(b, j):
                bank = bank_for(b, "hT", j)
                pe.wait_ge(xn_ready, b * NT + j + 1)
                for k in range(KC):
                    last = nc.tensor.transpose(bank[:, k * P:(k + 1) * P], xt[:, j, k * P:(k + 1) * P], K.ident[:, :])
                last.then_inc(t_done, 1)

            def values(b, j):
                bank = bank_for(b, "v", j)
                pe.wait_ge(hlo_ready, b * NT + j + 1 + PRIMED)
                terms = [(x_, w_, k) for k in range(KC) for x_, w_ in ((hhi, K.whi), (hhi, K.wlo), (hlo, K.whi))]
                for n, (x_, w_, k) in enumerate(terms):
                    last = nc.tensor.matmul(bank[:, :], x_[:, k, j * P:(j + 1) * P], w_[:, k, 2 * D:3 * D],
                                            start=(n == 0), stop=(n == len(terms) - 1))
                last.then_inc(v_done, 1)

            def project(b, hg):
                pe.wait_ge(hlo_ready, b * NT + NT + PRIMED)
                for n in range(4):
                    which, c = n // 2, n % 2
                    bank = bank_for(b, "p", 4 * hg + n)
                    cols = slice(which * D + hg * P, which * D + (hg + 1) * P)
                    terms = [(w_, x_, k) for k in range(KC) for w_, x_ in ((K.whi, hhi), (K.whi, hlo), (K.wlo, hhi))]
                    for t, (w_, x_, k) in enumerate(terms):
                        last = nc.tensor.matmul(bank[:, :], w_[:, k, cols], x_[:, k, c * CH:(c + 1) * CH],
                                                start=(t == 0), stop=(t == len(terms) - 1))
                    last.then_inc(p_done, 1)

            def m_scores(b, p, n):
                heads, qt, k0, w, part = MUSES[n]
                bank = bank_for(b, "m", NM * p + n)
                diag = k0 <= qt * P < k0 + w
                for x_, e in enumerate(heads):
                    o = bank[:, x_ * w:(x_ + 1) * w]
                    last = nc.tensor.matmul(o, K.stk[0:96, p % 2, 0, e, qt * P:(qt + 1) * P], K.stk[0:96, p % 2, 1, e, k0:k0 + w],
                                            start=True, stop=not diag)
                    if diag:
                        last = nc.tensor.matmul(o[:, qt * P - k0:qt * P - k0 + P], K.identb[:, :], K.mask_qk[:, :],
                                                start=False, stop=True)
                last.then_inc(m_done, 1)

            def m_transpose(b, p):
                for z, c in enumerate(CHUNKS):
                    bank = bank_for(b, "mt", 2 * p + z)
                    pe.wait_ge(s_ready, b * NPAIR + p + 1)
                    apart(pe)
                    for t in range(4):
                        last = nc.tensor.transpose(bank[0:64, t * P:(t + 1) * P], S_t[:, 4 * c + t, :], K.ident[:, :])
                    last.then_inc(mt_done, 1)

            def scores(b, p, s):
                c, i = STEPS[s]
                off = max(0, i * P - c * CH)
                g = p * NST + s
                if g >= 2:
                    pe.wait_ge(exp_done, b * NPAIR * NST + g - 1 + PRIMED)
                else:
                    pe.wait_ge(exp_done, b * NPAIR * NST + PRIMED)
                pe.wait_ge(mt_ready, b * 16 + 2 * p + CHUNKS.index(c) + 1)
                diag = i * P >= c * CH
                for e in range(2):
                    last = nc.tensor.matmul(sc[g % 2][:, e, off:], K.stk[:, p % 2, 1, e, i * P:(i + 1) * P],
                                            K.stk[:, p % 2, 0, e, c * CH + off:(c + 1) * CH], start=True, stop=not diag)
                    if diag:
                        last = nc.tensor.matmul(sc[g % 2][:, e, off:off + P], K.identb[:, :], K.mask_kq[:, :], start=False, stop=True)
                last.then_inc(sc_done, 1)

            def weighted(b, p, s):
                c, i = STEPS[s]
                off = max(0, i * P - c * CH)
                g = p * NST + s
                n = 2 * p + CHUNKS.index(c)
                if i == 0:
                    pe.wait_ge(o_copied, b * 16 + n + PRIMED)
                pe.wait_ge(exp_done, b * NPAIR * NST + g + 1 + PRIMED)
                for e in range(2):
                    at = i * D + (2 * p + e) * DH
                    for z, col in ((p % 2, at), (1 - p % 2, NT * D)):
                        row = 64 * z + 32 * e
                        last = nc.tensor.matmul(O[row:row + 32, off:], V[:, col:col + DH], pr[:, g % 3, e, off:],
                                                start=(i == 0), stop=(i == 4 * c + 3))
                last.then_inc(pv_done, 1)

            def output(b, j):
                bank = bank_for(b, "w", j)
                pe.wait_ge(o_norm, b * 8 + 7 + j // (NT // 2) + PRIMED)
                t = OUT[j]
                for k in range(KC):
                    last = nc.tensor.matmul(bank[:, :], oT[:, k, t * P:(t + 1) * P], K.wo[:, k, :], start=(k == 0), stop=(k == KC - 1))
                last.then_inc(w_done, 1)

            with pe.Fori(0, NB) as b:
                for j in range(NT):
                    transposes(b, j)
                    if j >= V_LAG:
                        values(b, j - V_LAG)
                project(b, 0)
                for j in range(NT - V_LAG, NT):
                    values(b, j)
                pe.wait_ge(stk_in[0], b * NHG * STACKED + STACKED + PRIMED)
                for n in range(NM):
                    m_scores(b, 0, n)
                m_transpose(b, 0)
                for p in range(NPAIR):
                    n = 0
                    for s in range(NST + 1):
                        if s < NST:
                            scores(b, p, s)
                        if p + 1 < NPAIR:
                            if n == 0 and M_DUE[s]:
                                pe.wait_ge(stk_in[(p + 1) % 2], (b * NHG + (p + 1) // 2 + 1) * STACKED + PRIMED)
                            while n < M_DUE[s]:
                                m_scores(b, p + 1, n)
                                n += 1
                        if s >= 1:
                            weighted(b, p, s - 1)
                    if p % 2 == 0 and p + 2 < NPAIR:
                        project(b, (p + 2) // 2)
                    if p + 1 < NPAIR:
                        m_transpose(b, p + 1)
                for j in range(NT):
                    output(b, j)


def apart(eng):
    eng.nop(nofuse=True)


class Kept:
    pass


def program_a(nc, K, ctx):
    f32, f32r, bf16 = mybir.dt.float32, mybir.dt.float32r, mybir.dt.bfloat16
    sb = lambda n, s, d=f32: ctx.enter_context(nc.sbuf_tensor(n, s, d))
    K.ident = sb("ident", [P, P])
    K.expo = sb("expo", [P, 4])
    a = ExitStack()
    with a:
        sb = lambda n, s, d=f32: a.enter_context(nc.sbuf_tensor(n, s, d))
        K.whi = sb("whi", [P, KC, 3 * D], f32r)
        K.wlo = sb("wlo", [P, KC, 3 * D], f32r)
        K.wo = sb("wo_sb", [P, KC, D])
        K.bias = sb("bias", [P, 3 * KC])
        K.identb = sb("identb", [P, P], bf16)
        K.mask_qk = sb("mask_qk", [P, P], bf16)
        K.mask_kq = sb("mask_kq", [P, P], bf16)
        K.V = sb("V", [P, NT * D + DH])
        K.S = sb("S", [P, NT, 64])
        K.stk = sb("stk", [P, 2, 2, 2, S], f32r)
        with nc.sbuf_tensor("ones_row", [P, S // 4], f32) as K.ones_row:
            setup_phase(nc, K)
        attention_phase(nc, K)

E = 16
NG, GSZ = 4, 4
F = 1024
FC = F // P
EI = 256
EC = EI // P
CH = 512
TPC = CH // P
NCH = T // CH
T_FROM = FC - TPC
NTILE = T // P
REGION = T + P
NET = (2 * T + E * (P - 1)) // P
DUMMY = E * REGION
ROWS = DUMMY + P


def shared_phase(nc, K):
    f32, f32r, bf16, u32 = mybir.dt.float32, mybir.dt.float32r, mybir.dt.bfloat16, mybir.dt.uint32
    ALU, ACT, AX = mybir.AluOpType, mybir.ActivationFunctionType, mybir.AxisListType
    ctx = ExitStack()
    with ctx:
        sb = lambda n, s, d=f32: ctx.enter_context(nc.sbuf_tensor(n, s, d))
        pb = lambda n, s: ctx.enter_context(nc.psum_tensor(n, s, f32))
        sem = lambda n: ctx.enter_context(nc.semaphore(n))
        xb = sb("xb", [P, 2, TPC, D])
        h2 = sb("h2", [P, 2, TPC, D])
        bc = sb("bc", [P, 2, 3, D])
        stats = sb("stats2", [P, TPC, 6])
        mv = sb("mv2", [P, TPC, 2])
        rstd = sb("rstd2", [P, 2, TPC])
        thi = sb("thi", [P, 2, KC, CH], f32r)
        tlo = sb("tlo", [P, 2, KC, CH], f32r)
        relu = sb("relu", [P, 2, CH])
        sq = sb("sq", [P, 2, CH])
        ahi = sb("ahi", [P, FC, CH], f32r)
        alo = sb("alo", [P, FC, CH], f32r)
        y = sb("y_sh", [P, 2, D])
        lgT = sb("lgT", [E, CH])
        s_ = sb("s_", [P, TPC, E])
        sbias = sb("sbias", [P, TPC, E])
        g2 = sb("g2", [P, 6, TPC, NG])
        cmp = sb("cmp", [P, 3, TPC, NG, NG])
        rank = sb("rank", [P, TPC, NG])
        m16 = sb("m16", [P, 3, TPC, E])
        top = sb("top", [P, 2, TPC, 1])
        oh = sb("oh", [P, 2, TPC, E])
        chosen = sb("chosen", [P, TPC, E], bf16)
        ws = sb("ws", [P, 4, TPC])
        place = sb("place", [P, TPC, E])
        slotf = sb("slotf", [P, 2, TPC])
        slotu = sb("slotu", [P, 2, 2, TPC], u32)
        tp = [pb(f"tp{i}", [P, KC, P]) for i in range(2)]
        rp = pb("rp", [P, 512])
        pl = pb("pl", [P, 512])
        lt = pl[:, 2 * P:2 * P + TPC * E]
        upb = [pb(f"up{i}", [P, CH]) for i in range(2)]
        dnb = [pb(f"dn{i}", [P, D]) for i in range(2)]

        xb_in = [sem(f"xb_in{i}") for i in range(2)]
        bc_in = [sem(f"bc_in{i}") for i in range(2)]
        bn, mv_ready, var_eps, rstd_ready = sem("bn2"), sem("mv2_ready"), sem("var_eps2"), sem("rstd2_ready")
        h2_scaled, h2_ready = sem("h2_scaled"), sem("h2_ready")
        t_done, thi_ready, tlo_ready = sem("t2_done"), sem("thi_ready"), sem("tlo_ready")
        r_done, s_ready, step = sem("r_done"), sem("sig_ready"), sem("route_step")
        chosen_ready, place_done, slots_ready = sem("chosen_ready"), sem("place_done"), sem("slots_ready")
        sent = [sem(f"sent{i}") for i in range(2)]
        up_done, relu_ready, sq_ready, ahi_ready, alo_ready = (sem(n) for n in
            ("up_done", "relu_ready", "sq_ready", "ahi_ready", "alo_ready"))
        dn_done, y_scaled, y_ready = sem("dn_done"), sem("y_scaled"), sem("y_ready")
        y_out = [sem(f"y_out{i}") for i in range(2)]
        rw_raw = relu[0:E, 0, :]
        zero = sb("zero", [P, D])
        dn_own = sb("dn_own", [P, FC - 2, D])
        up_raw = [(slice(0, 2), xb[:, 1, :, :].rearrange("p j d -> p (j d)").rearrange("p (k n) -> p k n", k=2)),
                  (slice(2, 4), h2[:, 1, :, :].rearrange("p j d -> p (j d)").rearrange("p (k n) -> p k n", k=2))]
        dn_raw = [(slice(0, FC - 2), dn_own[:, :, :]), (slice(FC - 2, FC), y[:, :, :])]
        raw_in, rw_in, hi_done, lo_done, rw_t, rw_split = (sem(n) for n in
            ("c_raw_in", "rw_in", "c_hi_done", "c_lo_done", "rw_t", "rw_split"))
        dn_in, dn_hi, dn_lo, rw_hi, zero_out, zeroed, consts = (sem(n) for n in ("dn_in", "dn_hi", "dn_lo", "rw_hi", "zero_out", "c_zeroed", "c_consts"))
        lg_copied, lt_done = sem("lg_copied"), sem("lt_done")
        block = ctx.enter_context(nc.Block())

        def rounds(first, loop, chunk):
            first()
            with loop as i:
                chunk(2 * i, 0, i)
                chunk(2 * i + 1, 1, i + 1)
            chunk(NCH - 2, 0, NB - 1)
            chunk(NCH - 1, 1, None)

        @block.sync
        def _(sp):
            def load_tile(r, par, j):
                sp.dma_start(xb[:, par, j, :], K.x1d[bass.ds(r * CH + j * P, P), :]).then_inc(xb_in[par], 16)

            def load_rows(b, par):
                sp.dma_start(bc[:, par, :, :], K.modd[bass.ds(b, 1), SB:GB + 1, :].broadcast_to([P, 3, D])).then_inc(bc_in[par], 16)

            def first():
                sp.dma_start(rw_raw, K.rw).then_inc(rw_in, 16)
                sp.dma_start(K.ebias[:, :], K.eb.rearrange("(a n) -> a n", a=1).broadcast_to([P, E])).then_inc(rw_in, 16)
                for j in range(TPC):
                    load_tile(0, 0, j)
                load_rows(0, 0)
                for ks, at in up_raw:
                    sp.dma_start(at, K.sup.rearrange("(k p) n -> p k n", p=P)[:, ks, :]).then_inc(raw_in, 16)
                for ks, at in dn_raw:
                    sp.dma_start(at, K.sdn.rearrange("(k p) n -> p k n", p=P)[:, ks, :]).then_inc(dn_in, 16)
                load_rows(0, 1)
                sp.wait_ge(lo_done, 1)
                for j in range(TPC):
                    load_tile(1, 1, j)
                sp.wait_ge(zeroed, 1)
                sp.dma_start(K.xs[DUMMY:DUMMY + P, :], zero[:, :]).then_inc(zero_out, 16)

            def chunk(q, par, b):
                more = not isinstance(q, int)
                for j in range(TPC):
                    sp.wait_ge(y_ready, q * TPC + j + 1 + PRIMED)
                    sp.dma_start(K.part[bass.ds(q * CH + j * P, P), :], y[:, j % 2, :]).then_inc(y_out[j % 2], 16)
                    if more:
                        load_tile(q + 2, par, j)
                if more:
                    load_rows(b + 1 - par, par)

            for s in (relu_ready, alo_ready, sq_ready, y_scaled, tlo_ready, s_ready, y_ready, *y_out):
                sp.sem_inc(s, PRIMED)
            rounds(first, sp.Fori(0, NCH // 2 - 1), chunk)
            sp.wait_ge(zero_out, 16)
            for i in range(2):
                sp.wait_ge(y_out[i], NCH * TPC // 2 * 16 + PRIMED)

        @block.gpsimd
        def _(pool):

            def inverse_deviation(r):
                pool.wait_ge(mv_ready, r * TPC + TPC)
                apart(pool)
                nc.gpsimd.tensor_scalar(rstd[:, 0, :], mv[:, :, 1], EPS, None, ALU.add).then_inc(var_eps, 1)
                pool.wait_ge(var_eps, r + 1)
                nc.gpsimd.tensor_tensor(rstd[:, 1, :], rstd[:, 0, :], K.expo[:, 0:TPC], ALU.pow).then_inc(rstd_ready, 1)

            def low(q, m):
                pool.wait_ge(ahi_ready, q * FC + m + 1)
                nc.gpsimd.tensor_tensor(alo[:, m, :], sq[:, m % 2, :], ahi[:, m, :].bitcast(f32), ALU.subtract).then_inc(alo_ready, 1)

            def send(par, n):
                c, j = n // TPC, n % TPC
                nc.gpsimd.indirect_dma_start(out=K.xs, out_offset=bass.IndirectOffsetOnAxis(ap=slotu[:, par, c, j:j + 1], axis=0),
                                             in_=h2[:, par, j, :], in_offset=None).then_inc(sent[par], 16)

            def chunk(q, par, b):
                n = 0
                for m in range(FC):
                    low(q, m)
                    if m == 1 and b is not None:
                        inverse_deviation(q + 1)
                    if m == 2:
                        pool.wait_ge(slots_ready, q + 1)
                        apart(pool)
                    for _ in range((0, 0, 1, 1, 1, 1, 2, 2)[m]):
                        send(par, n)
                        n += 1
                for j in range(TPC):
                    if j == TPC - 1:
                        pool.wait_ge(sent[par], (q - par) * (TPC * 16) + TPC * 2 * 16)
                        apart(pool)
                    pool.wait_ge(y_scaled, q * TPC + j + 1 + PRIMED)
                    nc.gpsimd.tensor_tensor(y[:, j % 2, :], y[:, j % 2, :], xb[:, par, j, :], ALU.add).then_inc(y_ready, 1)

            def first():
                nc.gpsimd.memset(zero[:, :], 0.0).then_inc(zeroed, 1)
                nc.gpsimd.memset(K.tri[:, :], 1.0).then_inc(zeroed, 1)
                nc.gpsimd.memset(K.ones[:, :], 1.0)
                nc.gpsimd.memset(K.expo[:, :], -0.5).then_inc(zeroed, 1)
                pool.wait_ge(zeroed, 3)
                nc.gpsimd.affine_select(out=K.tri[:, :], in_=K.tri[:, :], compare_op=ALU.is_gt, fill=0.0, base=0,
                                        pattern=[[1, P]], channel_multiplier=-1).then_inc(consts, 1)
                inverse_deviation(0)
                pool.wait_ge(dn_hi, 1)
                for ks, at in dn_raw:
                    last = nc.gpsimd.tensor_tensor(K.dnlo[:, ks, :], at, K.dnhi[:, ks, :].bitcast(f32), ALU.subtract)
                last.then_inc(dn_lo, 1)

            rounds(first, pool.Fori(0, NCH // 2 - 1), chunk)
            for i in range(2):
                pool.wait_ge(sent[i], NCH * TPC * 16)

        @block.scalar
        def _(act):
            def high(r, par, j):
                act.wait_ge(t_done, r * TPC + j + 1)
                nc.scalar.activation(thi[:, par, :, j * P:(j + 1) * P], tp[j % 2][:, :, :], ACT.Copy).then_inc(thi_ready, 1)

            def sigmoid(r):
                act.wait_ge(r_done, r + 1)
                nc.scalar.activation(lgT[:, :], rp[0:E, :], ACT.Copy).then_inc(lg_copied, 1)
                act.wait_ge(lt_done, r + 1)
                nc.scalar.activation(s_[:, :, :], lt.rearrange("p (t e) -> p t e", e=E), ACT.Sigmoid).then_inc(s_ready, 1)

            def first():
                for j in range(TPC):
                    high(0, 0, j)
                act.wait_ge(raw_in, 32)
                for ks, at in up_raw:
                    last = nc.scalar.activation(K.uphi[:, ks, :], at, ACT.Copy)
                last.then_inc(hi_done, 1)
                sigmoid(0)
                act.wait_ge(dn_in, 32)
                for ks, at in dn_raw:
                    last = nc.scalar.activation(K.dnhi[:, ks, :], at, ACT.Copy)
                last.then_inc(dn_hi, 1)

            def chunk(q, par, b):
                for m in range(FC + 1):
                    if m < FC:
                        act.wait_ge(up_done, q * FC + m + 1)
                        if m >= 2:
                            act.wait_ge(sq_ready, q * FC + m - 1 + PRIMED)
                        else:
                            act.wait_ge(sq_ready, q * FC + PRIMED)
                        nc.scalar.activation(relu[:, m % 2, :], upb[m % 2][:, :], ACT.Relu).then_inc(relu_ready, 1)
                    if m >= 1:
                        act.wait_ge(sq_ready, q * FC + m + PRIMED)
                        nc.scalar.activation(ahi[:, m - 1, :], sq[:, (m - 1) % 2, :], ACT.Copy).then_inc(ahi_ready, 1)
                    if b is not None and T_FROM <= m < T_FROM + TPC:
                        high(q + 1, 1 - par, m - T_FROM)
                if b is not None:
                    sigmoid(q + 1)

            rounds(first, act.Fori(0, NCH // 2 - 1), chunk)

        @block.vector
        def _(dve):
            STEPS_R = 32

            def ln_stats(r, par, b):
                dve.wait_ge(xb_in[par], b * (TPC * 16) + TPC * 16)
                for j in range(TPC):
                    nc.vector.bn_stats(stats[:, j, :], xb[:, par, j, :]).then_inc(bn, 1)
                dve.wait_ge(bn, r * TPC + TPC)
                apart(dve)
                for j in range(TPC):
                    nc.vector.bn_aggr(mv[:, j, :], stats[:, j, :]).then_inc(mv_ready, 1)

            def ln_norm(r, par, b, j):
                hj = h2[:, par, j, :]
                if j == 0:
                    dve.wait_ge(rstd_ready, r + 1)
                    dve.wait_ge(bc_in[par], b * 16 + 16)
                nc.vector.scalar_tensor_tensor(hj, xb[:, par, j, :], mv[:, j, 0:1], bc[:, par, 1, :], ALU.subtract, ALU.mult)\
                    .then_inc(h2_scaled, 1)
                dve.wait_ge(h2_scaled, r * TPC + j + 1)
                nc.vector.scalar_tensor_tensor(hj, hj, rstd[:, 1, j:j + 1], bc[:, par, 0, :], ALU.mult, ALU.add).then_inc(h2_ready, 1)

            def low(r, par, j):
                dve.wait_ge(thi_ready, r * TPC + j + 1)
                nc.vector.tensor_tensor(tlo[:, par, :, j * P:(j + 1) * P], tp[j % 2][:, :, :],
                                        thi[:, par, :, j * P:(j + 1) * P].bitcast(f32), ALU.subtract).then_inc(tlo_ready, 1)

            n = [0]

            def step_of(r):
                def then(ins):
                    n[0] += 1
                    ins.then_inc(step, 1)
                    dve.wait_ge(step, r * STEPS_R + n[0])
                return then

            def route(r, par):
                n[0] = 0
                then = step_of(r)
                tt, ts, red = nc.vector.tensor_tensor, nc.vector.tensor_scalar, nc.vector.tensor_reduce
                dve.wait_ge(s_ready, r + 1 + PRIMED)
                then(tt(sbias[:, :, :], s_[:, :, :], K.ebias[:, :].unsqueeze(1).broadcast_to([P, TPC, E]), ALU.add))
                v = sbias[:, :, :].rearrange("p t (g a b) -> p t g a b", a=2, b=2)
                tt(g2[:, 0, :, :], v[:, :, :, 0, 0], v[:, :, :, 0, 1], ALU.max)
                tt(g2[:, 1, :, :], v[:, :, :, 1, 0], v[:, :, :, 1, 1], ALU.max)
                tt(g2[:, 2, :, :], v[:, :, :, 0, 0], v[:, :, :, 0, 1], ALU.min)
                then(tt(g2[:, 3, :, :], v[:, :, :, 1, 0], v[:, :, :, 1, 1], ALU.min))
                tt(g2[:, 4, :, :], g2[:, 0, :, :], g2[:, 1, :, :], ALU.min)
                tt(g2[:, 5, :, :], g2[:, 2, :, :], g2[:, 3, :, :], ALU.max)
                then(tt(g2[:, 0, :, :], g2[:, 0, :, :], g2[:, 1, :, :], ALU.max))
                then(tt(g2[:, 1, :, :], g2[:, 4, :, :], g2[:, 5, :, :], ALU.max))
                then(tt(g2[:, 2, :, :], g2[:, 0, :, :], g2[:, 1, :, :], ALU.add))
                gi = g2[:, 2, :, :].unsqueeze(2).broadcast_to([P, TPC, NG, NG])
                gj = g2[:, 2, :, :].unsqueeze(3).broadcast_to([P, TPC, NG, NG])
                tt(cmp[:, 0], gi, gj, ALU.is_gt)
                then(tt(cmp[:, 1], gi, gj, ALU.is_equal))
                then(tt(cmp[:, 1], cmp[:, 1], K.gtri[:, :, :].unsqueeze(1).broadcast_to([P, TPC, NG, NG]), ALU.mult))
                then(tt(cmp[:, 0], cmp[:, 0], cmp[:, 1], ALU.add))
                then(red(rank[:, :, :], cmp[:, 0], AX.X, ALU.add))
                then(ts(rank[:, :, :], rank[:, :, :], float(2), None, ALU.is_lt))
                masked = m16[:, 0, :, :]
                then(tt(masked.rearrange("p t (g i) -> p t g i", i=GSZ), sbias[:, :, :].rearrange("p t (g i) -> p t g i", i=GSZ),
                        rank[:, :, :].unsqueeze(3).broadcast_to([P, TPC, NG, GSZ]), ALU.mult))
                order = K.order[:, :].unsqueeze(1).broadcast_to([P, TPC, E])
                for c in range(2):
                    then(red(top[:, 0, :, 0], masked, AX.X, ALU.max))
                    then(tt(m16[:, 1, :, :], masked, top[:, 0, :, :].broadcast_to([P, TPC, E]), ALU.is_equal))
                    then(tt(m16[:, 1, :, :], m16[:, 1, :, :], order, ALU.mult))
                    then(red(top[:, 1, :, 0], m16[:, 1, :, :], AX.X, ALU.max))
                    nc.vector.tensor_copy(K.choice[:, c, bass.ds(r * TPC, TPC)], top[:, 1, :, 0])
                    then(tt(oh[:, c, :, :], order, top[:, 1, :, :].broadcast_to([P, TPC, E]), ALU.is_equal))
                    if c == 0:
                        then(nc.vector.scalar_tensor_tensor(m16[:, 0, :, :], oh[:, 0, :, :], -3e38, masked, ALU.mult, ALU.add))
                nc.vector.tensor_tensor(chosen[:, :, :], oh[:, 0, :, :], oh[:, 1, :, :], ALU.add).then_inc(chosen_ready, 1)
                for c in range(2):
                    last = tt(m16[:, 1 + c, :, :], oh[:, c, :, :], s_[:, :, :], ALU.mult)
                then(last)
                red(ws[:, 0, :], m16[:, 1, :, :], AX.X, ALU.add)
                then(red(ws[:, 1, :], m16[:, 2, :, :], AX.X, ALU.add))
                then(tt(ws[:, 2, :], ws[:, 0, :], ws[:, 1, :], ALU.add))
                then(ts(ws[:, 2, :], ws[:, 2, :], 1e-20, None, ALU.add))
                then(nc.vector.reciprocal(ws[:, 3, :], ws[:, 2, :]))
                for c in range(2):
                    tt(K.wts[:, c, bass.ds(r * TPC, TPC)], ws[:, c, :], ws[:, 3, :], ALU.mult)

            def place_rows(r, par):
                then = step_of(r)
                tt, red = nc.vector.tensor_tensor, nc.vector.tensor_reduce
                dve.wait_ge(place_done, r + 1)
                then(tt(place[:, :, :], pl[:, 0:TPC * E].rearrange("p (t e) -> p t e", e=E),
                        K.count[:, :].unsqueeze(1).broadcast_to([P, TPC, E]), ALU.add))
                then(tt(K.count[:, :], K.count[:, :], pl[:, TPC * E:(TPC + 1) * E], ALU.add))
                then(tt(place[:, :, :], place[:, :, :], K.region[:, :].unsqueeze(1).broadcast_to([P, TPC, E]), ALU.add))
                for c in range(2):
                    last = tt(m16[:, 1 + c, :, :], place[:, :, :], oh[:, c, :, :], ALU.mult)
                then(last)
                for c in range(2):
                    last = red(slotf[:, c, :], m16[:, 1 + c, :, :], AX.X, ALU.add)
                then(last)
                nc.vector.tensor_copy(K.slots[:, :, bass.ds(r * TPC, TPC)], slotf[:, :, :])
                nc.vector.tensor_copy(slotu[:, par, :, :], slotf[:, :, :]).then_inc(slots_ready, 1)
                assert n[0] == STEPS_R, n[0]

            def square(q, m):
                dve.wait_ge(relu_ready, q * FC + m + 1 + PRIMED)
                if m >= 2:
                    dve.wait_ge(alo_ready, q * FC + m - 1 + PRIMED)
                else:
                    dve.wait_ge(alo_ready, q * FC + PRIMED)
                nc.vector.tensor_tensor(sq[:, m % 2, :], relu[:, m % 2, :], relu[:, m % 2, :], ALU.mult).then_inc(sq_ready, 1)

            def scaled(q, par, j):
                dve.wait_ge(dn_done, q * TPC + j + 1)
                dve.wait_ge(y_out[j % 2], q * (TPC // 2 * 16) + j // 2 * 16 + PRIMED)
                nc.vector.tensor_tensor(y[:, j % 2, :], dnb[j % 2][:, :], bc[:, par, 2, :], ALU.mult).then_inc(y_scaled, 1)

            def first():
                for e in range(E):
                    nc.vector.memset(K.order[:, e:e + 1], float(E - e))
                    nc.vector.memset(K.region[:, e:e + 1], float(e * REGION))
                for i in range(NG):
                    for j in range(NG):
                        nc.vector.memset(K.gtri[:, j, i:i + 1], 1.0 if i < j else 0.0)
                nc.vector.memset(K.count[:, :], 0.0)
                dve.wait_ge(rw_t, 1)
                nc.vector.tensor_copy(K.rwhi[:, :, :], tp[0][:, :, 0:E]).then_inc(rw_hi, 1)
                dve.wait_ge(rw_hi, 1)
                nc.vector.tensor_tensor(K.rwlo[:, :, :], tp[0][:, :, 0:E], K.rwhi[:, :, :].bitcast(f32), ALU.subtract).then_inc(rw_split, 1)
                ln_stats(0, 0, 0)
                for j in range(TPC):
                    ln_norm(0, 0, 0, j)
                for j in range(TPC):
                    low(0, 0, j)
                dve.wait_ge(hi_done, 1)
                for ks, at in up_raw:
                    last = nc.vector.tensor_tensor(K.uplo[:, ks, :], at, K.uphi[:, ks, :].bitcast(f32), ALU.subtract)
                last.then_inc(lo_done, 1)
                route(0, 0)

            def chunk(q, par, b):
                for m in range(FC):
                    square(q, m)
                    if m == 1:
                        place_rows(q, par)
                    if b is not None:
                        if m == 1:
                            ln_stats(q + 1, 1 - par, b)
                            dve.wait_ge(y_ready, q * TPC + PRIMED)
                        if T_FROM - 2 <= m < T_FROM - 2 + TPC:
                            ln_norm(q + 1, 1 - par, b, m - (T_FROM - 2))
                        if T_FROM <= m:
                            low(q + 1, 1 - par, m - T_FROM)
                scaled(q, par, 0)
                if b is not None:
                    route(q + 1, 1 - par)
                scaled(q, par, 1)
                scaled(q, par, 2)
                scaled(q, par, 3)

            rounds(first, dve.Fori(0, NCH // 2 - 1), chunk)

        @block.tensor
        def _(pe):
            def transposes(r, par, j):
                pe.wait_ge(h2_ready, r * TPC + j + 1)
                if j >= 2:
                    pe.wait_ge(tlo_ready, r * TPC + j - 1 + PRIMED)
                else:
                    pe.wait_ge(tlo_ready, r * TPC + PRIMED)
                for k in range(KC):
                    last = nc.tensor.transpose(tp[j % 2][:, k, :], h2[:, par, j, k * P:(k + 1) * P], K.ident[:, :])
                last.then_inc(t_done, 1)

            def router(r, par):
                pe.wait_ge(tlo_ready, r * TPC + TPC + PRIMED)
                pe.wait_ge(s_ready, r + PRIMED)
                terms = [(w_, x_, k) for k in range(KC) for w_, x_ in ((K.rwhi, thi), (K.rwlo, thi), (K.rwhi, tlo))]
                for n, (w_, x_, k) in enumerate(terms):
                    last = nc.tensor.matmul(rp[0:E, :], w_[:, k, :], x_[:, par, k, :], start=(n == 0), stop=(n == len(terms) - 1))
                last.then_inc(r_done, 1)

            def logits_by_token(r):
                pe.wait_ge(lg_copied, r + 1)
                apart(pe)
                for j in range(TPC):
                    last = nc.tensor.transpose(lt[:, j * E:(j + 1) * E], lgT[:, j * P:(j + 1) * P], K.ident[0:E, 0:E])
                last.then_inc(lt_done, 1)

            def places(r):
                pe.wait_ge(chosen_ready, r + 1)
                for j in range(TPC + 1):
                    o = pl[:, j * E:(j + 1) * E]
                    for i in range(j):
                        last = nc.tensor.matmul(o, K.ones[:, :], chosen[:, i, :], start=(i == 0), stop=(i == j - 1 and j == TPC))
                    if j < TPC:
                        last = nc.tensor.matmul(o, K.tri[:, :], chosen[:, j, :], start=(j == 0), stop=True)
                last.then_inc(place_done, 1)

            def up(q, par, m):
                if m >= 2:
                    pe.wait_ge(relu_ready, q * FC + m - 1 + PRIMED)
                else:
                    pe.wait_ge(relu_ready, q * FC + PRIMED)
                terms = [(w_, x_, k) for k in range(KC) for w_, x_ in ((K.uphi, thi), (K.uphi, tlo), (K.uplo, thi))]
                for n, (w_, x_, k) in enumerate(terms):
                    last = nc.tensor.matmul(upb[m % 2][:, :], w_[:, k, m * P:(m + 1) * P], x_[:, par, k, :],
                                            start=(n == 0), stop=(n == len(terms) - 1))
                last.then_inc(up_done, 1)

            def down(q, j, ks=range(FC)):
                if ks[0] == 0:
                    if j >= 2:
                        pe.wait_ge(y_scaled, q * TPC + j - 1 + PRIMED)
                    else:
                        pe.wait_ge(y_scaled, q * TPC + PRIMED)
                for k in ks:
                    if j == 0:
                        pe.wait_ge(alo_ready, q * FC + k + 1 + PRIMED)
                    for n, (a_, w_) in enumerate(((ahi, K.dnhi), (ahi, K.dnlo), (alo, K.dnhi))):
                        last = nc.tensor.matmul(dnb[j % 2][:, :], a_[:, k, j * P:(j + 1) * P], w_[:, k, :],
                                                start=(k == 0 and n == 0), stop=(k == FC - 1 and n == 2))
                if ks[-1] == FC - 1:
                    last.then_inc(dn_done, 1)

            def first():
                pe.wait_ge(rw_in, 32)
                for k in range(KC):
                    last = nc.tensor.transpose(tp[0][:, k, 0:E], relu[0:E, 0, k * P:(k + 1) * P], K.ident[0:E, 0:E])
                last.then_inc(rw_t, 1)
                pe.wait_ge(rw_split, 1)
                for j in range(TPC):
                    transposes(0, 0, j)
                router(0, 0)
                logits_by_token(0)
                pe.wait_ge(lo_done, 1)
                pe.wait_ge(consts, 1)

            def chunk(q, par, b):
                for m in range(FC):
                    up(q, par, m)
                    if m == 1:
                        places(q)
                    if b is not None and m >= T_FROM:
                        transposes(q + 1, 1 - par, m - T_FROM)
                pe.wait_ge(dn_lo, 1)
                down(q, 0)
                if b is not None:
                    router(q + 1, 1 - par)
                down(q, 1, range(FC // 2))
                if b is not None:
                    logits_by_token(q + 1)
                down(q, 1, range(FC // 2, FC))
                down(q, 2)
                down(q, 3)

            rounds(first, pe.Fori(0, NCH // 2 - 1), chunk)


def program_c(nc, K, ctx):
    f32, f32r, bf16 = mybir.dt.float32, mybir.dt.float32r, mybir.dt.bfloat16
    with ExitStack() as a:
        sb = lambda n, s, d=f32: a.enter_context(nc.sbuf_tensor(n, s, d))
        K.uphi = sb("uphi", [P, KC, F], f32r)
        K.uplo = sb("uplo", [P, KC, F], f32r)
        K.dnhi = sb("dnhi", [P, FC, D], f32r)
        K.dnlo = sb("dnlo", [P, FC, D], f32r)
        K.rwhi = sb("rwhi", [P, KC, E], f32r)
        K.rwlo = sb("rwlo", [P, KC, E], f32r)
        K.ebias = sb("ebias", [P, E])
        K.order = sb("order", [P, E])
        K.region = sb("region", [P, E])
        K.gtri = sb("gtri", [P, NG, NG])
        K.tri = sb("tri", [P, P], bf16)
        K.ones = sb("ones", [P, P], bf16)
        shared_phase(nc, K)

AHEAD = 3
XR = 4


def expert_phase(nc, K):
    f32, i32 = mybir.dt.float32, mybir.dt.int32
    ALU, ACT, AX = mybir.AluOpType, mybir.ActivationFunctionType, mybir.AxisListType
    ctx = ExitStack()
    with ctx:
        sb = lambda n, s, d=f32: ctx.enter_context(nc.sbuf_tensor(n, s, d))
        pb = lambda n, s: ctx.enter_context(nc.psum_tensor(n, s, f32))
        sem = lambda n: ctx.enter_context(nc.semaphore(n))
        x = sb("x_e", [P, XR, D])
        xT = sb("xT_e", [P, 2, KC, P])
        r = sb("r_e", [P, 2, EI])
        a = sb("a_e", [P, 2, EI])
        aT = sb("aT_e", [P, 2, EC, P])
        y = sb("y_e", [P, XR, D])
        txb = [pb(f"tx{i}", [P, KC, P]) for i in range(2)]
        ub = [pb(f"ue{i}", [P, 512]) for i in range(2)]
        tab = [pb(f"ta{i}", [P, 512]) for i in range(2)]
        db = [pb(f"de{i}", [P, D]) for i in range(2)]
        x_in = [sem(f"xe_in{i}") for i in range(XR)]
        y_out = [sem(f"ye_out{i}") for i in range(XR)]
        tx_done, xT_ready, u_done, r_ready, a_ready, ta_done, aT_ready, d_done, y_ready = (sem(n) for n in
            ("tx_done", "xT_ready", "ue_done", "re_ready", "ae_ready", "ta_done", "aT_ready", "de_done", "ye_ready"))
        zero = sb("zero_rows", [P, D])
        k_i, j_i, e_i = sb("k_i", [P, NTILE], i32), sb("j_i", [P, 1], i32), sb("e_i", [P, E], i32)
        kf, jf, ef = sb("kf", [P, NTILE]), sb("jf", [P, 1]), sb("ef", [P, E])
        more = sb("more", [P, E, NTILE])
        ntile = sb("ntile", [P, E])
        ones = sb("ones_e", [P, E])
        ends = sb("ends", [P, E])
        starts = sb("starts", [P, E])
        base = sb("base", [P, E])
        inside, other, mine_e = sb("inside", [P, E]), sb("other", [P, E]), sb("mine_e", [P, E])
        rowf = sb("rowf", [P, 4])
        padf = sb("padf", [P, E])
        order, shift = sb("order_e", [P, E]), sb("shift", [P, E])
        mine = sb("mine", [P, 2 * NTILE, E])
        moved = sb("moved", [P, 2 * NTILE])
        padi = sb("padi", [P, E], i32)
        iotas, zeroed, step, tables = sem("iotas"), sem("rows_zeroed"), sem("table_step"), sem("tables")
        in_columns, in_rows = sem("in_columns"), sem("in_rows")
        w_in = [sem(f"we_in{i}") for i in range(2)]
        w_ready, padded = sem("we_ready"), sem("padded")
        block = ctx.enter_context(nc.Block())
        FULL = (NET - AHEAD) // XR * XR

        def rounds(eng, round_):
            for j in range(-AHEAD, XR):
                round_(j, j % XR)
            with eng.Fori(1, FULL // XR) as i:
                for s in range(XR):
                    round_(i * XR + s, s)
            for j in range(FULL, NET):
                round_(j, j % XR)

        def known(j):
            return isinstance(j, int)

        def has(j):
            return not known(j) or 0 <= j < NET

        def wait(eng, s, value):
            if not (known(value) and value <= 0):
                eng.wait_ge(s, value)

        @block.sync
        def _(sp):
            def load(j, k, s):
                if has(j + k if known(j) else j):
                    t = j + k
                    wait(sp, tx_done, t - XR + 1)
                    row = sp.value_load(K.xrow[0:1, t:t + 1] if known(t) else K.xrow[0:1, bass.ds(t, 1)], min_val=0, max_val=ROWS - P)
                    sp.dma_start(x[:, (s + k) % XR, :], K.xs[bass.ds(row, P), :]).then_inc(x_in[(s + k) % XR], 16)

            def store(j, s):
                if has(j):
                    wait(sp, y_ready, j + 1)
                    sp.dma_start(K.ys[bass.ds(j * P, P), :], y[:, s, :]).then_inc(y_out[s], 16)

            sp.wait_ge(tables, 1)
            sp.wait_ge(zeroed, 1)
            for e in range(E):
                row = sp.value_load(padi[0:1, e:e + 1], min_val=e * REGION, max_val=e * REGION + T)
                sp.dma_start(K.xs[bass.ds(row, P), :], zero[:, :]).then_inc(padded, 16)
            sp.wait_ge(padded, 16 * E)
            for t in range(AHEAD):
                load(t - 2 * AHEAD, 2 * AHEAD, (t - 2 * AHEAD) % XR)
            for j in range(-AHEAD, 0):
                load(j, 2 * AHEAD, j % XR)
            L = (NET - 2 * AHEAD) // XR * XR
            with sp.Fori(0, L // XR) as i:
                for s in range(XR):
                    load(i * XR + s, 2 * AHEAD, s)
                    store(i * XR + s, s)
            for j in range(L, NET):
                load(j, 2 * AHEAD, j % XR)
                store(j, j % XR)
            for s in range(XR):
                sp.wait_ge(y_out[s], 16 * len(range(s, NET, XR)))

        @block.gpsimd
        def _(pool):
            nc.gpsimd.memset(zero[:, :], 0.0).then_inc(zeroed, 1)
            nc.gpsimd.iota(k_i[:, :], pattern=[[P, NTILE]], base=0, channel_multiplier=0).then_inc(iotas, 1)
            nc.gpsimd.iota(j_i[:, :], pattern=[[1, 1]], base=0, channel_multiplier=1).then_inc(iotas, 1)
            nc.gpsimd.iota(e_i[:, :], pattern=[[1, E]], base=0, channel_multiplier=0).then_inc(iotas, 1)
            for e in range(E + 2):
                if e >= 2:
                    pool.wait_ge(w_in[e % 2], e // 2 * 32)
                    pool.sem_inc(w_ready, 1)
                if e == 2:
                    pool.wait_ge(padded, 16 * E)
                if e < E:
                    pool.dma_start(K.wu[:, e * KC * EI:(e + 1) * KC * EI].rearrange("p (k n) -> p k n", k=KC),
                                   K.wup[e, :, :].rearrange("(k p) n -> p k n", p=P)).then_inc(w_in[e % 2], 16)
                    pool.dma_start(K.wd[:, e * EC * D:(e + 1) * EC * D].rearrange("p (k n) -> p k n", k=EC),
                                   K.wdn[e, :, :].rearrange("(k p) n -> p k n", p=P)).then_inc(w_in[e % 2], 16)

        @block.scalar
        def _(act):
            def round_(j, s):
                if has(j + 3 if known(j) else j):
                    act.wait_ge(tx_done, j + 4)
                    wait(act, u_done, j + 2)
                    nc.scalar.activation(xT[:, (s + 3) % 2, :, :], txb[(s + 3) % 2][:, :, :], ACT.Copy).then_inc(xT_ready, 1)
                if has(j + 2 if known(j) else j):
                    act.wait_ge(u_done, j + 3)
                    wait(act, a_ready, j + 1)
                    nc.scalar.activation(r[:, s % 2, :], ub[s % 2][:, 0:EI], ACT.Relu).then_inc(r_ready, 1)

            rounds(act, round_)

        @block.vector
        def _(dve):
            def round_(j, s):
                if has(j + 2 if known(j) else j):
                    dve.wait_ge(r_ready, j + 3)
                    wait(dve, ta_done, j + 1)
                    nc.vector.tensor_tensor(a[:, s % 2, :], r[:, s % 2, :], r[:, s % 2, :], ALU.mult).then_inc(a_ready, 1)
                if has(j + 1 if known(j) else j):
                    dve.wait_ge(ta_done, j + 2)
                    wait(dve, d_done, j)
                    nc.vector.tensor_copy(aT[:, (s + 1) % 2, :, :], tab[(s + 1) % 2][:, 0:EC * P]).then_inc(aT_ready, 1)
                if has(j):
                    dve.wait_ge(d_done, j + 1)
                    if known(j):
                        wait(dve, y_out[s], j // XR * 16)
                    else:
                        dve.wait_ge(y_out[s], (j - s) * (16 // XR))
                    nc.vector.tensor_copy(y[:, s, :], db[s % 2][:, :]).then_inc(y_ready, 1)

            n = [0]

            def then(ins):
                n[0] += 1
                ins.then_inc(step, 1)
                dve.wait_ge(step, n[0])

            tt, ts, red = nc.vector.tensor_tensor, nc.vector.tensor_scalar, nc.vector.tensor_reduce
            dve.wait_ge(iotas, 3)
            nc.vector.memset(ones[:, :], 1.0)
            nc.vector.tensor_copy(kf[:, :], k_i[:, :])
            nc.vector.tensor_copy(jf[:, :], j_i[:, :])
            then(nc.vector.tensor_copy(ef[:, :], e_i[:, :]))
            then(tt(more[:, :, :], K.count[:, :].unsqueeze(2).broadcast_to([P, E, NTILE]),
                    kf[:, :].unsqueeze(1).broadcast_to([P, E, NTILE]), ALU.is_gt))
            then(red(ntile[:, :], more[:, :, :], AX.X, ALU.add))
            then(nc.vector.tensor_tensor_scan(ends[:, :], ones[:, :], ntile[:, :], 0.0, ALU.mult, ALU.add))
            then(tt(starts[:, :], ends[:, :], ntile[:, :], ALU.subtract))
            then(ts(base[:, :], starts[:, :], -float(P), -float(DUMMY), ALU.mult, ALU.add))
            ts(padf[:, :], ef[:, :], float(REGION), None, ALU.mult)
            then(nc.vector.scalar_tensor_tensor(base[:, :], ef[:, :], float(REGION), base[:, :], ALU.mult, ALU.add))
            then(tt(padf[:, :], padf[:, :], K.count[:, :], ALU.add))
            nc.vector.tensor_copy(padi[:, :], padf[:, :])
            ts(inside[:, :], starts[:, :], jf[:, 0:1], None, ALU.is_le)
            then(ts(other[:, :], ends[:, :], jf[:, 0:1], None, ALU.is_le))
            then(tt(inside[:, :], inside[:, :], other[:, :], ALU.subtract))
            red(rowf[:, 0:1], inside[:, :], AX.X, ALU.add)
            tt(other[:, :], inside[:, :], base[:, :], ALU.mult)
            then(tt(mine_e[:, :], inside[:, :], ef[:, :], ALU.mult))
            red(rowf[:, 1:2], other[:, :], AX.X, ALU.add)
            red(rowf[:, 2:3], mine_e[:, :], AX.X, ALU.add)
            then(ts(rowf[:, 3:4], jf[:, :], float(P), None, ALU.mult))
            then(tt(rowf[:, 3:4], rowf[:, 3:4], rowf[:, 0:1], ALU.mult))
            then(tt(rowf[:, 3:4], rowf[:, 3:4], rowf[:, 1:2], ALU.add))
            ts(rowf[:, 3:4], rowf[:, 3:4], float(DUMMY), None, ALU.add).then_inc(in_columns, 1)
            dve.wait_ge(in_rows, 1)
            nc.vector.tensor_copy(K.eid[0:1, :], txb[0][0:1, 0, 0:NET])
            nc.vector.tensor_copy(K.xrow[0:1, :], txb[0][0:1, 1, 0:NET]).then_inc(tables, 1)
            bc = K.choice[:, :, :].rearrange("p c t -> p (c t)").unsqueeze(2).broadcast_to([P, 2 * NTILE, E])
            bx = lambda a: a[:, :].unsqueeze(1).broadcast_to([P, 2 * NTILE, E])
            ts(order[:, :], ef[:, :], -1.0, float(E), ALU.mult, ALU.add)
            then(ts(shift[:, :], base[:, :], float(DUMMY), None, ALU.add))
            then(tt(mine[:, :, :], bc, bx(order), ALU.is_equal))
            then(tt(mine[:, :, :], mine[:, :, :], bx(shift), ALU.mult))
            then(red(moved[:, :], mine[:, :, :], AX.X, ALU.add))
            then(tt(moved[:, :], K.slots[:, :, :].rearrange("p c t -> p (c t)"), moved[:, :], ALU.subtract))
            nc.vector.tensor_copy(K.rows[:, :, :].rearrange("p c t -> p (c t)"), moved[:, :])
            rounds(dve, round_)

        @block.tensor
        def _(pe):
            pe.wait_ge(in_columns, 1)
            for n in range(2):
                last = nc.tensor.transpose(txb[0][0:1, n, 0:NET], rowf[0:NET, 2 + n:3 + n], K.ident[0:NET, 0:NET])
            last.then_inc(in_rows, 1)
            pe.wait_ge(tables, 1)

            def expert(t):
                return pe.value_load(K.eid[0:1, t:t + 1] if known(t) else K.eid[0:1, bass.ds(t, 1)], min_val=0, max_val=E - 1)

            def round_(j, s):
                if has(j + 3 if known(j) else j):
                    t, z = j + 3, (s + 3) % XR
                    pe.wait_ge(x_in[z], t // XR * 16 + 16 if known(t) else (j - s) * (16 // XR) + ((s + 3) // XR + 1) * 16)
                    wait(pe, xT_ready, j + 2)
                    for k in range(KC):
                        last = nc.tensor.transpose(txb[z % 2][:, k, :], x[:, z, k * P:(k + 1) * P], K.ident[:, :])
                    last.then_inc(tx_done, 1)
                if has(j + 2 if known(j) else j):
                    e = expert(j + 2)
                    pe.wait_ge(w_ready, e + 1)
                    pe.wait_ge(xT_ready, j + 3)
                    wait(pe, r_ready, j + 1)
                    for k in range(KC):
                        last = nc.tensor.matmul(ub[s % 2][:, 0:EI], xT[:, s % 2, k, :], K.wu[:, bass.ds(e * (KC * EI) + k * EI, EI)],
                                                start=(k == 0), stop=(k == KC - 1))
                    last.then_inc(u_done, 1)
                if has(j + 1 if known(j) else j):
                    pe.wait_ge(a_ready, j + 2)
                    wait(pe, aT_ready, j)
                    for k in range(EC):
                        last = nc.tensor.transpose(tab[(s + 1) % 2][:, k * P:(k + 1) * P], a[:, (s + 1) % 2, k * P:(k + 1) * P], K.ident[:, :])
                    last.then_inc(ta_done, 1)
                if has(j):
                    e = expert(j)
                    pe.wait_ge(aT_ready, j + 1)
                    wait(pe, y_ready, j - 1)
                    for k in range(EC):
                        last = nc.tensor.matmul(db[s % 2][:, :], aT[:, s % 2, k, :], K.wd[:, bass.ds(e * (EC * D) + k * D, D)],
                                                start=(k == 0), stop=(k == EC - 1))
                    last.then_inc(d_done, 1)

            rounds(pe, round_)


def combine_phase(nc, K):
    f32, u32 = mybir.dt.float32, mybir.dt.uint32
    ALU = mybir.AluOpType
    ctx = ExitStack()
    with ctx:
        sb = lambda n, s, d=f32: ctx.enter_context(nc.sbuf_tensor(n, s, d))
        sem = lambda n: ctx.enter_context(nc.semaphore(n))
        gb = sb("gb_f", [P, 2, D])
        base = sb("base_f", [P, 2, TPC, D])
        g = sb("g_f", [P, 2, TPC, 2, D])
        z = sb("z_f", [P, 2, TPC, D])
        idx = sb("idx_f", [P, 2, 2, TPC], u32)
        w = sb("w_f", [P, 2, 2, TPC])
        gb_in = [sem(f"gb_in{i}") for i in range(2)]
        out_sent = [sem(f"out_sent{i}") for i in range(2)]
        base_in = [sem(f"base_in{i}") for i in range(2)]
        g_in = [[sem(f"g_in{i}_{j}") for j in range(TPC)] for i in range(2)]
        idx_ready, first_done, both_done, gated, z_ready = (sem(n) for n in ("idx_ready", "first_done", "both_done", "gated", "z_ready"))
        block = ctx.enter_context(nc.Block())

        @block.sync
        def _(sp):
            def load(c, par, b, done):
                if done is not None:
                    sp.wait_ge(z_ready, done)
                sp.dma_start(gb[:, par, :], K.modd[bass.ds(b, 1), GB, :].broadcast_to([P, D])).then_inc(gb_in[par], 16)
                sp.dma_start(base[:, par, :, :], K.part[bass.ds(c * CH, CH), :].rearrange("(j p) d -> p j d", p=P)).then_inc(base_in[par], 16)

            def store(c, par):
                for j in range(TPC):
                    sp.wait_ge(z_ready, c * TPC + j + 1)
                    sp.dma_start(K.out[bass.ds(c * CH + j * P, P), :], z[:, par, j, :]).then_inc(out_sent[par], 16)

            for par in range(2):
                sp.sem_inc(out_sent[par], PRIMED)
            load(0, 0, 0, None)
            load(1, 1, 0, None)
            with sp.Fori(0, NB - 1) as b:
                for par in range(2):
                    store(2 * b + par, par)
                    load(2 * b + par + 2, par, b + 1, (2 * b + par + 1) * TPC)
            for par in range(2):
                store(NCH - 2 + par, par)
            for par in range(2):
                sp.wait_ge(out_sent[par], NCH // 2 * TPC * 16 + PRIMED)

        @block.gpsimd
        def _(pool):
            with pool.Fori(0, NB) as b:
                for par in range(2):
                    pool.wait_ge(idx_ready, 2 * b + par + 1)
                    apart(pool)
                    for j in range(TPC):
                        for c in range(2):
                            nc.gpsimd.indirect_dma_start(out=g[:, par, j, c, :], out_offset=None, in_=K.ys,
                                                         in_offset=bass.IndirectOffsetOnAxis(ap=idx[:, par, c, j:j + 1], axis=0))\
                                .then_inc(g_in[par][j], 16)

        @block.vector
        def _(dve):
            def indices(c, par):
                nc.vector.tensor_copy(w[:, par, :, :], K.wts[:, :, bass.ds(c * TPC, TPC)])
                nc.vector.tensor_copy(idx[:, par, :, :], K.rows[:, :, bass.ds(c * TPC, TPC)]).then_inc(idx_ready, 1)

            def chunk(b, par):
                c = 2 * b + par
                dve.wait_ge(gb_in[par], b * 16 + 16)
                dve.wait_ge(base_in[par], b * 16 + 16)
                dve.wait_ge(out_sent[par], b * (TPC * 16) + PRIMED)
                for j in range(TPC):
                    n = c * TPC + j
                    dve.wait_ge(g_in[par][j], b * 32 + 32)
                    zj = z[:, par, j, :]
                    nc.vector.tensor_scalar(zj, g[:, par, j, 0, :], w[:, par, 0, j:j + 1], None, ALU.mult).then_inc(first_done, 1)
                    dve.wait_ge(first_done, n + 1)
                    nc.vector.scalar_tensor_tensor(zj, g[:, par, j, 1, :], w[:, par, 1, j:j + 1], zj, ALU.mult, ALU.add).then_inc(both_done, 1)
                    dve.wait_ge(both_done, n + 1)
                    nc.vector.tensor_tensor(zj, zj, gb[:, par, :], ALU.mult).then_inc(gated, 1)
                    dve.wait_ge(gated, n + 1)
                    nc.vector.tensor_tensor(zj, zj, base[:, par, j, :], ALU.add).then_inc(z_ready, 1)

            indices(0, 0)
            with dve.Fori(0, NB - 1) as b:
                indices(2 * b + 1, 1)
                chunk(b, 0)
                indices(2 * b + 2, 0)
                chunk(b, 1)
            indices(NCH - 1, 1)
            chunk(NB - 1, 0)
            chunk(NB - 1, 1)


def program_e(nc, K, ctx):
    f32, i32 = mybir.dt.float32, mybir.dt.int32
    with ExitStack() as a:
        sb = lambda n, s, d=f32: a.enter_context(nc.sbuf_tensor(n, s, d))
        K.wu = sb("wu_e", [P, E * KC * EI])
        K.wd = sb("wd_e", [P, E * EC * D])
        K.eid = sb("eid", [P, NET], i32)
        K.xrow = sb("xrow", [P, NET], i32)
        expert_phase(nc, K)
    combine_phase(nc, K)


def block_kernel(nc, x, Wqkv, bqkv, Wo, bo, rw, eb, wup, wdn, sup, sdn, c, wmod, out):
    f32, u32 = mybir.dt.float32, mybir.dt.uint32
    K = Kept()
    K.x = x.rearrange("b s d -> (b s) d")
    K.out = out.rearrange("b s d -> (b s) d")
    K.Wqkv, K.bqkv, K.Wo, K.bo, K.rw, K.eb, K.wup, K.wdn, K.sup, K.sdn, K.c, K.wmod = (
        Wqkv, bqkv, Wo, bo, rw, eb, wup, wdn, sup, sdn, c, wmod)
    K.modd = nc.dram_tensor("modd", [NB, 7, D], f32, kind="Internal").ap()
    K.x1d = nc.dram_tensor("x1d", [T, D], f32, kind="Internal").ap()
    K.part = nc.dram_tensor("part", [T, D], f32, kind="Internal").ap()
    K.xs = nc.dram_tensor("xs", [ROWS, D], f32, kind="Internal").ap()
    K.ys = nc.dram_tensor("ys", [NET * P, D], f32, kind="Internal").ap()
    with ExitStack() as ctx:
        K.count = ctx.enter_context(nc.sbuf_tensor("count", [P, E], f32))
        K.wts = ctx.enter_context(nc.sbuf_tensor("wts", [P, 2, NTILE], f32))
        K.slots = ctx.enter_context(nc.sbuf_tensor("slots", [P, 2, NTILE], f32))
        K.choice = ctx.enter_context(nc.sbuf_tensor("choice", [P, 2, NTILE], f32))
        K.rows = ctx.enter_context(nc.sbuf_tensor("rows", [P, 2, NTILE], u32))
        program_a(nc, K, ctx)
        program_c(nc, K, ctx)
        program_e(nc, K, ctx)


_INS = ['L0_attn_x', 'L0_attn_Wqkv', 'L0_attn_bqkv', 'L0_attn_Wo', 'L0_attn_bo', 'L0_ffn_router_weight', 'L0_ffn_e_bias',
        'L0_ffn_w_up', 'L0_ffn_w_down', 'L0_ffn_shared_up', 'L0_ffn_shared_down', 'L0_c', 'L0_wmod']
_OUTS = [((4, 1024, 512), 'float32')]


def kernel(**inputs):
    import numpy as _np
    import concourse.bacc as _bacc
    from concourse import mybir as _mybir
    from concourse.bass_utils import run_bass_kernel_spmd as _run

    nc = _bacc.Bacc("TRN2", target_bir_lowering=False, num_devices=1)
    arrays, args = {}, []
    for name in _INS:
        a = _np.ascontiguousarray(inputs[name])
        arrays[f"in_{name}_dram"] = a
        args.append(nc.dram_tensor(f"in_{name}_dram", a.shape, _mybir.dt.from_np(a.dtype), kind="ExternalInput").ap())
    for i, (shape, dtype) in enumerate(_OUTS):
        dt = _mybir.dt.from_np(_np.dtype(dtype))
        args.append(nc.dram_tensor(f"out_{i}_dram", shape, dt, kind="ExternalOutput").ap())
    block_kernel(nc, *args)
    r = _run(nc, [arrays], core_ids=[0])
    got = tuple(r.results[0][f"out_{i}_dram"] for i in range(len(_OUTS)))
    return got[0]
```
